# Optimizing a Trainium2 kernel written in Bass

```python
import numpy as np
import jax
import jax.numpy as jnp

def _softmax(x, axis=-1):
    return jax.nn.softmax(x, axis=axis)

def _gelu(x):
    return jax.nn.gelu(x, approximate=True)

def _silu(x):
    return jax.nn.silu(x)

def _sigmoid(x):
    return jax.nn.sigmoid(x)

def _layernorm(x, axis=-1, eps=1e-05):
    m = jnp.mean(x, axis=axis, keepdims=True)
    v = jnp.var(x, axis=axis, keepdims=True)
    return (x - m) / jnp.sqrt(v + eps)

def _scatter_add(tgt, idx, src, axis=0):
    return tgt.at[idx].add(src)

def _segment_sum(src, seg, n):
    return jax.ops.segment_sum(src, seg, n)
kernel_name = 'mk_gnn_ffn_d2_gnn_r32_4fa6ed'

def setup_inputs(seed: int=0):
    np.random.seed(seed)
    _w = jnp.asarray

    def _rec_inputs():
        import jax
        import jax.numpy as jnp
        _gk = jax.random.key(seed)
        x = -0.0002928 + 1 * jax.random.normal(jax.random.fold_in(_gk, 1), (256, 512), jnp.float32)
        src = jax.random.randint(jax.random.fold_in(_gk, 2), (8192,), 0, 256, jnp.int32)
        dst = jax.random.randint(jax.random.fold_in(_gk, 3), (8192,), 0, 256, jnp.int32)
        _o = jnp.argsort(dst, stable=True)
        src = src[_o]
        dst = dst[_o]
        edge_attr_64 = 0.000279952 + 1.00013 * jax.random.normal(jax.random.fold_in(_gk, 11), (8192, 64), jnp.float32)
        return (x, src, dst, edge_attr_64)
    x, src, dst, edge_attr_64 = _rec_inputs()

    def _L0_gnn_setup():
        import jax, jax.numpy as jnp
        import numpy as np
        N_NODES = 256
        N_EDGES = 8192
        D_IN = 512
        D_OUT = 512
        key = jax.random.key(seed)
        k1, k2, k3 = jax.random.split(key, 3)
        x = jax.random.normal(k1, (N_NODES, D_IN), dtype=jnp.float32)
        edge_index = jax.random.randint(k2, (2, N_EDGES), 0, N_NODES, dtype=jnp.int64)
        weight = jax.random.normal(k3, (D_IN, D_OUT), dtype=jnp.float32)
        bias = jnp.zeros((D_OUT,), dtype=jnp.float32)
        return {'x': x, 'edge_index': edge_index, 'weight': weight, 'bias': bias}
    _L0_gnn_all = _L0_gnn_setup()
    _L0_gnn_in = {k: v for k, v in _L0_gnn_all.items() if k in ('weight', 'bias')}
    del _L0_gnn_all

    def _L0_ffn_setup():
        import jax, jax.numpy as jnp
        import numpy as np
        MARK_AX = 0
        OPCODE_BASE = 16
        OP_SHL = OPCODE_BASE + 23
        OP_SHR = OPCODE_BASE + 24
        ALU_LO = 64
        ALU_HI = 80
        AX_CARRY_LO = 96
        OUTPUT_LO = 128
        OUTPUT_HI = 144
        B, SEQ, D = (8, 1024, 512)
        key = jax.random.key(seed)
        ks = jax.random.split(key, 6)
        x = jax.random.uniform(ks[0], (B, SEQ, D), dtype=jnp.float32) * 0.4
        mark = (jax.random.uniform(ks[1], (B, SEQ)) < 0.75).astype(jnp.float32)
        op_sel = jax.random.randint(ks[2], (B, SEQ), 0, 3)
        lo = jax.random.randint(ks[3], (B, SEQ), 0, 16)
        hi = jax.random.randint(ks[4], (B, SEQ), 0, 16)
        sa = jax.random.randint(ks[5], (B, SEQ), 0, 16)
        oh = lambda idx: jax.nn.one_hot(idx, 16, dtype=jnp.float32)
        x = x.at[..., MARK_AX].set(mark)
        x = x.at[..., OP_SHL].set((op_sel == 1).astype(jnp.float32))
        x = x.at[..., OP_SHR].set((op_sel == 2).astype(jnp.float32))
        x = x.at[..., ALU_LO:ALU_LO + 16].set(oh(lo))
        x = x.at[..., ALU_HI:ALU_HI + 16].set(oh(hi))
        x = x.at[..., AX_CARRY_LO:AX_CARRY_LO + 16].set(oh(sa))
        return {'x_bd': x}
    _L0_ffn_all = _L0_ffn_setup()
    _L0_ffn_in = {k: v for k, v in _L0_ffn_all.items() if k in ()}
    del _L0_ffn_all

    def _L1_gnn_setup():
        import jax, jax.numpy as jnp
        import numpy as np
        N_NODES = 625
        N_EDGES = 10000
        HIDDEN = 512
        EDGE_DIM = 64
        LN_EPS = 1e-05

        def mish(x):
            return x * jnp.tanh(jax.nn.softplus(x))
        key = jax.random.key(seed)
        ks = jax.random.split(key, 8)
        s = lambda fan_in: 1.0 / np.sqrt(fan_in)
        return {'x': jax.random.normal(ks[0], (N_NODES, HIDDEN), dtype=jnp.float32), 'edge_index': jax.random.randint(ks[1], (2, N_EDGES), 0, N_NODES, dtype=jnp.int64), 'edge_attr': jax.random.normal(ks[2], (N_EDGES, EDGE_DIM), dtype=jnp.float32), 'W1': jax.random.normal(ks[3], (2 * HIDDEN + EDGE_DIM, HIDDEN), dtype=jnp.float32) * s(2 * HIDDEN + EDGE_DIM), 'b1': jnp.zeros((HIDDEN,), dtype=jnp.float32), 'W2': jax.random.normal(ks[4], (HIDDEN, HIDDEN), dtype=jnp.float32) * s(HIDDEN), 'b2': jnp.zeros((HIDDEN,), dtype=jnp.float32), 'W3': jax.random.normal(ks[5], (2 * HIDDEN, HIDDEN), dtype=jnp.float32) * s(2 * HIDDEN), 'b3': jnp.zeros((HIDDEN,), dtype=jnp.float32), 'W4': jax.random.normal(ks[6], (HIDDEN, HIDDEN), dtype=jnp.float32) * s(HIDDEN), 'b4': jnp.zeros((HIDDEN,), dtype=jnp.float32), 'gamma': jnp.ones((HIDDEN,), dtype=jnp.float32), 'beta': jnp.zeros((HIDDEN,), dtype=jnp.float32)}
    _L1_gnn_all = _L1_gnn_setup()
    _L1_gnn_in = {k: v for k, v in _L1_gnn_all.items() if k in ('W1', 'b1', 'W2', 'b2', 'W3', 'b3', 'W4', 'b4', 'gamma', 'beta')}
    del _L1_gnn_all

    def _L1_ffn_setup():
        import jax, jax.numpy as jnp
        import numpy as np
        B, S, D, H, E, K = (2, 1024, 512, 64, 64, 2)
        EPS = 1e-05
        key = jax.random.key(seed)
        ks = jax.random.split(key, 5)
        s = 0.02
        return {'x': jax.random.normal(ks[0], (B, S, D), dtype=jnp.float32), 'Wg': jax.random.normal(ks[1], (D, E), dtype=jnp.float32) * s, 'bg': jnp.zeros((E,), dtype=jnp.float32), 'W1': jax.random.normal(ks[2], (E, D, H), dtype=jnp.float32) * s, 'b1': jnp.zeros((E, H), dtype=jnp.float32), 'W2': jax.random.normal(ks[3], (E, H, D), dtype=jnp.float32) * s, 'b2': jnp.zeros((E, D), dtype=jnp.float32), 'gamma': jnp.ones((D,), dtype=jnp.float32), 'beta': jnp.zeros((D,), dtype=jnp.float32)}
    _L1_ffn_all = _L1_ffn_setup()
    _L1_ffn_in = {k: v for k, v in _L1_ffn_all.items() if k in ('Wg', 'bg', 'W1', 'b1', 'W2', 'b2', 'gamma', 'beta')}
    del _L1_ffn_all
    return {'x': x, 'src': src, 'dst': dst, 'edge_attr_64': edge_attr_64, 'L0_gnn_weight': _L0_gnn_in['weight'], 'L0_gnn_bias': _L0_gnn_in['bias'], 'L1_gnn_W1': _L1_gnn_in['W1'], 'L1_gnn_b1': _L1_gnn_in['b1'], 'L1_gnn_W2': _L1_gnn_in['W2'], 'L1_gnn_b2': _L1_gnn_in['b2'], 'L1_gnn_W3': _L1_gnn_in['W3'], 'L1_gnn_b3': _L1_gnn_in['b3'], 'L1_gnn_W4': _L1_gnn_in['W4'], 'L1_gnn_b4': _L1_gnn_in['b4'], 'L1_gnn_gamma': _L1_gnn_in['gamma'], 'L1_gnn_beta': _L1_gnn_in['beta'], 'L1_ffn_Wg': _L1_ffn_in['Wg'], 'L1_ffn_bg': _L1_ffn_in['bg'], 'L1_ffn_W1': _L1_ffn_in['W1'], 'L1_ffn_b1': _L1_ffn_in['b1'], 'L1_ffn_W2': _L1_ffn_in['W2'], 'L1_ffn_b2': _L1_ffn_in['b2'], 'L1_ffn_gamma': _L1_ffn_in['gamma'], 'L1_ffn_beta': _L1_ffn_in['beta']}

def reference(x, src, dst, edge_attr_64, L0_gnn_weight, L0_gnn_bias, L1_gnn_W1, L1_gnn_b1, L1_gnn_W2, L1_gnn_b2, L1_gnn_W3, L1_gnn_b3, L1_gnn_W4, L1_gnn_b4, L1_gnn_gamma, L1_gnn_beta, L1_ffn_Wg, L1_ffn_bg, L1_ffn_W1, L1_ffn_b1, L1_ffn_W2, L1_ffn_b2, L1_ffn_gamma, L1_ffn_beta):
    import jax
    import jax.numpy as jnp

    def _L0_gnn_ref(x, edge_index, weight, bias):
        import jax, jax.numpy as jnp
        import numpy as np
        N_NODES = 256
        N_EDGES = 8192
        D_IN = 512
        D_OUT = 512
        n = x.shape[0]
        adj = jnp.zeros((n, n), dtype=x.dtype)
        adj = adj.at[edge_index[0], edge_index[1]].set(1.0)
        adj = adj.at[edge_index[1], edge_index[0]].set(1.0)
        adj = adj + jnp.eye(n, dtype=x.dtype)
        deg = jnp.sum(adj, axis=1)
        dinv = 1.0 / jnp.sqrt(deg)
        adj = adj * dinv[:, None] * dinv[None, :]
        return adj @ (x @ weight) + bias

    def _L0_ffn_ref(x_bd):
        import jax, jax.numpy as jnp
        import numpy as np
        MARK_AX = 0
        OPCODE_BASE = 16
        OP_SHL = OPCODE_BASE + 23
        OP_SHR = OPCODE_BASE + 24
        ALU_LO = 64
        ALU_HI = 80
        AX_CARRY_LO = 96
        OUTPUT_LO = 128
        OUTPUT_HI = 144
        B, SEQ, D = (8, 1024, 512)
        hot = x_bd > 0.5
        first16 = lambda off: jnp.argmax(hot[..., off:off + 16], axis=-1).astype(jnp.int32)
        lo = first16(ALU_LO)
        hi = first16(ALU_HI)
        sa = first16(AX_CARRY_LO)
        val = lo + 16 * hi
        shl = jnp.left_shift(val, sa) & 255
        shr = jnp.right_shift(val, sa)
        mark = hot[..., MARK_AX]
        is_shl = hot[..., OP_SHL]
        is_shr = jnp.logical_and(hot[..., OP_SHR], jnp.logical_not(is_shl))
        act_shl = jnp.logical_and(mark, is_shl)
        act_shr = jnp.logical_and(mark, is_shr)
        active = jnp.logical_or(act_shl, act_shr)
        res = jnp.where(act_shl, shl, jnp.where(act_shr, shr, 0))
        res = jnp.clip(res, 0, 255)
        rlo = res & 15
        rhi = res >> 4
        amp = 2.0 * active.astype(x_bd.dtype)
        add_lo = amp[..., None] * jax.nn.one_hot(rlo, 16, dtype=x_bd.dtype)
        add_hi = amp[..., None] * jax.nn.one_hot(rhi, 16, dtype=x_bd.dtype)
        out = x_bd.at[..., OUTPUT_LO:OUTPUT_LO + 16].add(add_lo)
        out = out.at[..., OUTPUT_HI:OUTPUT_HI + 16].add(add_hi)
        return out

    def _L1_gnn_ref(x, edge_index, edge_attr, W1, b1, W2, b2, W3, b3, W4, b4, gamma, beta):
        import jax, jax.numpy as jnp
        import numpy as np
        N_NODES = 625
        N_EDGES = 10000
        HIDDEN = 512
        EDGE_DIM = 64
        LN_EPS = 1e-05

        def mish(x):
            return x * jnp.tanh(jax.nn.softplus(x))
        src, dst = (edge_index[0], edge_index[1])
        edge_feat = jnp.concatenate([x[src], x[dst], edge_attr], axis=-1)
        h = mish(edge_feat @ W1 + b1)
        messages = mish(h @ W2 + b2)
        agg = jax.ops.segment_sum(messages, dst, num_segments=x.shape[0])
        u = mish(jnp.concatenate([x, agg], axis=-1) @ W3 + b3)
        out = u @ W4 + b4
        y = x + out
        mu = jnp.mean(y, axis=-1, keepdims=True)
        var = jnp.mean(jnp.square(y - mu), axis=-1, keepdims=True)
        return (y - mu) * jax.lax.rsqrt(var + LN_EPS) * gamma + beta

    def _L1_ffn_ref(x, Wg, bg, W1, b1, W2, b2, gamma, beta):
        import jax, jax.numpy as jnp
        import numpy as np
        B, S, D, H, E, K = (2, 1024, 512, 64, 64, 2)
        EPS = 1e-05
        probs = jax.nn.softmax(x @ Wg + bg, axis=-1)
        topk_vals, topk_idx = jax.lax.top_k(probs, K)
        sparse_w = jnp.sum(jax.nn.one_hot(topk_idx, E, dtype=probs.dtype) * topk_vals[..., None], axis=-2)
        h = jax.nn.relu(jnp.einsum('bsd,edh->bseh', x, W1) + b1)
        expert_out = jnp.einsum('bseh,ehd->bsed', h, W2) + b2
        out = jnp.einsum('bse,bsed->bsd', sparse_w, expert_out) + x
        mu = out.mean(-1, keepdims=True)
        var = ((out - mu) ** 2).mean(-1, keepdims=True)
        return (out - mu) * jax.lax.rsqrt(var + EPS) * gamma + beta
    edge_index = jnp.stack([src, dst])
    x = x + _L0_gnn_ref(_layernorm(x, axis=-1), edge_index, L0_gnn_weight, L0_gnn_bias)
    x = x + _L0_ffn_ref(_layernorm(x, axis=-1)[None])[0]
    x = x + _L1_gnn_ref(_layernorm(x, axis=-1), edge_index, edge_attr_64, L1_gnn_W1, L1_gnn_b1, L1_gnn_W2, L1_gnn_b2, L1_gnn_W3, L1_gnn_b3, L1_gnn_W4, L1_gnn_b4, L1_gnn_gamma, L1_gnn_beta)
    x = x + _L1_ffn_ref(_layernorm(x, axis=-1)[None], L1_ffn_Wg, L1_ffn_bg, L1_ffn_W1, L1_ffn_b1, L1_ffn_W2, L1_ffn_b2, L1_ffn_gamma, L1_ffn_beta)[0]
    return x

_drawn_inputs = setup_inputs


def setup_inputs(seed=0):
    import zlib

    import numpy as np

    out = dict(_drawn_inputs(seed))
    spreads = {'L0_gnn_bias': (0.0, 0.1),
     'L1_gnn_b1': (0.0, 0.278),
     'L1_gnn_b2': (0.0, 0.1),
     'L1_gnn_b3': (0.0, 2.0),
     'L1_gnn_b4': (0.0, 0.8),
     'L1_gnn_gamma': (1.0, 0.2),
     'L1_gnn_beta': (0.0, 0.335),
     'L1_ffn_bg': (0.0, 0.8),
     'L1_ffn_b1': (0.0, 0.8),
     'L1_ffn_b2': (0.0, 0.8),
     'L1_ffn_gamma': (1.0, 0.2),
     'L1_ffn_beta': (0.0, 0.448)}
    factors = {'edge_attr_64': 4.309, 'L1_ffn_Wg': 8.0, 'L1_ffn_W1': 8.0, 'L1_ffn_W2': 8.0}
    for name, (base, spread) in spreads.items():
        noise = np.random.default_rng([zlib.crc32(name.encode()), seed]).standard_normal(out[name].shape)
        drawn = base * np.exp(spread * noise) if base else spread * noise
        out[name] = jnp.asarray(drawn.astype(out[name].dtype))
    for name, factor in factors.items():
        out[name] = (out[name] * factor).astype(out[name].dtype)
    return out
```

```python
from contextlib import ExitStack

import concourse.bass as bass
from concourse import mybir

F32 = mybir.dt.float32
F32R = mybir.dt.float32r
BF16 = mybir.dt.bfloat16
I32 = mybir.dt.int32
U32 = mybir.dt.uint32
ALU = mybir.AluOpType
ACT = mybir.ActivationFunctionType
AX = mybir.AxisListType

P = 128
EPS = 1e-5
EXP_CAP = float(2 ** 30)
HOT = 0.5


def gnn_ffn_stack(nc, x, src, dst, edge_attr, w0, b0, w1, b1, w2, b2, w3, b3, w4, b4, gamma1, beta1,
                  wg, bg, fw1, fb1, fw2, fb2, gamma2, beta2, out):
    N, D = x.shape
    E, EA = edge_attr.shape
    NC, DC = N // P, D // P
    NT = E // P
    SE = 512
    TPS = SE // P
    NS = E // SE
    CT = 8
    EX = wg.shape[1]
    EH = fw1.shape[2]
    HC = 512
    XS = HC // EH
    FS = EX * EH // HC
    assert (NC, DC, P % EA, NS % 2) == (2, 4, 0, 0)

    with ExitStack() as ctx:
        def sem(name):
            return ctx.enter_context(nc.semaphore(name))

        cursor = [(nc.sbuf_base + 31) // 32 * 32]

        def sb(name, shape, dt):
            size = 4 if dt in (F32, F32R, I32, U32) else 2
            for n in shape[1:]:
                size *= n
            t = nc.alloc_sbuf_tensor_at(name, shape, dt, offset=cursor[0])
            cursor[0] += (size + 31) // 32 * 32
            return t

        ident = sb("ident", [P, P], F32)
        zeros_pp = sb("zeros_pp", [P, P], F32)
        iota_i = sb("iota_i", [P, N], I32)
        iota_row = sb("iota_row", [P, N], F32)
        iota_bf = sb("iota_bf", [P, N], BF16)
        node_i = sb("node_i", [P, NC], I32)
        node_id = sb("node_id", [P, NC], F32)
        minus_half = sb("minus_half", [P, NC], F32)
        gate = sb("gate", [P, 1], F32)
        idx_cols = sb("idx_cols", [P, 2, NT], F32)
        x2 = sb("x2", [P, NC, D], F32)
        z = sb("z", [P, NC, D], F32)
        zT = sb("zT", [P, DC, N], F32)
        stats = sb("stats", [P, 5, NC, 6], F32)
        moments = sb("moments", [P, 5, NC, 2], F32)
        var_eps = sb("var_eps", [P, 5, NC], F32)
        rstd = sb("rstd", [P, 5, NC], F32)
        shared = cursor[0]

        eaT = sb("eaT", [P, E], F32R)
        eaT_end = cursor[0]
        w2_hi = sb("w2_hi", [P, DC, D], F32R)
        w2_lo = sb("w2_lo", [P, DC, D], F32R)
        w1c_hi = sb("w1c_hi", [P, D], F32R)
        w1c_lo = sb("w1c_lo", [EA, D], F32R)
        xs_at = cursor[0]
        xs_hi = sb("xs_hi", [P, NC, D], F32R)
        xs_lo = sb("xs_lo", [P, NC, D], F32R)
        xd_at = cursor[0]
        xd_hi = sb("xd_hi", [P, NC, D], F32R)
        xd_lo = sb("xd_lo", [P, NC, D], F32R)
        ohT = sb("ohT", [P, 2, 2, NC, SE], F32R)
        idx_rows = sb("idx_rows", [P, 2, 2, SE], I32)
        ohd_at = cursor[0]
        ohd = sb("ohd", [P, 2, TPS, N], F32R)
        b2_rows = sb("b2_rows", [P, D], F32)
        over = cursor[0]
        h_hi = sb("h_hi", [P, 2, DC, SE], F32R)
        h_lo = sb("h_lo", [P, 2, DC, SE], F32R)
        m_hi = sb("m_hi", [P, 2, 2, D], F32R)
        m_lo = sb("m_lo", [P, 2, 2, D], F32R)
        t1 = sb("t1", [P, 2, 2, SE], F32)
        t2 = sb("t2", [P, 2, 2, D], F32)
        pre2 = sb("pre2", [P, 2, 2, D], F32)
        edge_end = cursor[0]

        cursor[0] = over
        xin = sb("xin", [P, NC, D], F32)
        xn = sb("xn", [P, NC, D], F32)
        xn_hi = sb("xn_hi", [P, NC, D], F32R)
        xn_lo = sb("xn_lo", [P, NC, D], F32R)
        w0_sb = sb("w0_sb", [P, DC, D], F32)
        w1_sb = sb("w1_sb", [P, 2, DC, D], F32)
        b0_rows = sb("b0_rows", [P, D], F32)
        b1_rows = sb("b1_rows", [P, D], F32)
        idx_i = sb("idx_i", [NT, 2, P], I32)
        idx_f = sb("idx_f", [NT, 2, P], F32)
        adj = sb("adj", [P, NC, N], F32R)
        counts = sb("counts", [P, NC, N], F32)
        eye = sb("eye", [P, NC, N], F32)
        deg = sb("deg", [P, NC], F32)
        dinv = sb("dinv", [P, NC], F32)
        aggT0 = sb("aggT0", [P, DC, N], F32)
        x1 = sb("x1", [P, NC, D], F32)
        y1 = sb("y1", [P, NC, D], F32)
        bits = sb("bits", [P, 16, NC], F32)
        ibits = sb("ibits", [P, 8, NC], I32)
        hot = sb("hot", [P, NC, P], F32)
        ramp_i = sb("ramp_i", [P, 48], I32)
        ramp = sb("ramp", [P, NC, 3, 16], F32)
        ranked = sb("ranked", [P, NC, 3, 16], F32)
        code = sb("code", [P, NC, 3], F32)
        digit = sb("digit", [P, 16], F32)
        adds = sb("adds", [P, NC, 2, 16], F32)
        prologue_end = cursor[0]
        oh_s = sb("oh_s", [P, 2, CT, N], BF16)
        oh_d = sb("oh_d", [P, 2, CT, N], BF16)
        w1c_raw = sb("w1c_raw", [P, D], F32)
        assert max(cursor[0], edge_end) <= nc.sbuf_usable_end, (cursor[0], edge_end)
        ea_hl = nc.alloc_sbuf_tensor_at("ea_hl", [P, 16, 2, EA], F32R, offset=ohd_at)
        ea_raw = nc.alloc_sbuf_tensor_at("ea_raw", [P, 16, EA], F32, offset=xs_at)
        w2_raw = nc.alloc_sbuf_tensor_at("w2_raw", [P, DC, D], F32, offset=xd_at)

        cursor[0] = shared
        w3_sb = sb("w3_sb", [P, 2 * DC, D], F32)
        w4_sb = sb("w4_sb", [P, DC, D], F32)
        b4_rows = sb("b4_rows", [P, D], F32)
        b3_nat = sb("b3_nat", [DC, P], F32)
        assert cursor[0] <= eaT_end
        cursor[0] = eaT_end
        b3_cols = sb("b3_cols", [P, DC], F32)
        gamma1_rows = sb("gamma1_rows", [P, D], F32)
        beta1_rows = sb("beta1_rows", [P, D], F32)
        gamma2_rows = sb("gamma2_rows", [P, D], F32)
        beta2_rows = sb("beta2_rows", [P, D], F32)
        agg = sb("agg", [P, NC, D], F32)
        aggT = sb("aggT", [P, DC, N], F32)
        pre_u = sb("pre_u", [P, DC, N], F32)
        uT = sb("uT", [P, DC, N], F32)
        y4 = sb("y4", [P, NC, D], F32)
        x3 = sb("x3", [P, NC, D], F32)
        tok = sb("tok", [P, NC, D], F32)
        tokT = sb("tokT", [P, DC, N], F32)
        wg_sb = sb("wg_sb", [P, DC, EX], F32)
        bg_rows = sb("bg_rows", [P, EX], F32)
        logits = sb("logits", [P, NC, EX], F32)
        probs = sb("probs", [P, NC, EX], F32)
        top = sb("top", [P, NC, 8], F32)
        top_at = sb("top_at", [P, NC, 8], U32)
        top_atf = sb("top_atf", [P, NC, 8], F32)
        chosen = sb("chosen", [P, NC, EX], F32)
        gates = sb("gates", [P, NC, EX], F32)
        gatesT = sb("gatesT", [EX, N], F32)
        small = sb("small", [P, 4, NC], F32)
        fb1_row = sb("fb1_row", [1, EX * EH], F32)
        ones_row = sb("ones_row", [1, P], F32)
        fb2_sb = sb("fb2_sb", [EX, D], F32)
        g_sb = sb("g_sb", [P, 2, HC], F32)
        gT = sb("gT", [P, HC // P, N], F32)
        y5 = sb("y5", [P, NC, D], F32)
        fin = sb("fin", [P, NC, D], F32)
        RW = 4
        fw1_sb = sb("fw1_sb", [P, RW, XS, DC, EH], F32)
        fw2_sb = sb("fw2_sb", [P, RW, HC // P, D], F32)
        assert cursor[0] <= nc.sbuf_usable_end, cursor[0]

        pa, pb, pc, pg = (ctx.enter_context(nc.psum_tensor(n, [P, 2, 512], F32)) for n in ("pa", "pb", "pc", "pg"))
        l1_ps = (pa, pb)

        ld_idx, ld_x, ld_ea, ld_w0, ld_b0, ld_w1, ld_b1, ld_rows, ld_w2, ld_w1c, ld_b2 = map(sem, (
            "ld_idx", "ld_x", "ld_ea", "ld_w0", "ld_b0", "ld_w1", "ld_b1", "ld_rows0", "ld_w2", "ld_w1c", "ld_b2"))
        ld_rows = (ld_rows, sem("ld_rows1"))
        ld_w3, ld_w4, ld_b3, ld_b4, ld_affine, ld_wg, ld_bias_ffn, ld_fw1, ld_fw2 = map(sem, (
            "ld_w3", "ld_w4", "ld_b3", "ld_b4", "ld_affine", "ld_wg", "ld_bias_ffn", "ld_fw1", "ld_fw2"))
        ld_fw1 = [ld_fw1] + [sem(f"ld_fw1_{k}") for k in range(1, RW)]
        ld_fw2 = [ld_fw2] + [sem(f"ld_fw2_{k}") for k in range(1, RW)]
        consts, idx_f_ready, idxT_ps, idx_cols_ready, dve_link, onehots, counted = map(sem, (
            "consts", "idx_f_ready", "idxT_ps", "idx_cols_ready", "dve_link", "onehots", "counted"))
        pool_link, act_link = map(sem, ("pool_link", "act_link"))
        counts_ready, countsT_ps, adj_ready, deg_ready, dinv_ready, var_ready, rstd_ready = map(sem, (
            "counts_ready", "countsT_ps", "adj_ready", "deg_ready", "dinv_ready", "var_ready", "rstd_ready"))
        xn_split, agg0_ps, agg0_ready, conv_ps, z_ready, zT_ps, zT_ready, xw_ps = map(sem, (
            "xn_split", "agg0_ps", "agg0_ready", "conv_ps", "z_ready", "zT_ps", "zT_ready", "xw_ps"))
        ea_hi_ready, ea_lo_ready, eaT_ps, eaT_ready, w_hi_ready, w_lo_ready, xw_hi, xw_lo, xd_sum = map(sem, (
            "ea_hi_ready", "ea_lo_ready", "eaT_ps", "eaT_ready", "w_hi_ready", "w_lo_ready", "xw_hi", "xw_lo", "xd_sum"))
        ohT_ready, ohd_ready, agg_done = map(sem, ("ohT_ready", "ohd_ready", "agg_done"))
        l1 = {k: sem("l1_" + k) for k in ("psum", "exp", "cap", "n", "ln", "r", "w", "y", "hi", "lo")}
        l2 = {k: sem("l2_" + k) for k in ("psum", "pre", "exp", "cap", "n", "ln", "r", "w", "y", "hi", "lo")}
        agg_ready, aggT_ps, aggT_ready, b3T_ps, b3_ready, u_ps, u_exp, u_cap, u_n, u_r, u_ready = map(sem, (
            "agg_ready", "aggT_ps", "aggT_ready", "b3T_ps", "b3_ready", "u_ps", "u_exp", "u_cap", "u_n", "u_r", "u_ready"))
        u_pre, out4_ps, tok_ready, tokT_ps, tokT_ready, logits_ps, neg_max, exp_sum, gates_ready, gatesT_ps, gatesT_ready = map(sem, (
            "u_pre", "out4_ps", "tok_ready", "tokT_ps", "tokT_ready", "logits_ps", "neg_max", "exp_sum", "gates_ready", "gatesT_ps", "gatesT_ready"))
        f1_ps, f1_g, gT_ps, gT_ready, f2_ps, f2_done, fin_ready, stored = map(sem, (
            "f1_ps", "f1_g", "gT_ps", "gT_ready", "f2_ps", "f2_done", "fin_ready", "stored"))

        by_node = lambda a: a.rearrange("(c p) d -> p c d", p=P)
        rows = lambda a, n: a.unsqueeze(0).broadcast_to((P, n))

        block = ctx.enter_context(nc.Block())

        @block.sync
        def _(sp):
            for k, idx in enumerate((src, dst)):
                sp.dma_start(idx_i[:, k, :], idx.rearrange("(t p) -> t p", p=P)).then_inc(ld_idx, 16)
            sp.dma_start(xin[:, :, :], by_node(x)).then_inc(ld_x, 16)
            ea_tiles = edge_attr.rearrange("(t p) a -> p t a", p=P)
            for c in range(NT // 16):
                if c:
                    sp.wait_ge(ea_lo_ready, c)
                sp.dma_start(ea_raw[:, :, :], ea_tiles[:, 16 * c:16 * c + 16, :]).then_inc(ld_ea, 16)
                if c == 0:
                    sp.dma_start(w0_sb[:, :, :], w0.rearrange("(k p) n -> p k n", p=P)).then_inc(ld_w0, 16)
                    sp.dma_start(b0_rows[:, :], rows(b0, D)).then_inc(ld_b0, 16)
                    sp.dma_start(w1_sb[:, :, :, :], w1[0:2 * D, :].rearrange("(g k p) n -> p g k n", g=2, p=P)).then_inc(ld_w1, 16)
                    sp.dma_start(b1_rows[:, :], rows(b1, D)).then_inc(ld_b1, 16)
                    for half in range(2):
                        sp.dma_start(w1c_raw[half * EA:half * EA + EA, :], w1[2 * D:2 * D + EA, :]).then_inc(ld_w1c, 16)
                    sp.dma_start(w2_raw[:, :, :], w2.rearrange("(k p) n -> p k n", p=P)).then_inc(ld_w2, 16)
                    sp.dma_start(b2_rows[:, :], rows(b2, D)).then_inc(ld_b2, 16)

            def load_idx_rows(s, parity):
                for k, idx in enumerate((src, dst)):
                    sp.dma_start(idx_rows[:, parity, k, :], rows(idx[bass.ts(s, SE)], SE)).then_inc(ld_rows[parity], 16)

            load_idx_rows(0, 0)
            load_idx_rows(1, 1)
            with sp.Fori(1, NS // 2) as i:
                for parity in range(2):
                    sp.wait_ge(ohT_ready, 2 * i + parity - 1)
                    load_idx_rows(2 * i + parity, parity)

            sp.wait_ge(l1["psum"], 2 * NS)
            sp.dma_start(b3_nat[:, :], b3.rearrange("(c p) -> c p", p=P)).then_inc(ld_b3, 16)
            sp.dma_start(w3_sb[:, :, :], w3.rearrange("(k p) n -> p k n", p=P)).then_inc(ld_w3, 16)
            sp.dma_start(w4_sb[:, :, :], w4.rearrange("(k p) n -> p k n", p=P)).then_inc(ld_w4, 16)
            sp.dma_start(b4_rows[:, :], rows(b4, D)).then_inc(ld_b4, 16)
            sp.wait_ge(agg_done, NS)
            for t, a in ((gamma1_rows, gamma1), (beta1_rows, beta1), (gamma2_rows, gamma2), (beta2_rows, beta2)):
                sp.dma_start(t[:, :], rows(a, D)).then_inc(ld_affine, 16)
            sp.dma_start(wg_sb[:, :, :], wg.rearrange("(p k) e -> p k e", k=DC)).then_inc(ld_wg, 16)
            sp.dma_start(bg_rows[:, :], rows(bg, EX)).then_inc(ld_wg, 16)
            sp.dma_start(fb1_row[:, :], fb1.rearrange("e h -> (e h)").unsqueeze(0)).then_inc(ld_bias_ffn, 16)
            sp.dma_start(fb2_sb[:, :], fb2).then_inc(ld_bias_ffn, 16)
            fw1_steps = fw1.rearrange("e (p k) h -> p e k h", k=DC)
            fw2_steps = fw2.rearrange("(f e) h d -> f (e h) d", f=FS).rearrange("f (j p) d -> f p j d", p=P)
            for f in range(FS):
                if f >= RW:
                    sp.wait_ge(f1_ps, f - RW + 1)
                sp.dma_start(fw1_sb[:, f % RW], fw1_steps[:, f * XS:f * XS + XS]).then_inc(ld_fw1[f % RW], 16)
                if f >= RW:
                    sp.wait_ge(f2_ps, f - RW + 1)
                sp.dma_start(fw2_sb[:, f % RW], fw2_steps[f]).then_inc(ld_fw2[f % RW], 16)
            for c in range(NC):
                sp.wait_ge(fin_ready, c + 1)
                sp.dma_start(by_node(out)[:, c, :], fin[:, c, :]).then_inc(stored, 16)
            sp.wait_ge(stored, 16 * NC)

        @block.gpsimd
        def _(pool):
            linked = [0]

            def link(ins):
                linked[0] += 1
                ins.then_inc(pool_link, 1)
                pool.wait_ge(pool_link, linked[0])

            link(pool.memset(zeros_pp[:, :], 0.0))
            pool.affine_select(out=ident[:, :], in_=zeros_pp[:, :], compare_op=ALU.not_equal, fill=1.0,
                               base=0, pattern=[[-1, P]], channel_multiplier=1).then_inc(consts, 1)
            pool.iota(iota_i[:, :], pattern=[[1, N]], base=0, channel_multiplier=0).then_inc(consts, 1)
            pool.iota(node_i[:, :], pattern=[[P, NC]], base=0, channel_multiplier=1).then_inc(consts, 1)
            pool.iota(ramp_i[:, :], pattern=[[0, 3], [-1, 16]], base=16, channel_multiplier=0).then_inc(consts, 1)
            pool.memset(minus_half[:, :], -0.5).then_inc(consts, 1)
            link(pool.memset(eye[:, :, :], 0.0))
            for c in range(NC):
                pool.affine_select(out=eye[:, c, :], in_=eye[:, c, :], compare_op=ALU.not_equal, fill=1.0,
                                   base=c * P, pattern=[[-1, N]], channel_multiplier=1).then_inc(consts, 1)

            def inverse_root(which, ready, ready_at, result, done):
                pool.wait_ge(ready, ready_at)
                pool.tensor_tensor(result, which, minus_half[:, :], ALU.pow).then_inc(done, 1)

            inverse_root(var_eps[:, 0, :], var_ready, 1, rstd[:, 0, :], rstd_ready)

            def ea_low(c):
                pool.wait_ge(ea_hi_ready, c + 1)
                pool.tensor_tensor(ea_hl[:, :, 1, :], ea_raw[:, :, :], ea_hl[:, :, 0, :].bitcast(F32),
                                   ALU.subtract).then_inc(ea_lo_ready, 1)

            ea_low(0)
            ea_low(1)
            ea_low(2)
            ea_low(3)
            inverse_root(deg[:, :], deg_ready, 1, dinv[:, :], dinv_ready)
            pool.wait_ge(w_hi_ready, 1)
            pool.tensor_tensor(w1c_lo[:, :], w1c_raw[0:EA, :], w1c_hi[0:EA, :].bitcast(F32), ALU.subtract).then_inc(w_lo_ready, 1)
            pool.wait_ge(w_hi_ready, 2)
            inverse_root(var_eps[:, 1, :], var_ready, 2, rstd[:, 1, :], rstd_ready)
            inverse_root(var_eps[:, 2, :], var_ready, 3, rstd[:, 2, :], rstd_ready)
            pool.tensor_tensor(w2_lo[:, :, :], w2_raw[:, :, :], w2_hi[:, :, :].bitcast(F32), ALU.subtract).then_inc(w_lo_ready, 1)

            def cap(layer, t, u, half):
                pool.wait_ge(layer["exp"], u + 1)
                pool.tensor_tensor(gate[:, :], minus_half[:, 0:1], minus_half[:, 0:1], ALU.mult)
                pool.tensor_scalar(t[:, half], t[:, half], EXP_CAP, 0.0, ALU.min, ALU.max).then_inc(layer["cap"], 1)

            def low(layer, t, hi, lo, u, half):
                pool.wait_ge(layer["hi"], u + 1)
                pool.tensor_tensor(lo, t[:, half], hi.bitcast(F32), ALU.subtract).then_inc(layer["lo"], 1)

            def low1(s, parity, half):
                low(l1, t1, h_hi[:, parity, 2 * half:2 * half + 2, :], h_lo[:, parity, 2 * half:2 * half + 2, :], 2 * s + half, half)

            def low2(s, half):
                low(l2, t2, m_hi[:, half], m_lo[:, half], 2 * s + half, half)

            def step(s, parity, more):
                cap(l2, t2, 2 * s, 0)
                low1(s + 1, 1 - parity, 1) if more != "last" else low2(s - 1, 1)
                cap(l2, t2, 2 * s + 1, 1)
                low2(s, 0)
                if more == "yes":
                    cap(l1, t1, 2 * s + 4, 0)
                    low2(s, 1)
                    cap(l1, t1, 2 * s + 5, 1)
                    low1(s + 2, parity, 0)

            cap(l1, t1, 0, 0)
            cap(l1, t1, 1, 1)
            low1(0, 0, 0)
            cap(l1, t1, 2, 0)
            low1(0, 0, 1)
            cap(l1, t1, 3, 1)
            low1(1, 1, 0)
            step(0, 0, "yes")
            with pool.Fori(0, (NS - 4) // 2) as i:
                step(2 * i + 1, 1, "yes")
                step(2 * i + 2, 0, "yes")
            step(NS - 3, 1, "yes")
            step(NS - 2, 0, "no")
            step(NS - 1, 1, "last")
            low2(NS - 1, 1)

            pool.wait_ge(u_exp, 1)
            pool.tensor_scalar(uT[:, :, :], uT[:, :, :], EXP_CAP, 0.0, ALU.min, ALU.max).then_inc(u_cap, 1)
            pool.memset(ones_row[:, :], 1.0).then_inc(consts, 1)
            inverse_root(var_eps[:, 3, :], var_ready, 4, rstd[:, 3, :], rstd_ready)
            inverse_root(var_eps[:, 4, :], var_ready, 5, rstd[:, 4, :], rstd_ready)
            pool.wait_ge(var_ready, 6)
            pool.tensor_tensor(rstd[:, 0, :], var_eps[:, 0, :], minus_half[:, :], ALU.pow).then_inc(rstd_ready, 1)

        @block.scalar
        def _(act):
            def ea_high(c):
                act.wait_ge(ld_ea, 16 * (c + 1))
                if c:
                    act.wait_ge(eaT_ps, 4 * c)
                act.activation(ea_hl[:, :, 0, :], ea_raw[:, :, :], ACT.Copy).then_inc(ea_hi_ready, 1)

            def ea_out(c):
                for g in range(4):
                    n = 4 * c + g
                    act.wait_ge(eaT_ps, n + 1)
                    act.activation(eaT[:, bass.ts(n, 4 * P)], pb[:, n % 2, :], ACT.Copy).then_inc(eaT_ready, 1)

            ea_high(0)
            ea_out(0)
            ea_high(1)
            ea_out(1)
            act.wait_ge(ld_w1c, 32)
            act.activation(w1c_hi[:, :], w1c_raw[:, :], ACT.Copy).then_inc(w_hi_ready, 1)
            act.wait_ge(ld_w2, 16)
            act.activation(w2_hi[:, :, :], w2_raw[:, :, :], ACT.Copy).then_inc(w_hi_ready, 1)
            ea_high(2)
            ea_out(2)
            ea_high(3)
            ea_out(3)
            act.wait_ge(zT_ps, 1)
            act.activation(zT[:, :, :], pc.rearrange("p b (k n) -> p (b k) n", n=N), ACT.Copy).then_inc(zT_ready, 1)
            act.wait_ge(xw_ps, 1)
            act.activation(xs_hi[:, :, :], pa[:, :, :], ACT.Copy).then_inc(xw_hi, 1)
            act.wait_ge(xd_sum, 1)
            act.wait_ge(w_lo_ready, 2)
            act.activation(xd_hi[:, :, :], x1[:, :, :], ACT.Copy).then_inc(xw_hi, 1)

            def exp(layer, t, source, u, half, ready):
                act.wait_ge(ready, u + 1)
                act.activation(t[:, half], source, ACT.Exp).then_inc(layer["exp"], 1)

            def exp1(s, half, first=False):
                if not first:
                    act.wait_ge(l1["lo"], 2 * s + half - 1)
                exp(l1, t1, l1_ps[half][:, :, :], 2 * s + half, half, l1["psum"])

            def exp2(s, half, first=False):
                if not first:
                    act.wait_ge(l2["lo"], 2 * s + half - 1)
                exp(l2, t2, pre2[:, half], 2 * s + half, half, l2["pre"])

            def quotient(layer, t, u, half):
                act.wait_ge(layer["n"], u + 1)
                act.activation(t[:, half], t[:, half], ACT.Ln, bias=2.0).then_inc(layer["ln"], 1)
                act.wait_ge(layer["ln"], u + 1)
                act.activation(t[:, half], t[:, half], ACT.Exp, scale=-1.0).then_inc(layer["r"], 1)

            def high1(s, parity, half, first=False):
                act.wait_ge(l1["y"], 2 * s + half + 1)
                if not first:
                    act.wait_ge(l2["psum"], 2 * s - 2)
                act.activation(h_hi[:, parity, 2 * half:2 * half + 2, :], t1[:, half], ACT.Copy).then_inc(l1["hi"], 1)

            def high2(s, half, first=False):
                act.wait_ge(l2["y"], 2 * s + half + 1)
                if not first:
                    act.wait_ge(agg_done, s)
                act.activation(m_hi[:, half], t2[:, half], ACT.Copy).then_inc(l2["hi"], 1)

            def step(s, parity, more, first=False):
                exp2(s, 0, first)
                high1(s + 1, 1 - parity, 1, first) if more != "last" else high2(s - 1, 1)
                quotient(l2, t2, 2 * s, 0)
                exp2(s, 1, first)
                high2(s, 0, first)
                quotient(l2, t2, 2 * s + 1, 1)
                if more == "yes":
                    exp1(s + 2, 0)
                    high2(s, 1, first)
                    quotient(l1, t1, 2 * s + 4, 0)
                    exp1(s + 2, 1)
                    high1(s + 2, parity, 0)
                    quotient(l1, t1, 2 * s + 5, 1)

            exp1(0, 0, True)
            quotient(l1, t1, 0, 0)
            exp1(0, 1, True)
            high1(0, 0, 0, True)
            quotient(l1, t1, 1, 1)
            exp1(1, 0)
            high1(0, 0, 1, True)
            quotient(l1, t1, 2, 0)
            exp1(1, 1)
            high1(1, 1, 0, True)
            quotient(l1, t1, 3, 1)
            step(0, 0, "yes", True)
            with act.Fori(0, (NS - 4) // 2) as i:
                step(2 * i + 1, 1, "yes")
                step(2 * i + 2, 0, "yes")
            step(NS - 3, 1, "yes")
            step(NS - 2, 0, "no")
            step(NS - 1, 1, "last")
            high2(NS - 1, 1)

            act.wait_ge(agg_done, NS)
            act.activation(agg[:, :, :], pg[:, :, :], ACT.Copy).then_inc(agg_ready, 1)
            act.wait_ge(aggT_ps, 1)
            act.activation(aggT[:, :, :], pc.rearrange("p b (k n) -> p (b k) n", n=N), ACT.Copy).then_inc(aggT_ready, 1)
            act.wait_ge(u_pre, 1)
            act.activation(uT[:, :, :], pre_u[:, :, :], ACT.Exp).then_inc(u_exp, 1)
            act.wait_ge(u_n, 1)
            act.activation(uT[:, :, :], uT[:, :, :], ACT.Ln, bias=2.0).then_inc(act_link, 1)
            act.wait_ge(act_link, 1)
            act.activation(uT[:, :, :], uT[:, :, :], ACT.Exp, scale=-1.0).then_inc(u_r, 1)
            act.wait_ge(tokT_ps, 1)
            act.activation(tokT[:, :, :], pc.rearrange("p b (k n) -> p (b k) n", n=N), ACT.Copy).then_inc(tokT_ready, 1)
            for c in range(NC):
                act.wait_ge(neg_max, c + 1)
                act.activation(probs[:, c, :], logits[:, c, :], ACT.Exp, bias=small[:, 0, c:c + 1],
                               accum_out=small[:, 1, c:c + 1]).then_inc(exp_sum, 1)
            act.wait_ge(gatesT_ps, 1)
            act.activation(gatesT[:, :], pc[0:EX, 0, 0:N], ACT.Copy).then_inc(gatesT_ready, 1)
            for f in range(FS):
                act.wait_ge(gT_ps, f + 1)
                if f:
                    act.wait_ge(f2_ps, f)
                act.activation(gT[:, :, :], pc.rearrange("p b (k n) -> p (b k) n", n=N), ACT.Copy).then_inc(gT_ready, 1)

        @block.tensor
        def _(pe):
            def transposed(dest, source, rows_in):
                return pe.transpose(dest, source, ident[0:rows_in, 0:rows_in])

            pe.wait_ge(consts, 1)
            pe.wait_ge(idx_f_ready, 1)
            for k in range(2):
                last = transposed(pc[:, 0, k * NT:(k + 1) * NT], idx_f[:, k, :], NT)
            last.then_inc(idxT_ps, 1)

            def ea_transposes(c):
                pe.wait_ge(ea_lo_ready, c + 1)
                for g in range(4):
                    n = 4 * c + g
                    if n >= 2:
                        pe.wait_ge(eaT_ready, n - 1)
                    for j in range(4):
                        last = transposed(pb[:, n % 2, j * P:(j + 1) * P],
                                          ea_hl[:, 4 * g + j, :, :].rearrange("p h a -> p (h a)").bitcast(F32), P)
                    last.then_inc(eaT_ps, 1)

            def count(c, parity, start, stop):
                pe.wait_ge(onehots, c + 1)
                for t in range(CT):
                    for k in range(NC):
                        last = pe.matmul(pa[:, k, 0:N], oh_s[:, parity, t, k * P:(k + 1) * P], oh_d[:, parity, t, :],
                                         start=start and t == 0, stop=stop and t == CT - 1)
                last.then_inc(counted, 1)

            NCH = NT // CT
            for c in range(NCH):
                count(c, c % 2, c == 0, c == NCH - 1)
                if c % 2 == 1:
                    ea_transposes(c // 2)

            pe.wait_ge(counts_ready, 1)
            for k in range(NC):
                for j in range(NC):
                    last = transposed(pc[:, 1, k * N + j * P:k * N + (j + 1) * P], counts[:, j, k * P:(k + 1) * P], P)
            last.then_inc(countsT_ps, 1)

            pe.wait_ge(adj_ready, 1)
            pe.wait_ge(xn_split, 2)
            ps = pg.rearrange("p b (k n) -> p (b k) n", n=N)
            for c in range(DC):
                for n, (part, k) in enumerate(((part, k) for part in (xn_hi, xn_lo) for k in range(NC))):
                    last = pe.matmul(ps[:, c, :], part[:, k, c * P:(c + 1) * P], adj[:, k, :],
                                     start=n == 0, stop=n == 3)
            last.then_inc(agg0_ps, 1)
            pe.wait_ge(agg0_ready, 1)
            pe.wait_ge(ld_w0, 16)
            for n in range(NC):
                for k in range(DC):
                    last = pe.matmul(pa[:, n, :], aggT0[:, k, n * P:(n + 1) * P], w0_sb[:, k, :],
                                     start=k == 0, stop=k == DC - 1)
            last.then_inc(conv_ps, 1)

            def transposes(dest, source, ready, at, done, strided=False):
                pe.wait_ge(ready, at)
                view = dest.rearrange("p b (k n) -> p (b k) n", n=N)
                for n in range(NC):
                    for k in range(DC):
                        part = source[:, n, k::DC] if strided else source[:, n, k * P:(k + 1) * P]
                        last = transposed(view[:, k, n * P:(n + 1) * P], part, P)
                last.then_inc(done, 1)

            transposes(pc, z, z_ready, 1, zT_ps)
            pe.wait_ge(zT_ready, 1)
            pe.wait_ge(ld_w1, 16)
            for g, dest in enumerate((pa, pg)):
                for n in range(NC):
                    for k in range(DC):
                        last = pe.matmul(dest[:, n, :], zT[:, k, n * P:(n + 1) * P], w1_sb[:, g, k, :],
                                         start=k == 0, stop=k == DC - 1)
                last.then_inc(xw_ps, 1)

            def layer1(s, parity, half, first=False):
                if half == 0:
                    pe.wait_ge(ohT_ready, s + 1)
                if not first:
                    pe.wait_ge(l1["y"], 2 * s + half - 1)
                ea = eaT[:, bass.ts(s, SE)]
                ea_high = eaT[0:EA, bass.ts(s, SE)]
                for j in range(2):
                    c = 2 * half + j
                    cols = slice(c * P, (c + 1) * P)
                    dest = l1_ps[half][:, j, :]
                    for n, (part, which, k) in enumerate((part, which, k) for which, parts in enumerate(((xs_hi, xs_lo), (xd_hi, xd_lo)))
                                                         for k in range(NC) for part in parts):
                        pe.matmul(dest, part[:, k, cols], ohT[:, parity, which, k, :], start=n == 0, stop=False)
                    pe.matmul(dest, w1c_hi[:, cols], ea, start=False, stop=False)
                    last = pe.matmul(dest, w1c_lo[:, cols], ea_high, start=False, stop=True)
                last.then_inc(l1["psum"], 1)

            def layer2(s, parity, half, first=False):
                pe.wait_ge(l1["lo"], 2 * s + 2)
                if not first:
                    pe.wait_ge(l2["pre"], 2 * s + half)
                for j in range(2):
                    at = slice((2 * half + j) * P, (2 * half + j + 1) * P)
                    n = 0
                    for k in range(DC):
                        for a, b in ((h_hi, w2_hi), (h_hi, w2_lo), (h_lo, w2_hi)):
                            last = pe.matmul(pc[:, j, :], a[:, parity, k, at], b[:, k, :], start=n == 0, stop=n == 3 * DC - 1)
                            n += 1
                last.then_inc(l2["psum"], 1)

            def sum_messages(s, parity, first=False, final=False):
                pe.wait_ge(ohd_ready, s + 1)
                for half in range(2):
                    pe.wait_ge(l2["lo"], 2 * s + half + 1)
                    for j in range(2):
                        for n in range(NC):
                            for part in (m_hi, m_lo):
                                last = pe.matmul(pg[:, n, :], ohd[:, parity, 2 * half + j, n * P:(n + 1) * P], part[:, half, j, :],
                                                 start=first and half == 0 and j == 0 and part is m_hi,
                                                 stop=final and half == 1 and j == 1 and part is m_lo)
                last.then_inc(agg_done, 1)

            def step(s, parity, more, first=False, second=False):
                layer2(s, parity, 0, first)
                if not first:
                    sum_messages(s - 1, 1 - parity, first=second)
                layer2(s, parity, 1)
                if more == "yes":
                    layer1(s + 2, parity, 0)
                    layer1(s + 2, parity, 1)

            pe.wait_ge(xw_lo, 2)
            pe.wait_ge(w_lo_ready, 2)
            pe.wait_ge(eaT_ready, NT // 4)
            layer1(0, 0, 0, True)
            layer1(0, 0, 1, True)
            layer1(1, 1, 0)
            layer1(1, 1, 1)
            step(0, 0, "yes", first=True)
            step(1, 1, "yes", second=True)
            with pe.Fori(0, (NS - 6) // 2) as i:
                step(2 * i + 2, 0, "yes")
                step(2 * i + 3, 1, "yes")
            step(NS - 4, 0, "yes")
            step(NS - 3, 1, "yes")
            step(NS - 2, 0, "no")
            step(NS - 1, 1, "last")

            pe.wait_ge(ld_b3, 16)
            pe.wait_ge(l1["y"], 2 * NS)
            pe.wait_ge(l2["pre"], 2 * NS)
            transposed(pc[:, 0, 0:DC], b3_nat[:, :], DC).then_inc(b3T_ps, 1)
            pe.wait_ge(ld_w3, 16)
            u_bank = [l1_ps[c // 2][:, c % 2, 0:N] for c in range(DC)]
            for c in range(DC):
                for k in range(DC):
                    pe.matmul(u_bank[c], w3_sb[:, k, c * P:(c + 1) * P], zT[:, k, :], start=k == 0, stop=False)
            sum_messages(NS - 1, 1, final=True)
            pe.wait_ge(b3_ready, 1)
            transposes(pc, agg, agg_ready, 1, aggT_ps)
            pe.wait_ge(aggT_ready, 1)
            for c in range(DC):
                for k in range(DC):
                    last = pe.matmul(u_bank[c], w3_sb[:, DC + k, c * P:(c + 1) * P], aggT[:, k, :], start=False, stop=k == DC - 1)
                last.then_inc(u_ps, 1)
            pe.wait_ge(u_ready, 1)
            pe.wait_ge(ld_w4, 16)
            for n in range(NC):
                for k in range(DC):
                    last = pe.matmul(pg[:, n, :], uT[:, k, n * P:(n + 1) * P], w4_sb[:, k, :], start=k == 0, stop=k == DC - 1)
                last.then_inc(out4_ps, 1)

            transposes(pc, tok, tok_ready, 1, tokT_ps, strided=True)
            pe.wait_ge(tokT_ready, 1)
            pe.wait_ge(ld_wg, 32)
            for n in range(NC):
                for k in range(DC):
                    last = pe.matmul(pa[:, n, 0:EX], tokT[:, k, n * P:(n + 1) * P], wg_sb[:, k, :], start=k == 0, stop=k == DC - 1)
            last.then_inc(logits_ps, 1)

            def hidden(f):
                pe.wait_ge(ld_fw1[f % RW], 16 * (f // RW + 1))
                if f == 0:
                    pe.wait_ge(ld_bias_ffn, 32)
                    pe.wait_ge(consts, 8)
                if f == 1:
                    pe.wait_ge(neg_max, 2)
                if f >= 2:
                    pe.wait_ge(f1_g, 2 * (f - 1))
                dest = (pb, pa)[f % 2]
                for n in range(NC):
                    for k in range(DC):
                        pe.matmul(dest[:, n, :], tokT[:, k, n * P:(n + 1) * P], fw1_sb[:, f % RW, :, k, :], start=k == 0, stop=False)
                    last = pe.matmul(dest[:, n, :], ones_row[:, :], fb1_row[:, f * HC:(f + 1) * HC], start=False, stop=True)
                last.then_inc(f1_ps, 1)

            hidden(0)
            pe.wait_ge(gates_ready, 1)
            for n in range(NC):
                last = transposed(pc[0:EX, 0, n * P:(n + 1) * P], gates[:, n, :], P)
            last.then_inc(gatesT_ps, 1)
            hidden(1)
            pe.wait_ge(gatesT_ready, 1)
            for n in range(NC):
                pe.matmul(pg[:, n, :], gatesT[:, n * P:(n + 1) * P], fb2_sb[:, :], start=True, stop=False)
            for f in range(FS):
                pe.wait_ge(f1_g, 2 * (f + 1))
                if f:
                    pe.wait_ge(gT_ready, f)
                view = pc.rearrange("p b (k n) -> p (b k) n", n=N)
                for n in range(NC):
                    for k in range(HC // P):
                        last = transposed(view[:, k, n * P:(n + 1) * P], g_sb[:, n, k * P:(k + 1) * P], P)
                last.then_inc(gT_ps, 1)
                if f + 2 < FS:
                    hidden(f + 2)
                pe.wait_ge(gT_ready, f + 1)
                pe.wait_ge(ld_fw2[f % RW], 16 * (f // RW + 1))
                for n in range(NC):
                    for k in range(HC // P):
                        last = pe.matmul(pg[:, n, :], gT[:, k, n * P:(n + 1) * P], fw2_sb[:, f % RW, k, :],
                                         start=False, stop=f == FS - 1 and k == HC // P - 1)
                last.then_inc(f2_ps, 1)

        @block.vector
        def _(dve):
            linked = [0]

            def link(ins):
                linked[0] += 1
                ins.then_inc(dve_link, 1)
                dve.wait_ge(dve_link, linked[0])

            def layer_norm_moments(t, which):
                for c in range(NC):
                    last = dve.bn_stats(stats[:, which, c, :], t[:, c, :])
                link(last)
                for c in range(NC):
                    last = dve.bn_aggr(moments[:, which, c, :], stats[:, which, c, :])
                link(last)
                dve.tensor_scalar(var_eps[:, which % 5, :], moments[:, which, :, 1], EPS, None, ALU.add).then_inc(var_ready, 1)

            def normalise(dest, t, which, count):
                dve.wait_ge(rstd_ready, count)
                for c in range(NC):
                    last = dve.tensor_scalar(dest[:, c, :], t[:, c, :], moments[:, which, c, 0:1], rstd[:, which, c:c + 1],
                                             ALU.subtract, ALU.mult)
                return last

            dve.wait_ge(ld_idx, 32)
            dve.tensor_copy(idx_f[:, :, :], idx_i[:, :, :]).then_inc(idx_f_ready, 1)
            dve.wait_ge(consts, 5)
            dve.tensor_copy(iota_row[:, :], iota_i[:, :])
            dve.tensor_copy(iota_bf[:, :], iota_i[:, :])
            dve.tensor_copy(node_id[:, :], node_i[:, :])
            for c in range(NC):
                link(dve.tensor_copy(ramp[:, c, :, :], ramp_i[:, :].rearrange("p (f w) -> p f w", f=3)))
            dve.wait_ge(idxT_ps, 1)
            link(dve.tensor_copy(idx_cols[:, :, :], pc[:, 0, 0:2 * NT].rearrange("p (k t) -> p k t", k=2)))

            def onehots_of(c, parity, first=False):
                if not first:
                    dve.wait_ge(counted, c - 1)
                for t in range(CT):
                    for dest, k in ((oh_s, 0), (oh_d, 1)):
                        at = c * CT + t
                        last = dve.tensor_scalar(dest[:, parity, t, :], iota_bf[:, :], idx_cols[:, k, bass.ds(at, 1)], None, ALU.is_equal)
                last.then_inc(onehots, 1)

            onehots_of(0, 0, True)
            onehots_of(1, 1, True)
            dve.wait_ge(ld_x, 16)
            layer_norm_moments(xin, 0)
            with dve.Fori(1, NT // CT // 2) as i:
                onehots_of(2 * i, 0)
                onehots_of(2 * i + 1, 1)
            link(normalise(xn, xin, 0, 1))

            dve.wait_ge(counted, NT // CT)
            dve.tensor_copy(counts[:, :, :], pa[:, :, 0:N]).then_inc(counts_ready, 1)
            dve.wait_ge(counts_ready, 1)
            dve.wait_ge(countsT_ps, 1)
            link(dve.tensor_tensor(counts[:, :, :], pc[:, 1, :].rearrange("p (k n) -> p k n", n=N), counts[:, :, :], ALU.add))
            dve.wait_ge(consts, 7)
            dve.scalar_tensor_tensor(out=adj[:, :, :], in0=counts[:, :, :], scalar=1.0, in1=eye[:, :, :],
                                     op0=ALU.min, op1=ALU.add).then_inc(adj_ready, 1)
            dve.wait_ge(adj_ready, 1)
            dve.tensor_reduce(deg[:, :], adj[:, :, :].bitcast(F32), AX.X, ALU.add).then_inc(deg_ready, 1)
            dve.wait_ge(dinv_ready, 1)
            for c in range(NC):
                last = dve.tensor_scalar(xn[:, c, :], xn[:, c, :], dinv[:, c:c + 1], None, ALU.mult)
            link(last)
            dve.tensor_copy(xn_hi[:, :, :], xn[:, :, :]).then_inc(xn_split, 1)
            dve.wait_ge(xn_split, 1)
            dve.tensor_tensor(xn_lo[:, :, :], xn[:, :, :], xn_hi[:, :, :].bitcast(F32), ALU.subtract).then_inc(xn_split, 1)
            dve.wait_ge(ld_b0, 16)
            for c in range(NC):
                last = dve.tensor_tensor(x1[:, c, :], xin[:, c, :], b0_rows[:, :], ALU.add)
            link(last)
            dve.wait_ge(agg0_ps, 1)
            dve.tensor_copy(aggT0[:, :, :], pg.rearrange("p b (k n) -> p (b k) n", n=N)).then_inc(agg0_ready, 1)
            dve.wait_ge(conv_ps, 1)
            for c in range(NC):
                last = dve.scalar_tensor_tensor(out=x1[:, c, :], in0=pa[:, c, :], scalar=dinv[:, c:c + 1], in1=x1[:, c, :],
                                                op0=ALU.mult, op1=ALU.add)
            link(last)

            layer_norm_moments(x1, 1)
            link(normalise(y1, x1, 1, 2))
            link(dve.tensor_scalar(hot[:, :, :], y1[:, :, 0:P], HOT, None, ALU.is_gt))
            for c in range(NC):
                last = dve.tensor_tensor(ranked[:, c], hot[:, c, 64:112].rearrange("p (f w) -> p f w", f=3), ramp[:, c], ALU.mult)
            link(last)
            link(dve.tensor_reduce(code[:, :, :], ranked[:, :, :, :], AX.X, ALU.max))
            link(dve.tensor_scalar(code[:, :, :], code[:, :, :], -1.0, 16.0, ALU.mult, ALU.add))
            link(dve.scalar_tensor_tensor(out=code[:, :, :], in0=code[:, :, :], scalar=16.0, in1=code[:, :, :],
                                          op0=ALU.is_lt, op1=ALU.mult))
            lo, hi, amount = (code[:, :, f] for f in range(3))
            value_i, amount_i, shl_i, shr_i, low_i, high_i, res_i = (ibits[:, f, :] for f in range(7))
            do_shl, do_shr, shl_f, shr_f, active, res, low_f, high_f, not_shl, both = (bits[:, f, :] for f in range(10))
            dve.scalar_tensor_tensor(out=value_i, in0=hi, scalar=16.0, in1=lo, op0=ALU.mult, op1=ALU.add)
            link(dve.tensor_copy(amount_i, amount))
            dve.tensor_tensor(shl_i, value_i, amount_i, ALU.logical_shift_left)
            link(dve.tensor_tensor(shr_i, value_i, amount_i, ALU.logical_shift_right))
            link(dve.tensor_scalar(shl_i, shl_i, 255, None, ALU.bitwise_and))
            dve.tensor_copy(shl_f, shl_i)
            dve.tensor_copy(shr_f, shr_i)
            dve.tensor_scalar(not_shl, hot[:, :, 39], -1.0, 1.0, ALU.mult, ALU.add)
            dve.tensor_tensor(do_shl, hot[:, :, 0], hot[:, :, 39], ALU.mult)
            link(dve.tensor_tensor(do_shr, hot[:, :, 0], hot[:, :, 40], ALU.mult))
            link(dve.tensor_tensor(do_shr, do_shr, not_shl, ALU.mult))
            dve.tensor_tensor(active, do_shl, do_shr, ALU.add)
            dve.tensor_tensor(res, do_shl, shl_f, ALU.mult)
            link(dve.tensor_tensor(both, do_shr, shr_f, ALU.mult))
            link(dve.tensor_tensor(res_i, res, both, ALU.add))
            dve.tensor_scalar(low_i, res_i, 15, None, ALU.bitwise_and)
            link(dve.tensor_scalar(high_i, res_i, 4, None, ALU.logical_shift_right))
            dve.tensor_copy(low_f, low_i)
            dve.tensor_copy(high_f, high_i)
            link(dve.tensor_scalar(active, active, 2.0, None, ALU.mult))
            for c in range(NC):
                for f, digit_f in enumerate((low_f, high_f)):
                    last = dve.tensor_scalar(adds[:, c, f, :], iota_row[:, 0:16], digit_f[:, c:c + 1], active[:, c:c + 1],
                                             ALU.is_equal, ALU.mult)
            link(last)
            link(dve.tensor_tensor(y1[:, :, 128:160], y1[:, :, 128:160], adds[:, :, :, :].rearrange("p c f w -> p c (f w)"), ALU.add))
            link(dve.tensor_tensor(x2[:, :, :], x1[:, :, :], y1[:, :, :], ALU.add))

            layer_norm_moments(x2, 2)
            normalise(z, x2, 2, 3).then_inc(z_ready, 1)

            def node_onehots(s, parity, first=False):
                dve.wait_ge(ld_rows[parity], 16 * (s - parity) + 32)
                if not first:
                    dve.wait_ge(l1["psum"], 2 * s - 2)
                for which in range(2):
                    for k in range(NC):
                        last = dve.tensor_scalar(ohT[:, parity, which, k, :], idx_rows[:, parity, which, :], node_id[:, k:k + 1], None, ALU.is_equal)
                last.then_inc(ohT_ready, 1)

            def dst_onehots(s, parity, first=False):
                if not first:
                    dve.wait_ge(agg_done, s - 1)
                for t in range(TPS):
                    last = dve.tensor_scalar(ohd[:, parity, t, :], iota_row[:, :], idx_cols[:, 1, bass.ds(s * TPS + t, 1)], None, ALU.is_equal)
                last.then_inc(ohd_ready, 1)

            node_onehots(0, 0, True)
            node_onehots(1, 1, True)
            dve.wait_ge(ld_b1, 16)
            dve.wait_ge(xw_ps, 2)
            for c in range(NC):
                last = dve.tensor_tensor(x1[:, c, :], pg[:, c, :], b1_rows[:, :], ALU.add)
            last.then_inc(xd_sum, 1)
            dve.wait_ge(xw_hi, 1)
            dve.tensor_tensor(xs_lo[:, :, :], pa[:, :, :], xs_hi[:, :, :].bitcast(F32), ALU.subtract).then_inc(xw_lo, 1)
            dve.wait_ge(xw_hi, 2)
            dve.tensor_tensor(xd_lo[:, :, :], x1[:, :, :], xd_hi[:, :, :].bitcast(F32), ALU.subtract).then_inc(xw_lo, 1)

            def n_of(layer, t, u, half):
                dve.wait_ge(layer["cap"], u + 1)
                dve.scalar_tensor_tensor(out=t[:, half], in0=t[:, half], scalar=2.0, in1=t[:, half],
                                         op0=ALU.add, op1=ALU.mult).then_inc(layer["n"], 1)

            def finish(layer, t, pre, u, half):
                dve.wait_ge(layer["r"], u + 1)
                dve.scalar_tensor_tensor(out=t[:, half], in0=t[:, half], scalar=-2.0, in1=pre,
                                         op0=ALU.mult, op1=ALU.mult).then_inc(layer["w"], 1)
                dve.wait_ge(layer["w"], u + 1)
                dve.tensor_tensor(t[:, half], t[:, half], pre, ALU.add).then_inc(layer["y"], 1)

            def n1(s, half):
                n_of(l1, t1, 2 * s + half, half)

            def n2(s, half):
                n_of(l2, t2, 2 * s + half, half)

            def finish1(s, half):
                finish(l1, t1, l1_ps[half][:, :, :], 2 * s + half, half)

            def finish2(s, half):
                finish(l2, t2, pre2[:, half], 2 * s + half, half)

            def with_bias(s, half, first=False):
                dve.wait_ge(l2["psum"], 2 * s + half + 1)
                if not first:
                    dve.wait_ge(l2["y"], 2 * s + half - 1)
                for j in range(2):
                    last = dve.tensor_tensor(pre2[:, half, j, :], pc[:, j, :], b2_rows[:, :], ALU.add)
                last.then_inc(l2["pre"], 1)

            def step(s, parity, more, first=False):
                if more == "yes":
                    node_onehots(s + 2, parity)
                with_bias(s, 0, first)
                finish1(s + 1, 1) if more != "last" else finish2(s - 1, 1)
                n2(s, 0)
                dst_onehots(s, parity, first)
                with_bias(s, 1, first)
                finish2(s, 0)
                n2(s, 1)
                if more == "yes":
                    finish2(s, 1)
                    n1(s + 2, 0)
                    finish1(s + 2, 0)
                    n1(s + 2, 1)

            dve.wait_ge(ld_b2, 16)
            n1(0, 0)
            finish1(0, 0)
            n1(0, 1)
            finish1(0, 1)
            n1(1, 0)
            finish1(1, 0)
            n1(1, 1)
            step(0, 0, "yes", True)
            with dve.Fori(0, (NS - 4) // 2) as i:
                step(2 * i + 1, 1, "yes")
                step(2 * i + 2, 0, "yes")
            step(NS - 3, 1, "yes")
            step(NS - 2, 0, "no")
            step(NS - 1, 1, "last")
            finish2(NS - 1, 1)

            dve.wait_ge(agg_done, NS)
            dve.wait_ge(b3T_ps, 1)
            dve.tensor_copy(b3_cols[:, :], pc[:, 0, 0:DC]).then_inc(b3_ready, 1)
            dve.wait_ge(b3_ready, 1)
            dve.wait_ge(u_ps, DC)
            for c in range(DC):
                last = dve.tensor_scalar(pre_u[:, c, :], l1_ps[c // 2][:, c % 2, 0:N], b3_cols[:, c:c + 1], None, ALU.add)
            last.then_inc(u_pre, 1)
            dve.wait_ge(u_cap, 1)
            dve.scalar_tensor_tensor(out=uT[:, :, :], in0=uT[:, :, :], scalar=2.0, in1=uT[:, :, :],
                                     op0=ALU.add, op1=ALU.mult).then_inc(u_n, 1)
            dve.wait_ge(ld_b4, 16)
            for c in range(NC):
                last = dve.tensor_tensor(y4[:, c, :], z[:, c, :], b4_rows[:, :], ALU.add)
            link(last)
            dve.wait_ge(u_r, 1)
            link(dve.scalar_tensor_tensor(out=uT[:, :, :], in0=uT[:, :, :], scalar=-2.0, in1=pre_u[:, :, :],
                                          op0=ALU.mult, op1=ALU.mult))
            dve.tensor_tensor(uT[:, :, :], uT[:, :, :], pre_u[:, :, :], ALU.add).then_inc(u_ready, 1)

            def affine(t, gain, shift, base, dest):
                for op, other in ((ALU.mult, gain), (ALU.add, shift)):
                    for c in range(NC):
                        last = dve.tensor_tensor(t[:, c, :], t[:, c, :], other[:, :], op)
                    link(last)
                return [dve.tensor_tensor(dest[:, c, :], t[:, c, :], base[:, c, :], ALU.add) for c in range(NC)]

            dve.wait_ge(out4_ps, NC)
            link(dve.tensor_tensor(y4[:, :, :], pg[:, :, :], y4[:, :, :], ALU.add))
            layer_norm_moments(y4, 3)
            link(normalise(y4, y4, 3, 4))
            dve.wait_ge(ld_affine, 64)
            link(affine(y4, gamma1_rows, beta1_rows, x2, x3)[-1])
            layer_norm_moments(x3, 4)
            normalise(tok, x3, 4, 5).then_inc(tok_ready, 1)

            dve.wait_ge(logits_ps, 1)
            for c in range(NC):
                last = dve.tensor_tensor(logits[:, c, :], pa[:, c, 0:EX], bg_rows[:, :], ALU.add)
            link(last)
            link(dve.tensor_reduce(small[:, 2, :], logits[:, :, :], AX.X, ALU.max))
            dve.tensor_scalar(small[:, 0, :], small[:, 2, :], -1.0, None, ALU.mult).then_inc(neg_max, 2)
            dve.wait_ge(exp_sum, 2)
            link(dve.reciprocal(small[:, 3, :], small[:, 1, :]))
            for c in range(NC):
                last = dve.tensor_scalar(probs[:, c, :], probs[:, c, :], small[:, 3, c:c + 1], None, ALU.mult)
            link(last)
            for c in range(NC):
                last = dve.max(top[:, c, :], probs[:, c, :])
            link(last)
            for c in range(NC):
                last = dve.max_index(top_at[:, c, :], top[:, c, :], probs[:, c, :])
            link(last)
            link(dve.tensor_copy(top_atf[:, :, :], top_at[:, :, :]))
            for c in range(NC):
                last = dve.tensor_scalar(chosen[:, c, :], iota_row[:, 0:EX], top_atf[:, c, 0:1], None, ALU.is_equal)
            link(last)
            for c in range(NC):
                last = dve.scalar_tensor_tensor(out=chosen[:, c, :], in0=iota_row[:, 0:EX], scalar=top_atf[:, c, 1:2],
                                                in1=chosen[:, c, :], op0=ALU.is_equal, op1=ALU.add)
            link(last)
            dve.tensor_tensor(gates[:, :, :], probs[:, :, :], chosen[:, :, :], ALU.mult).then_inc(gates_ready, 1)
            dve.wait_ge(gates_ready, 1)

            for f in range(FS):
                dve.wait_ge(f1_ps, f + 1)
                if f:
                    dve.wait_ge(gT_ps, f)
                for c in range(NC):
                    gate = gates[:, c, f * XS:(f + 1) * XS].unsqueeze(2).broadcast_to((P, XS, EH))
                    dve.scalar_tensor_tensor(out=g_sb[:, c, :].rearrange("p (e h) -> p e h", h=EH),
                                             in0=(pb, pa)[f % 2][:, c, :].rearrange("p (e h) -> p e h", h=EH), scalar=0.0,
                                             in1=gate, op0=ALU.max, op1=ALU.mult).then_inc(f1_g, 1)

            dve.wait_ge(f2_ps, FS)
            link(dve.tensor_tensor(y5[:, :, :], pg[:, :, :], tok[:, :, :], ALU.add))
            layer_norm_moments(y5, 0)
            link(normalise(y5, y5, 0, 6))
            for ins in affine(y5, gamma2_rows, beta2_rows, x3, fin):
                ins.then_inc(fin_ready, 1)


_INS = ["x", "src", "dst", "edge_attr_64", "L0_gnn_weight", "L0_gnn_bias", "L1_gnn_W1", "L1_gnn_b1", "L1_gnn_W2",
        "L1_gnn_b2", "L1_gnn_W3", "L1_gnn_b3", "L1_gnn_W4", "L1_gnn_b4", "L1_gnn_gamma", "L1_gnn_beta", "L1_ffn_Wg",
        "L1_ffn_bg", "L1_ffn_W1", "L1_ffn_b1", "L1_ffn_W2", "L1_ffn_b2", "L1_ffn_gamma", "L1_ffn_beta"]


def kernel(**inputs):
    import numpy as _np
    import concourse.bacc as _bacc
    from concourse import mybir as _mybir
    from concourse.bass_utils import run_bass_kernel_spmd as _run

    nc = _bacc.Bacc("TRN2", target_bir_lowering=False, num_devices=1)
    arrays, args = {}, []
    for name in _INS:
        a = _np.ascontiguousarray(inputs[name])
        arrays[f"in_{name}_dram"] = a
        args.append(nc.dram_tensor(f"in_{name}_dram", a.shape, _mybir.dt.from_np(a.dtype), kind="ExternalInput").ap())
    out = nc.dram_tensor("out_0_dram", inputs["x"].shape, _mybir.dt.float32, kind="ExternalOutput").ap()
    gnn_ffn_stack(nc, *args, out)
    r = _run(nc, [arrays], core_ids=[0])
    return r.results[0]["out_0_dram"]
```

```python
from contextlib import ExitStack

import concourse.bass as bass
from concourse import mybir

F32 = mybir.dt.float32
F32R = mybir.dt.float32r
BF16 = mybir.dt.bfloat16
I32 = mybir.dt.int32
U32 = mybir.dt.uint32
ALU = mybir.AluOpType
ACT = mybir.ActivationFunctionType
AX = mybir.AxisListType

P = 128
EPS = 1e-5
EXP_CAP = float(2 ** 30)
HOT = 0.5


def gnn_ffn_stack(nc, x, src, dst, edge_attr, w0, b0, w1, b1, w2, b2, w3, b3, w4, b4, gamma1, beta1,
                  wg, bg, fw1, fb1, fw2, fb2, gamma2, beta2, out):
    N, D = x.shape
    E, EA = edge_attr.shape
    NC, DC = N // P, D // P
    NT = E // P
    SE = 512
    TPS = SE // P
    NS = E // SE
    CT = 8
    EX = wg.shape[1]
    EH = fw1.shape[2]
    HC = 512
    XS = HC // EH
    FS = EX * EH // HC
    assert (NC, DC, P % EA, NS % 2) == (2, 4, 0, 0)

    with ExitStack() as ctx:
        def sem(name):
            return ctx.enter_context(nc.semaphore(name))

        cursor = [(nc.sbuf_base + 31) // 32 * 32]

        def sb(name, shape, dt):
            size = 4 if dt in (F32, F32R, I32, U32) else 2
            for n in shape[1:]:
                size *= n
            t = nc.alloc_sbuf_tensor_at(name, shape, dt, offset=cursor[0])
            cursor[0] += (size + 31) // 32 * 32
            return t

        ident = sb("ident", [P, P], F32)
        zeros_pp = sb("zeros_pp", [P, P], F32)
        iota_i = sb("iota_i", [P, N], I32)
        iota_row = sb("iota_row", [P, N], F32)
        iota_bf = sb("iota_bf", [P, N], BF16)
        node_i = sb("node_i", [P, NC], I32)
        node_id = sb("node_id", [P, NC], F32)
        minus_half = sb("minus_half", [P, NC], F32)
        idx_cols = sb("idx_cols", [P, 2, NT], F32)
        x2 = sb("x2", [P, NC, D], F32)
        z = sb("z", [P, NC, D], F32)
        zT = sb("zT", [P, DC, N], F32)
        stats = sb("stats", [P, 5, NC, 6], F32)
        moments = sb("moments", [P, 5, NC, 2], F32)
        var_eps = sb("var_eps", [P, 5, NC], F32)
        rstd = sb("rstd", [P, 5, NC], F32)
        shared = cursor[0]

        eaT = sb("eaT", [P, E], F32R)
        eaT_end = cursor[0]
        w2_hi = sb("w2_hi", [P, DC, D], F32R)
        w2_lo = sb("w2_lo", [P, DC, D], F32R)
        w1c_hi = sb("w1c_hi", [P, D], F32R)
        w1c_lo = sb("w1c_lo", [EA, D], F32R)
        xs_at = cursor[0]
        xs_hi = sb("xs_hi", [P, NC, D], F32R)
        xs_lo = sb("xs_lo", [P, NC, D], F32R)
        xd_at = cursor[0]
        xd_hi = sb("xd_hi", [P, NC, D], F32R)
        xd_lo = sb("xd_lo", [P, NC, D], F32R)
        ohT = sb("ohT", [P, 2, 2, NC, SE], F32R)
        idx_rows = sb("idx_rows", [P, 2, 2, SE], I32)
        ohd_at = cursor[0]
        ohd = sb("ohd", [P, 2, TPS, N], F32R)
        b2_rows = sb("b2_rows", [P, D], F32)
        over = cursor[0]
        h_hi = sb("h_hi", [P, 2, DC, SE], F32R)
        h_lo = sb("h_lo", [P, 2, DC, SE], F32R)
        m_hi = sb("m_hi", [P, 2, 2, D], F32R)
        m_lo = sb("m_lo", [P, 2, 2, D], F32R)
        t1 = sb("t1", [P, 2, 2, SE], F32)
        t2 = sb("t2", [P, 2, 2, D], F32)
        pre2 = sb("pre2", [P, 2, 2, D], F32)
        edge_end = cursor[0]

        cursor[0] = over
        xin = sb("xin", [P, NC, D], F32)
        xn = sb("xn", [P, NC, D], F32)
        xn_hi = sb("xn_hi", [P, NC, D], F32R)
        xn_lo = sb("xn_lo", [P, NC, D], F32R)
        w0_sb = sb("w0_sb", [P, DC, D], F32)
        w1_sb = sb("w1_sb", [P, 2, DC, D], F32)
        b0_rows = sb("b0_rows", [P, D], F32)
        b1_rows = sb("b1_rows", [P, D], F32)
        idx_i = sb("idx_i", [NT, 2, P], I32)
        idx_f = sb("idx_f", [NT, 2, P], F32)
        adj = sb("adj", [P, NC, N], F32R)
        counts = sb("counts", [P, NC, N], F32)
        eye = sb("eye", [P, NC, N], F32)
        deg = sb("deg", [P, NC], F32)
        dinv = sb("dinv", [P, NC], F32)
        aggT0 = sb("aggT0", [P, DC, N], F32)
        x1 = sb("x1", [P, NC, D], F32)
        y1 = sb("y1", [P, NC, D], F32)
        bits = sb("bits", [P, 16, NC], F32)
        ibits = sb("ibits", [P, 8, NC], I32)
        hot = sb("hot", [P, NC, P], F32)
        ramp_i = sb("ramp_i", [P, 48], I32)
        ramp = sb("ramp", [P, NC, 3, 16], F32)
        ranked = sb("ranked", [P, NC, 3, 16], F32)
        code = sb("code", [P, NC, 3], F32)
        digit = sb("digit", [P, 16], F32)
        adds = sb("adds", [P, NC, 2, 16], F32)
        prologue_end = cursor[0]
        oh_s = sb("oh_s", [P, 2, CT, N], BF16)
        oh_d = sb("oh_d", [P, 2, CT, N], BF16)
        w1c_raw = sb("w1c_raw", [P, D], F32)
        assert max(cursor[0], edge_end) <= nc.sbuf_usable_end, (cursor[0], edge_end)
        ea_hl = nc.alloc_sbuf_tensor_at("ea_hl", [P, 16, 2, EA], F32R, offset=ohd_at)
        ea_raw = nc.alloc_sbuf_tensor_at("ea_raw", [P, 16, EA], F32, offset=xs_at)
        w2_raw = nc.alloc_sbuf_tensor_at("w2_raw", [P, DC, D], F32, offset=xd_at)

        cursor[0] = shared
        w3_sb = sb("w3_sb", [P, 2 * DC, D], F32)
        w4_sb = sb("w4_sb", [P, DC, D], F32)
        b4_rows = sb("b4_rows", [P, D], F32)
        b3_nat = sb("b3_nat", [DC, P], F32)
        assert cursor[0] <= eaT_end
        cursor[0] = eaT_end
        b3_cols = sb("b3_cols", [P, DC], F32)
        gamma1_rows = sb("gamma1_rows", [P, D], F32)
        beta1_rows = sb("beta1_rows", [P, D], F32)
        gamma2_rows = sb("gamma2_rows", [P, D], F32)
        beta2_rows = sb("beta2_rows", [P, D], F32)
        agg = sb("agg", [P, NC, D], F32)
        aggT = sb("aggT", [P, DC, N], F32)
        tokT_at = cursor[0]
        pre_u = sb("pre_u", [P, DC, N], F32)
        uT = sb("uT", [P, DC, N], F32)
        fin_at = cursor[0]
        y4 = sb("y4", [P, NC, D], F32)
        x3 = sb("x3", [P, NC, D], F32)
        tok = sb("tok", [P, NC, D], F32)
        tokT_hi = sb("tokT_hi", [P, DC, N], F32R)
        tokT_lo = sb("tokT_lo", [P, DC, N], F32R)
        wg_sb = sb("wg_sb", [P, DC, EX], F32)
        bg_rows = sb("bg_rows", [P, EX], F32)
        logits = sb("logits", [P, NC, EX], F32)
        probs = sb("probs", [P, NC, EX], F32)
        top = sb("top", [P, NC, 8], F32)
        top_at = sb("top_at", [P, NC, 8], U32)
        top_atf = sb("top_atf", [P, NC, 8], F32)
        chosen = sb("chosen", [P, NC, EX], F32)
        gates = sb("gates", [P, NC, EX], F32)
        gatesT = sb("gatesT", [EX, N], F32)
        small = sb("small", [P, 4, NC], F32)
        ones_2 = sb("ones_2", [2, P], F32R)
        signs = sb("signs", [2, 2], F32)
        fb1_hl = sb("fb1_hl", [2, EX * EH], F32R)
        fb2_sb = sb("fb2_sb", [EX, D], F32)
        fb1_raw_at = cursor[0]
        g_sb = sb("g_sb", [P, NC, HC], F32)
        gT_hi = sb("gT_hi", [P, HC // P, N], F32R)
        gT_lo = sb("gT_lo", [P, HC // P, N], F32R)
        y5 = sb("y5", [P, NC, D], F32)
        fw1_hi = sb("fw1_hi", [P, 2, XS, DC, EH], F32R)
        fw1_lo = sb("fw1_lo", [P, 2, XS, DC, EH], F32R)
        fw1_raw = sb("fw1_raw", [P, 2, XS, DC, EH], F32)
        fw2_raw = sb("fw2_raw", [P, 2, HC // P, D], F32)
        assert cursor[0] <= nc.sbuf_usable_end, cursor[0]
        cursor[0] = shared
        fw2_hi = sb("fw2_hi", [P, 2, HC // P, D], F32R)
        fw2_lo = sb("fw2_lo", [P, 2, HC // P, D], F32R)
        assert cursor[0] <= eaT_end
        fb1_raw = nc.alloc_sbuf_tensor_at("fb1_raw", [2, EX * EH], F32, offset=fb1_raw_at)
        tokT = nc.alloc_sbuf_tensor_at("tokT", [P, DC, N], F32, offset=tokT_at)
        fin = nc.alloc_sbuf_tensor_at("fin", [P, NC, D], F32, offset=fin_at)

        pa, pb, pc, pg = (ctx.enter_context(nc.psum_tensor(n, [P, 2, 512], F32)) for n in ("pa", "pb", "pc", "pg"))
        l1_ps = (pa, pb)

        ld_idx, ld_x, ld_ea, ld_w0, ld_b0, ld_w1, ld_b1, ld_rows, ld_w2, ld_w1c, ld_b2 = map(sem, (
            "ld_idx", "ld_x", "ld_ea", "ld_w0", "ld_b0", "ld_w1", "ld_b1", "ld_rows0", "ld_w2", "ld_w1c", "ld_b2"))
        ld_rows = (ld_rows, sem("ld_rows1"))
        ld_w3, ld_w4, ld_b3, ld_b4, ld_affine, ld_wg, ld_bias_ffn, ld_fw1, ld_fw2 = map(sem, (
            "ld_w3", "ld_w4", "ld_b3", "ld_b4", "ld_affine", "ld_wg", "ld_bias_ffn", "ld_fw1", "ld_fw2"))
        ld_fw1, ld_fw2 = (ld_fw1, sem("ld_fw1_odd")), (ld_fw2, sem("ld_fw2_odd"))
        fw1_hi_ready, fw1_lo_ready, fw2_hi_ready, fw2_lo_ready, fb1_ready, gT_hi_ready = map(sem, (
            "fw1_hi_ready", "fw1_lo_ready", "fw2_hi_ready", "fw2_lo_ready", "fb1_ready", "gT_hi_ready"))
        consts, idx_f_ready, idxT_ps, idx_cols_ready, dve_link, onehots, counted = map(sem, (
            "consts", "idx_f_ready", "idxT_ps", "idx_cols_ready", "dve_link", "onehots", "counted"))
        pool_link, act_link = map(sem, ("pool_link", "act_link"))
        counts_ready, countsT_ps, adj_ready, deg_ready, dinv_ready, var_ready, rstd_ready = map(sem, (
            "counts_ready", "countsT_ps", "adj_ready", "deg_ready", "dinv_ready", "var_ready", "rstd_ready"))
        xn_split, agg0_ps, agg0_ready, conv_ps, z_ready, zT_ps, zT_ready, xw_ps = map(sem, (
            "xn_split", "agg0_ps", "agg0_ready", "conv_ps", "z_ready", "zT_ps", "zT_ready", "xw_ps"))
        ea_hi_ready, ea_lo_ready, eaT_ps, eaT_ready, w_hi_ready, w_lo_ready, xw_hi, xw_lo, xd_sum = map(sem, (
            "ea_hi_ready", "ea_lo_ready", "eaT_ps", "eaT_ready", "w_hi_ready", "w_lo_ready", "xw_hi", "xw_lo", "xd_sum"))
        ohT_ready, ohd_ready, agg_done = map(sem, ("ohT_ready", "ohd_ready", "agg_done"))
        l1 = {k: sem("l1_" + k) for k in ("psum", "exp", "cap", "n", "ln", "r", "w", "y", "hi", "lo")}
        l2 = {k: sem("l2_" + k) for k in ("psum", "pre", "exp", "cap", "n", "ln", "r", "w", "y", "hi", "lo")}
        agg_ready, aggT_ps, aggT_ready, b3T_ps, b3_ready, u_ps, u_exp, u_cap, u_n, u_r, u_ready = map(sem, (
            "agg_ready", "aggT_ps", "aggT_ready", "b3T_ps", "b3_ready", "u_ps", "u_exp", "u_cap", "u_n", "u_r", "u_ready"))
        u_pre, out4_ps, tok_ready, tokT_ps, tokT_ready, logits_ps, neg_max, exp_sum, gates_ready, gatesT_ps, gatesT_ready = map(sem, (
            "u_pre", "out4_ps", "tok_ready", "tokT_ps", "tokT_ready", "logits_ps", "neg_max", "exp_sum", "gates_ready", "gatesT_ps", "gatesT_ready"))
        f1_ps, f1_g, gT_ps, gT_ready, f2_ps, f2_done, fin_ready, stored = map(sem, (
            "f1_ps", "f1_g", "gT_ps", "gT_ready", "f2_ps", "f2_done", "fin_ready", "stored"))

        by_node = lambda a: a.rearrange("(c p) d -> p c d", p=P)
        rows = lambda a, n: a.unsqueeze(0).broadcast_to((P, n))

        block = ctx.enter_context(nc.Block())

        @block.sync
        def _(sp):
            for k, idx in enumerate((src, dst)):
                sp.dma_start(idx_i[:, k, :], idx.rearrange("(t p) -> t p", p=P)).then_inc(ld_idx, 16)
            sp.dma_start(xin[:, :, :], by_node(x)).then_inc(ld_x, 16)
            ea_tiles = edge_attr.rearrange("(t p) a -> p t a", p=P)
            for c in range(NT // 16):
                if c:
                    sp.wait_ge(ea_lo_ready, c)
                sp.dma_start(ea_raw[:, :, :], ea_tiles[:, 16 * c:16 * c + 16, :]).then_inc(ld_ea, 16)
                if c == 0:
                    sp.dma_start(w0_sb[:, :, :], w0.rearrange("(k p) n -> p k n", p=P)).then_inc(ld_w0, 16)
                    sp.dma_start(b0_rows[:, :], rows(b0, D)).then_inc(ld_b0, 16)
                    sp.dma_start(w1_sb[:, :, :, :], w1[0:2 * D, :].rearrange("(g k p) n -> p g k n", g=2, p=P)).then_inc(ld_w1, 16)
                    sp.dma_start(b1_rows[:, :], rows(b1, D)).then_inc(ld_b1, 16)
                    for half in range(2):
                        sp.dma_start(w1c_raw[half * EA:half * EA + EA, :], w1[2 * D:2 * D + EA, :]).then_inc(ld_w1c, 16)
                    sp.dma_start(w2_raw[:, :, :], w2.rearrange("(k p) n -> p k n", p=P)).then_inc(ld_w2, 16)
                    sp.dma_start(b2_rows[:, :], rows(b2, D)).then_inc(ld_b2, 16)

            def load_idx_rows(s, parity):
                for k, idx in enumerate((src, dst)):
                    sp.dma_start(idx_rows[:, parity, k, :], rows(idx[bass.ts(s, SE)], SE)).then_inc(ld_rows[parity], 16)

            load_idx_rows(0, 0)
            load_idx_rows(1, 1)
            with sp.Fori(1, NS // 2) as i:
                for parity in range(2):
                    sp.wait_ge(ohT_ready, 2 * i + parity - 1)
                    load_idx_rows(2 * i + parity, parity)

            sp.wait_ge(l1["psum"], 2 * NS)
            sp.dma_start(b3_nat[:, :], b3.rearrange("(c p) -> c p", p=P)).then_inc(ld_b3, 16)
            sp.dma_start(w3_sb[:, :, :], w3.rearrange("(k p) n -> p k n", p=P)).then_inc(ld_w3, 16)
            sp.dma_start(w4_sb[:, :, :], w4.rearrange("(k p) n -> p k n", p=P)).then_inc(ld_w4, 16)
            sp.dma_start(b4_rows[:, :], rows(b4, D)).then_inc(ld_b4, 16)
            sp.wait_ge(agg_done, NS)
            for t, a in ((gamma1_rows, gamma1), (beta1_rows, beta1), (gamma2_rows, gamma2), (beta2_rows, beta2)):
                sp.dma_start(t[:, :], rows(a, D)).then_inc(ld_affine, 16)
            sp.dma_start(wg_sb[:, :, :], wg.rearrange("(p k) e -> p k e", k=DC)).then_inc(ld_wg, 16)
            sp.dma_start(bg_rows[:, :], rows(bg, EX)).then_inc(ld_wg, 16)
            sp.dma_start(fb1_raw[:, :], fb1.rearrange("e h -> (e h)").unsqueeze(0).broadcast_to((2, EX * EH))).then_inc(ld_bias_ffn, 16)
            sp.dma_start(fb2_sb[:, :], fb2).then_inc(ld_bias_ffn, 16)
            fw1_steps = fw1.rearrange("e (p k) h -> p e k h", k=DC)
            fw2_steps = fw2.rearrange("e h d -> (e h) d").rearrange("(f j p) d -> p f j d", j=HC // P, p=P)

            def load_fw(f, parity):
                sp.dma_start(fw1_raw[:, parity], fw1_steps[:, bass.ts(f, XS)]).then_inc(ld_fw1[parity], 16)

            def load_fw2(f, parity):
                sp.dma_start(fw2_raw[:, parity], fw2_steps[:, bass.ds(f, 1)].rearrange("p f j d -> p (f j) d")).then_inc(ld_fw2[parity], 16)

            for f in range(2):
                load_fw(f, f)
                load_fw2(f, f)
            with sp.Fori(1, FS // 2) as i:
                for parity in range(2):
                    sp.wait_ge(fw1_lo_ready, 2 * i + parity - 1)
                    load_fw(2 * i + parity, parity)
                    sp.wait_ge(fw2_lo_ready, 2 * i + parity - 1)
                    load_fw2(2 * i + parity, parity)
            for c in range(NC):
                sp.wait_ge(fin_ready, c + 1)
                sp.dma_start(by_node(out)[:, c, :], fin[:, c, :]).then_inc(stored, 16)
            sp.wait_ge(stored, 16 * NC)

        @block.gpsimd
        def _(pool):
            linked = [0]

            def link(ins):
                linked[0] += 1
                ins.then_inc(pool_link, 1)
                pool.wait_ge(pool_link, linked[0])

            link(pool.memset(zeros_pp[:, :], 0.0))
            pool.affine_select(out=ident[:, :], in_=zeros_pp[:, :], compare_op=ALU.not_equal, fill=1.0,
                               base=0, pattern=[[-1, P]], channel_multiplier=1).then_inc(consts, 1)
            pool.iota(iota_i[:, :], pattern=[[1, N]], base=0, channel_multiplier=0).then_inc(consts, 1)
            pool.iota(node_i[:, :], pattern=[[P, NC]], base=0, channel_multiplier=1).then_inc(consts, 1)
            pool.iota(ramp_i[:, :], pattern=[[0, 3], [-1, 16]], base=16, channel_multiplier=0).then_inc(consts, 1)
            pool.memset(minus_half[:, :], -0.5).then_inc(consts, 1)
            link(pool.memset(eye[:, :, :], 0.0))
            for c in range(NC):
                pool.affine_select(out=eye[:, c, :], in_=eye[:, c, :], compare_op=ALU.not_equal, fill=1.0,
                                   base=c * P, pattern=[[-1, N]], channel_multiplier=1).then_inc(consts, 1)

            def inverse_root(which, ready, ready_at, result, done):
                pool.wait_ge(ready, ready_at)
                pool.tensor_tensor(result, which, minus_half[:, :], ALU.pow).then_inc(done, 1)

            inverse_root(var_eps[:, 0, :], var_ready, 1, rstd[:, 0, :], rstd_ready)

            def ea_low(c):
                pool.wait_ge(ea_hi_ready, c + 1)
                pool.tensor_tensor(ea_hl[:, :, 1, :], ea_raw[:, :, :], ea_hl[:, :, 0, :].bitcast(F32),
                                   ALU.subtract).then_inc(ea_lo_ready, 1)

            ea_low(0)
            ea_low(1)
            ea_low(2)
            ea_low(3)
            inverse_root(deg[:, :], deg_ready, 1, dinv[:, :], dinv_ready)
            pool.wait_ge(w_hi_ready, 1)
            pool.tensor_tensor(w1c_lo[:, :], w1c_raw[0:EA, :], w1c_hi[0:EA, :].bitcast(F32), ALU.subtract).then_inc(w_lo_ready, 1)
            pool.wait_ge(w_hi_ready, 2)
            inverse_root(var_eps[:, 1, :], var_ready, 2, rstd[:, 1, :], rstd_ready)
            inverse_root(var_eps[:, 2, :], var_ready, 3, rstd[:, 2, :], rstd_ready)
            pool.tensor_tensor(w2_lo[:, :, :], w2_raw[:, :, :], w2_hi[:, :, :].bitcast(F32), ALU.subtract).then_inc(w_lo_ready, 1)

            def low(layer, t, hi, lo, u, half):
                pool.wait_ge(layer["hi"], u + 1)
                pool.tensor_tensor(lo, t[:, half], hi.bitcast(F32), ALU.subtract).then_inc(layer["lo"], 1)

            def low1(s, parity, half):
                low(l1, t1, h_hi[:, parity, 2 * half:2 * half + 2, :], h_lo[:, parity, 2 * half:2 * half + 2, :], 2 * s + half, half)

            def sum2(s, half):
                pool.wait_ge(l2["w"], 2 * s + half + 1)
                pool.tensor_tensor(t2[:, half], t2[:, half], pre2[:, half], ALU.add).then_inc(l2["y"], 1)

            def low2(s, half):
                low(l2, t2, m_hi[:, half], m_lo[:, half], 2 * s + half, half)

            def step(s, parity, at=None):
                if at != "first":
                    sum2(s - 1, 1)
                    low2(s - 1, 1)
                if at != "last":
                    low1(s + 1, 1 - parity, 0)
                    low1(s + 1, 1 - parity, 1)
                sum2(s, 0)
                low2(s, 0)

            low1(0, 0, 0)
            low1(0, 0, 1)
            step(0, 0, "first")
            step(1, 1, "second")
            with pool.Fori(0, (NS - 6) // 2) as i:
                step(2 * i + 2, 0)
                step(2 * i + 3, 1)
            step(NS - 4, 0)
            step(NS - 3, 1)
            step(NS - 2, 0, "no layer 1 after")
            step(NS - 1, 1, "last")
            sum2(NS - 1, 1)
            low2(NS - 1, 1)

            inverse_root(var_eps[:, 3, :], var_ready, 4, rstd[:, 3, :], rstd_ready)
            inverse_root(var_eps[:, 4, :], var_ready, 5, rstd[:, 4, :], rstd_ready)
            pool.wait_ge(var_ready, 6)
            pool.tensor_tensor(rstd[:, 0, :], var_eps[:, 0, :], minus_half[:, :], ALU.pow).then_inc(rstd_ready, 1)

        @block.scalar
        def _(act):
            act.preload_act_table_set("natural_log_exp_and_others")

            def ea_high(c):
                act.wait_ge(ld_ea, 16 * (c + 1))
                if c:
                    act.wait_ge(eaT_ps, 4 * c)
                act.activation(ea_hl[:, :, 0, :], ea_raw[:, :, :], ACT.Copy).then_inc(ea_hi_ready, 1)

            def ea_out(c):
                for g in range(4):
                    n = 4 * c + g
                    act.wait_ge(eaT_ps, n + 1)
                    act.activation(eaT[:, bass.ts(n, 4 * P)], pb[:, n % 2, :], ACT.Copy).then_inc(eaT_ready, 1)

            ea_high(0)
            ea_out(0)
            ea_high(1)
            ea_out(1)
            act.wait_ge(ld_w1c, 32)
            act.activation(w1c_hi[:, :], w1c_raw[:, :], ACT.Copy).then_inc(w_hi_ready, 1)
            act.wait_ge(ld_w2, 16)
            act.activation(w2_hi[:, :, :], w2_raw[:, :, :], ACT.Copy).then_inc(w_hi_ready, 1)
            ea_high(2)
            ea_out(2)
            ea_high(3)
            ea_out(3)
            act.wait_ge(zT_ps, 1)
            act.activation(zT[:, :, :], pc.rearrange("p b (k n) -> p (b k) n", n=N), ACT.Copy).then_inc(zT_ready, 1)
            act.wait_ge(xw_ps, 1)
            act.activation(xs_hi[:, :, :], pa[:, :, :], ACT.Copy).then_inc(xw_hi, 1)
            act.wait_ge(xd_sum, 1)
            act.wait_ge(w_lo_ready, 2)
            act.activation(xd_hi[:, :, :], x1[:, :, :], ACT.Copy).then_inc(xw_hi, 1)

            def exp(layer, t, source, u, half, ready):
                act.wait_ge(ready, u + 1)
                act.activation(t[:, half], source, ACT.Exp).then_inc(layer["exp"], 1)

            def exp1(s, half, first=False):
                if not first:
                    act.wait_ge(l1["lo"], 2 * s + half - 1)
                exp(l1, t1, l1_ps[half][:, :, :], 2 * s + half, half, l1["psum"])

            def exp2(s, half, first=False):
                if not first:
                    act.wait_ge(l2["lo"], 2 * s + half - 1)
                exp(l2, t2, pre2[:, half], 2 * s + half, half, l2["pre"])

            def quotient(layer, t, u, half):
                act.wait_ge(layer["n"], u + 1)
                act.activation(t[:, half], t[:, half], ACT.Ln, bias=2.0).then_inc(layer["ln"], 1)
                act.wait_ge(layer["ln"], u + 1)
                act.activation(t[:, half], t[:, half], ACT.Exp, scale=-1.0).then_inc(layer["r"], 1)

            def high1(s, parity, half, first=False):
                act.wait_ge(l1["y"], 2 * s + half + 1)
                if not first:
                    act.wait_ge(l2["psum"], 2 * s - 2)
                act.activation(h_hi[:, parity, 2 * half:2 * half + 2, :], t1[:, half], ACT.Copy).then_inc(l1["hi"], 1)

            def high2(s, half, first=False):
                act.wait_ge(l2["y"], 2 * s + half + 1)
                if not first:
                    act.wait_ge(agg_done, s)
                act.activation(m_hi[:, half], t2[:, half], ACT.Copy).then_inc(l2["hi"], 1)

            def step(s, parity, at=None):
                first = at == "first"
                if at != "last":
                    exp1(s + 1, 1)
                    quotient(l1, t1, 2 * s + 2, 0)
                if not first:
                    high2(s - 1, 1, at == "second")
                if at != "last":
                    quotient(l1, t1, 2 * s + 3, 1)
                exp2(s, 0, first)
                if at != "last":
                    high1(s + 1, 1 - parity, 0, first)
                    high1(s + 1, 1 - parity, 1, first)
                quotient(l2, t2, 2 * s, 0)
                exp2(s, 1, first)
                high2(s, 0, first)
                if at not in ("no layer 1 after", "last"):
                    exp1(s + 2, 0)
                quotient(l2, t2, 2 * s + 1, 1)

            exp1(0, 0, True)
            quotient(l1, t1, 0, 0)
            exp1(0, 1, True)
            high1(0, 0, 0, True)
            quotient(l1, t1, 1, 1)
            high1(0, 0, 1, True)
            exp1(1, 0)
            step(0, 0, "first")
            step(1, 1, "second")
            with act.Fori(0, (NS - 6) // 2) as i:
                step(2 * i + 2, 0)
                step(2 * i + 3, 1)
            step(NS - 4, 0)
            step(NS - 3, 1)
            step(NS - 2, 0, "no layer 1 after")
            step(NS - 1, 1, "last")
            high2(NS - 1, 1)

            act.wait_ge(agg_done, NS)
            act.activation(agg[:, :, :], pg[:, :, :], ACT.Copy).then_inc(agg_ready, 1)
            act.wait_ge(aggT_ps, 1)
            act.activation(aggT[:, :, :], pc.rearrange("p b (k n) -> p (b k) n", n=N), ACT.Copy).then_inc(aggT_ready, 1)
            def fw1_high(f, parity, first=False):
                act.wait_ge(ld_fw1[parity], 8 * (f - parity) + 16)
                if not first:
                    act.wait_ge(f1_ps, f - 1)
                act.activation(fw1_hi[:, parity], fw1_raw[:, parity], ACT.Copy).then_inc(fw1_hi_ready, 1)

            def fw2_high(f, parity, first=False):
                act.wait_ge(ld_fw2[parity], 8 * (f - parity) + 16)
                if first:
                    act.wait_ge(out4_ps, NC)
                else:
                    act.wait_ge(f2_ps, f - 1)
                act.activation(fw2_hi[:, parity], fw2_raw[:, parity], ACT.Copy).then_inc(fw2_hi_ready, 1)

            fw1_high(0, 0, True)
            act.wait_ge(u_pre, 1)
            act.activation(uT[:, :, :], pre_u[:, :, :], ACT.Exp).then_inc(u_exp, 1)
            act.wait_ge(u_n, 1)
            act.activation(uT[:, :, :], uT[:, :, :], ACT.Ln, bias=2.0).then_inc(act_link, 1)
            act.wait_ge(act_link, 1)
            act.activation(uT[:, :, :], uT[:, :, :], ACT.Exp, scale=-1.0).then_inc(u_r, 1)
            fw1_high(1, 1, True)
            fw2_high(0, 0, True)
            act.wait_ge(tokT_ps, 1)
            act.activation(tokT_hi[:, :, :], pc.rearrange("p b (k n) -> p (b k) n", n=N), ACT.Copy).then_inc(tokT_ready, 1)
            act.activation(tokT[:, :, :], pc.rearrange("p b (k n) -> p (b k) n", n=N), ACT.Copy).then_inc(tokT_ready, 1)
            for c in range(NC):
                act.wait_ge(neg_max, 1)
                act.activation(probs[:, c, :], logits[:, c, :], ACT.Exp, bias=small[:, 0, c:c + 1],
                               accum_out=small[:, 1, c:c + 1]).then_inc(exp_sum, 1)
            fw1_high(2, 0)
            act.wait_ge(gatesT_ps, 1)
            act.activation(gatesT[:, :], pc[0:EX, 0, 0:N], ACT.Copy).then_inc(gatesT_ready, 1)
            def gated_high(f, first=False):
                act.wait_ge(gT_ps, f + 1)
                if not first:
                    act.wait_ge(f2_ps, f)
                act.activation(gT_hi[:, :, :], pc.rearrange("p b (k n) -> p (b k) n", n=N), ACT.Copy).then_inc(gT_hi_ready, 1)

            def step(f, parity, fw1_more=True, fw2_more=True, first=False):
                gated_high(f, first)
                if fw1_more:
                    fw1_high(f + 3, 1 - parity)
                if fw2_more:
                    fw2_high(f + 1, 1 - parity, first)

            step(0, 0, first=True)
            with act.Fori(0, (FS - 4) // 2) as i:
                step(2 * i + 1, 1)
                step(2 * i + 2, 0)
            step(FS - 3, 1, fw1_more=False)
            step(FS - 2, 0, fw1_more=False)
            step(FS - 1, 1, fw1_more=False, fw2_more=False)

        @block.tensor
        def _(pe):
            def transposed(dest, source, rows_in):
                return pe.transpose(dest, source, ident[0:rows_in, 0:rows_in])

            pe.wait_ge(consts, 1)
            pe.wait_ge(idx_f_ready, 1)
            for k in range(2):
                last = transposed(pc[:, 0, k * NT:(k + 1) * NT], idx_f[:, k, :], NT)
            last.then_inc(idxT_ps, 1)

            def ea_transposes(c):
                pe.wait_ge(ea_lo_ready, c + 1)
                for g in range(4):
                    n = 4 * c + g
                    if n >= 2:
                        pe.wait_ge(eaT_ready, n - 1)
                    for j in range(4):
                        last = transposed(pb[:, n % 2, j * P:(j + 1) * P],
                                          ea_hl[:, 4 * g + j, :, :].rearrange("p h a -> p (h a)").bitcast(F32), P)
                    last.then_inc(eaT_ps, 1)

            def count(c, parity, start, stop):
                pe.wait_ge(onehots, c + 1)
                for t in range(CT):
                    for k in range(NC):
                        last = pe.matmul(pa[:, k, 0:N], oh_s[:, parity, t, k * P:(k + 1) * P], oh_d[:, parity, t, :],
                                         start=start and t == 0, stop=stop and t == CT - 1)
                last.then_inc(counted, 1)

            NCH = NT // CT
            for c in range(NCH):
                count(c, c % 2, c == 0, c == NCH - 1)
                if c % 2 == 1:
                    ea_transposes(c // 2)

            pe.wait_ge(counts_ready, 1)
            for k in range(NC):
                for j in range(NC):
                    last = transposed(pc[:, 1, k * N + j * P:k * N + (j + 1) * P], counts[:, j, k * P:(k + 1) * P], P)
            last.then_inc(countsT_ps, 1)

            pe.wait_ge(adj_ready, 1)
            pe.wait_ge(xn_split, 2)
            ps = pg.rearrange("p b (k n) -> p (b k) n", n=N)
            for c in range(DC):
                for n, (part, k) in enumerate(((part, k) for part in (xn_hi, xn_lo) for k in range(NC))):
                    last = pe.matmul(ps[:, c, :], part[:, k, c * P:(c + 1) * P], adj[:, k, :],
                                     start=n == 0, stop=n == 3)
            last.then_inc(agg0_ps, 1)
            pe.wait_ge(agg0_ready, 1)
            pe.wait_ge(ld_w0, 16)
            for n in range(NC):
                for k in range(DC):
                    last = pe.matmul(pa[:, n, :], aggT0[:, k, n * P:(n + 1) * P], w0_sb[:, k, :],
                                     start=k == 0, stop=k == DC - 1)
            last.then_inc(conv_ps, 1)

            def transposes(dest, source, ready, at, done, strided=False):
                pe.wait_ge(ready, at)
                view = dest.rearrange("p b (k n) -> p (b k) n", n=N)
                for n in range(NC):
                    for k in range(DC):
                        part = source[:, n, k::DC] if strided else source[:, n, k * P:(k + 1) * P]
                        last = transposed(view[:, k, n * P:(n + 1) * P], part, P)
                last.then_inc(done, 1)

            transposes(pc, z, z_ready, 1, zT_ps)
            pe.wait_ge(zT_ready, 1)
            pe.wait_ge(ld_w1, 16)
            for g, dest in enumerate((pa, pg)):
                for n in range(NC):
                    for k in range(DC):
                        last = pe.matmul(dest[:, n, :], zT[:, k, n * P:(n + 1) * P], w1_sb[:, g, k, :],
                                         start=k == 0, stop=k == DC - 1)
                last.then_inc(xw_ps, 1)

            def layer1(s, parity, half, first=False):
                if half == 0:
                    pe.wait_ge(ohT_ready, s + 1)
                if not first:
                    pe.wait_ge(l1["y"], 2 * s + half - 1)
                ea = eaT[:, bass.ts(s, SE)]
                ea_high = eaT[0:EA, bass.ts(s, SE)]
                for j in range(2):
                    c = 2 * half + j
                    cols = slice(c * P, (c + 1) * P)
                    dest = l1_ps[half][:, j, :]
                    for n, (part, which, k) in enumerate((part, which, k) for which, parts in enumerate(((xs_hi, xs_lo), (xd_hi, xd_lo)))
                                                         for k in range(NC) for part in parts):
                        pe.matmul(dest, part[:, k, cols], ohT[:, parity, which, k, :], start=n == 0, stop=False)
                    pe.matmul(dest, w1c_hi[:, cols], ea, start=False, stop=False)
                    last = pe.matmul(dest, w1c_lo[:, cols], ea_high, start=False, stop=True)
                last.then_inc(l1["psum"], 1)

            def layer2(s, parity, half, first=False):
                pe.wait_ge(l1["lo"], 2 * s + 2)
                if not first:
                    pe.wait_ge(l2["pre"], 2 * s + half)
                for j in range(2):
                    at = slice((2 * half + j) * P, (2 * half + j + 1) * P)
                    n = 0
                    for k in range(DC):
                        for a, b in ((h_hi, w2_hi), (h_hi, w2_lo), (h_lo, w2_hi)):
                            last = pe.matmul(pc[:, j, :], a[:, parity, k, at], b[:, k, :], start=n == 0, stop=n == 3 * DC - 1)
                            n += 1
                last.then_inc(l2["psum"], 1)

            def sum_messages(s, parity, first=False, final=False):
                pe.wait_ge(ohd_ready, s + 1)
                for half in range(2):
                    pe.wait_ge(l2["lo"], 2 * s + half + 1)
                    for j in range(2):
                        for n in range(NC):
                            for part in (m_hi, m_lo):
                                last = pe.matmul(pg[:, n, :], ohd[:, parity, 2 * half + j, n * P:(n + 1) * P], part[:, half, j, :],
                                                 start=first and half == 0 and j == 0 and part is m_hi,
                                                 stop=final and half == 1 and j == 1 and part is m_lo)
                last.then_inc(agg_done, 1)

            def step(s, parity, more, first=False, second=False):
                layer2(s, parity, 0, first)
                if not first:
                    sum_messages(s - 1, 1 - parity, first=second)
                layer2(s, parity, 1)
                if more == "yes":
                    layer1(s + 2, parity, 0)
                    layer1(s + 2, parity, 1)

            pe.wait_ge(xw_lo, 2)
            pe.wait_ge(w_lo_ready, 2)
            pe.wait_ge(eaT_ready, NT // 4)
            layer1(0, 0, 0, True)
            layer1(0, 0, 1, True)
            layer1(1, 1, 0)
            layer1(1, 1, 1)
            step(0, 0, "yes", first=True)
            step(1, 1, "yes", second=True)
            with pe.Fori(0, (NS - 6) // 2) as i:
                step(2 * i + 2, 0, "yes")
                step(2 * i + 3, 1, "yes")
            step(NS - 4, 0, "yes")
            step(NS - 3, 1, "yes")
            step(NS - 2, 0, "no")
            step(NS - 1, 1, "last")

            pe.wait_ge(ld_b3, 16)
            pe.wait_ge(l1["y"], 2 * NS)
            pe.wait_ge(l2["pre"], 2 * NS)
            transposed(pc[:, 0, 0:DC], b3_nat[:, :], DC).then_inc(b3T_ps, 1)
            pe.wait_ge(ld_w3, 16)
            u_bank = [l1_ps[c // 2][:, c % 2, 0:N] for c in range(DC)]
            for c in range(DC):
                for k in range(DC):
                    pe.matmul(u_bank[c], w3_sb[:, k, c * P:(c + 1) * P], zT[:, k, :], start=k == 0, stop=False)
            sum_messages(NS - 1, 1, final=True)
            pe.wait_ge(b3_ready, 1)
            transposes(pc, agg, agg_ready, 1, aggT_ps)
            pe.wait_ge(aggT_ready, 1)
            for c in range(DC):
                for k in range(DC):
                    last = pe.matmul(u_bank[c], w3_sb[:, DC + k, c * P:(c + 1) * P], aggT[:, k, :], start=False, stop=k == DC - 1)
                last.then_inc(u_ps, 1)
            pe.wait_ge(u_ready, 1)
            pe.wait_ge(ld_w4, 16)
            for n in range(NC):
                for k in range(DC):
                    last = pe.matmul(pg[:, n, :], uT[:, k, n * P:(n + 1) * P], w4_sb[:, k, :], start=k == 0, stop=k == DC - 1)
                last.then_inc(out4_ps, 1)

            transposes(pc, tok, tok_ready, 1, tokT_ps, strided=True)
            pe.wait_ge(tokT_ready, 2)
            pe.wait_ge(ld_wg, 32)
            for n in range(NC):
                for k in range(DC):
                    last = pe.matmul(pa[:, n, 0:EX], tokT[:, k, n * P:(n + 1) * P], wg_sb[:, k, :], start=k == 0, stop=k == DC - 1)
            last.then_inc(logits_ps, 1)

            def hidden(f, parity):
                pe.wait_ge(fw1_lo_ready, f + 1)
                dest = (pb, pa)[parity]
                for n in range(NC):
                    at = slice(n * P, (n + 1) * P)
                    pe.matmul(dest[:, n, :], ones_2[:, :], fb1_hl[:, bass.ts(f, HC)], start=True, stop=False)
                    for k in range(DC):
                        for a, b in ((tokT_hi, fw1_hi), (tokT_hi, fw1_lo), (tokT_lo, fw1_hi)):
                            last = pe.matmul(dest[:, n, :], a[:, k, at], b[:, parity, :, k, :],
                                             start=False, stop=k == DC - 1 and a is tokT_lo)
                last.then_inc(f1_ps, 1)

            def gated_transposes(f, first=False):
                pe.wait_ge(f1_g, 2 * f + 2)
                if not first:
                    pe.wait_ge(gT_ready, f)
                view = pc.rearrange("p b (k n) -> p (b k) n", n=N)
                for n in range(NC):
                    for k in range(HC // P):
                        last = transposed(view[:, k, n * P:(n + 1) * P], g_sb[:, n, k * P:(k + 1) * P], P)
                last.then_inc(gT_ps, 1)

            def expert_out(f, parity, final=False):
                pe.wait_ge(gT_ready, f + 1)
                pe.wait_ge(fw2_lo_ready, f + 1)
                for n in range(NC):
                    at = slice(n * P, (n + 1) * P)
                    for k in range(HC // P):
                        for a, b in ((gT_hi, fw2_hi), (gT_hi, fw2_lo), (gT_lo, fw2_hi)):
                            last = pe.matmul(pg[:, n, :], a[:, k, at], b[:, parity, k, :],
                                             start=False, stop=final and k == HC // P - 1 and a is gT_lo)
                last.then_inc(f2_ps, 1)

            pe.wait_ge(tokT_ready, 3)
            pe.wait_ge(fb1_ready, 1)
            hidden(0, 0)
            pe.wait_ge(gates_ready, 1)
            for n in range(NC):
                last = transposed(pc[0:EX, 0, n * P:(n + 1) * P], gates[:, n, :], P)
            last.then_inc(gatesT_ps, 1)
            pe.wait_ge(neg_max, 1)
            hidden(1, 1)
            pe.wait_ge(gatesT_ready, 1)
            pe.wait_ge(ld_bias_ffn, 32)
            for n in range(NC):
                pe.matmul(pg[:, n, :], gatesT[:, n * P:(n + 1) * P], fb2_sb[:, :], start=True, stop=False)

            def step(f, parity, more=True, first=False, final=False):
                gated_transposes(f, first)
                if more:
                    hidden(f + 2, parity)
                expert_out(f, parity, final)

            step(0, 0, first=True)
            with pe.Fori(0, (FS - 4) // 2) as i:
                step(2 * i + 1, 1)
                step(2 * i + 2, 0)
            step(FS - 3, 1)
            step(FS - 2, 0, more=False)
            step(FS - 1, 1, more=False, final=True)

        @block.vector
        def _(dve):
            linked = [0]

            def link(ins):
                linked[0] += 1
                ins.then_inc(dve_link, 1)
                dve.wait_ge(dve_link, linked[0])

            def layer_norm_moments(t, which):
                for c in range(NC):
                    last = dve.bn_stats(stats[:, which, c, :], t[:, c, :])
                link(last)
                for c in range(NC):
                    last = dve.bn_aggr(moments[:, which, c, :], stats[:, which, c, :])
                link(last)
                dve.tensor_scalar(var_eps[:, which % 5, :], moments[:, which, :, 1], EPS, None, ALU.add).then_inc(var_ready, 1)

            def normalise(dest, t, which, count):
                dve.wait_ge(rstd_ready, count)
                for c in range(NC):
                    last = dve.tensor_scalar(dest[:, c, :], t[:, c, :], moments[:, which, c, 0:1], rstd[:, which, c:c + 1],
                                             ALU.subtract, ALU.mult)
                return last

            dve.wait_ge(ld_idx, 32)
            dve.tensor_copy(idx_f[:, :, :], idx_i[:, :, :]).then_inc(idx_f_ready, 1)
            dve.wait_ge(consts, 5)
            dve.tensor_copy(iota_row[:, :], iota_i[:, :])
            dve.tensor_copy(iota_bf[:, :], iota_i[:, :])
            dve.tensor_copy(node_id[:, :], node_i[:, :])
            for c in range(NC):
                link(dve.tensor_copy(ramp[:, c, :, :], ramp_i[:, :].rearrange("p (f w) -> p f w", f=3)))
            dve.wait_ge(idxT_ps, 1)
            link(dve.tensor_copy(idx_cols[:, :, :], pc[:, 0, 0:2 * NT].rearrange("p (k t) -> p k t", k=2)))

            def onehots_of(c, parity, first=False):
                if not first:
                    dve.wait_ge(counted, c - 1)
                for t in range(CT):
                    for dest, k in ((oh_s, 0), (oh_d, 1)):
                        at = c * CT + t
                        last = dve.tensor_scalar(dest[:, parity, t, :], iota_bf[:, :], idx_cols[:, k, bass.ds(at, 1)], None, ALU.is_equal)
                last.then_inc(onehots, 1)

            onehots_of(0, 0, True)
            onehots_of(1, 1, True)
            dve.wait_ge(ld_x, 16)
            layer_norm_moments(xin, 0)
            with dve.Fori(1, NT // CT // 2) as i:
                onehots_of(2 * i, 0)
                onehots_of(2 * i + 1, 1)
            link(normalise(xn, xin, 0, 1))

            dve.wait_ge(counted, NT // CT)
            dve.tensor_copy(counts[:, :, :], pa[:, :, 0:N]).then_inc(counts_ready, 1)
            dve.wait_ge(counts_ready, 1)
            dve.wait_ge(countsT_ps, 1)
            link(dve.tensor_tensor(counts[:, :, :], pc[:, 1, :].rearrange("p (k n) -> p k n", n=N), counts[:, :, :], ALU.add))
            dve.wait_ge(consts, 7)
            dve.scalar_tensor_tensor(out=adj[:, :, :], in0=counts[:, :, :], scalar=1.0, in1=eye[:, :, :],
                                     op0=ALU.min, op1=ALU.add).then_inc(adj_ready, 1)
            dve.wait_ge(adj_ready, 1)
            dve.tensor_reduce(deg[:, :], adj[:, :, :].bitcast(F32), AX.X, ALU.add).then_inc(deg_ready, 1)
            dve.wait_ge(dinv_ready, 1)
            for c in range(NC):
                last = dve.tensor_scalar(xn[:, c, :], xn[:, c, :], dinv[:, c:c + 1], None, ALU.mult)
            link(last)
            dve.tensor_copy(xn_hi[:, :, :], xn[:, :, :]).then_inc(xn_split, 1)
            dve.wait_ge(xn_split, 1)
            dve.tensor_tensor(xn_lo[:, :, :], xn[:, :, :], xn_hi[:, :, :].bitcast(F32), ALU.subtract).then_inc(xn_split, 1)
            dve.wait_ge(ld_b0, 16)
            for c in range(NC):
                last = dve.tensor_tensor(x1[:, c, :], xin[:, c, :], b0_rows[:, :], ALU.add)
            link(last)
            dve.wait_ge(agg0_ps, 1)
            dve.tensor_copy(aggT0[:, :, :], pg.rearrange("p b (k n) -> p (b k) n", n=N)).then_inc(agg0_ready, 1)
            dve.wait_ge(conv_ps, 1)
            for c in range(NC):
                last = dve.scalar_tensor_tensor(out=x1[:, c, :], in0=pa[:, c, :], scalar=dinv[:, c:c + 1], in1=x1[:, c, :],
                                                op0=ALU.mult, op1=ALU.add)
            link(last)

            layer_norm_moments(x1, 1)
            link(normalise(y1, x1, 1, 2))
            link(dve.tensor_scalar(hot[:, :, :], y1[:, :, 0:P], HOT, None, ALU.is_gt))
            for c in range(NC):
                last = dve.tensor_tensor(ranked[:, c], hot[:, c, 64:112].rearrange("p (f w) -> p f w", f=3), ramp[:, c], ALU.mult)
            link(last)
            link(dve.tensor_reduce(code[:, :, :], ranked[:, :, :, :], AX.X, ALU.max))
            link(dve.tensor_scalar(code[:, :, :], code[:, :, :], -1.0, 16.0, ALU.mult, ALU.add))
            link(dve.scalar_tensor_tensor(out=code[:, :, :], in0=code[:, :, :], scalar=16.0, in1=code[:, :, :],
                                          op0=ALU.is_lt, op1=ALU.mult))
            lo, hi, amount = (code[:, :, f] for f in range(3))
            value_i, amount_i, shl_i, shr_i, low_i, high_i, res_i = (ibits[:, f, :] for f in range(7))
            do_shl, do_shr, shl_f, shr_f, active, res, low_f, high_f, not_shl, both = (bits[:, f, :] for f in range(10))
            dve.scalar_tensor_tensor(out=value_i, in0=hi, scalar=16.0, in1=lo, op0=ALU.mult, op1=ALU.add)
            link(dve.tensor_copy(amount_i, amount))
            dve.tensor_tensor(shl_i, value_i, amount_i, ALU.logical_shift_left)
            link(dve.tensor_tensor(shr_i, value_i, amount_i, ALU.logical_shift_right))
            link(dve.tensor_scalar(shl_i, shl_i, 255, None, ALU.bitwise_and))
            dve.tensor_copy(shl_f, shl_i)
            dve.tensor_copy(shr_f, shr_i)
            dve.tensor_scalar(not_shl, hot[:, :, 39], -1.0, 1.0, ALU.mult, ALU.add)
            dve.tensor_tensor(do_shl, hot[:, :, 0], hot[:, :, 39], ALU.mult)
            link(dve.tensor_tensor(do_shr, hot[:, :, 0], hot[:, :, 40], ALU.mult))
            link(dve.tensor_tensor(do_shr, do_shr, not_shl, ALU.mult))
            dve.tensor_tensor(active, do_shl, do_shr, ALU.add)
            dve.tensor_tensor(res, do_shl, shl_f, ALU.mult)
            link(dve.tensor_tensor(both, do_shr, shr_f, ALU.mult))
            link(dve.tensor_tensor(res_i, res, both, ALU.add))
            dve.tensor_scalar(low_i, res_i, 15, None, ALU.bitwise_and)
            link(dve.tensor_scalar(high_i, res_i, 4, None, ALU.logical_shift_right))
            dve.tensor_copy(low_f, low_i)
            dve.tensor_copy(high_f, high_i)
            link(dve.tensor_scalar(active, active, 2.0, None, ALU.mult))
            for c in range(NC):
                for f, digit_f in enumerate((low_f, high_f)):
                    last = dve.tensor_scalar(adds[:, c, f, :], iota_row[:, 0:16], digit_f[:, c:c + 1], active[:, c:c + 1],
                                             ALU.is_equal, ALU.mult)
            link(last)
            link(dve.tensor_tensor(y1[:, :, 128:160], y1[:, :, 128:160], adds[:, :, :, :].rearrange("p c f w -> p c (f w)"), ALU.add))
            link(dve.tensor_tensor(x2[:, :, :], x1[:, :, :], y1[:, :, :], ALU.add))

            layer_norm_moments(x2, 2)
            normalise(z, x2, 2, 3).then_inc(z_ready, 1)

            def node_onehots(s, parity, first=False):
                dve.wait_ge(ld_rows[parity], 16 * (s - parity) + 32)
                if not first:
                    dve.wait_ge(l1["psum"], 2 * s - 2)
                for which in range(2):
                    for k in range(NC):
                        last = dve.tensor_scalar(ohT[:, parity, which, k, :], idx_rows[:, parity, which, :], node_id[:, k:k + 1], None, ALU.is_equal)
                last.then_inc(ohT_ready, 1)

            def dst_onehots(s, parity, first=False):
                if not first:
                    dve.wait_ge(agg_done, s - 1)
                for t in range(TPS):
                    last = dve.tensor_scalar(ohd[:, parity, t, :], iota_row[:, :], idx_cols[:, 1, bass.ds(s * TPS + t, 1)], None, ALU.is_equal)
                last.then_inc(ohd_ready, 1)

            node_onehots(0, 0, True)
            node_onehots(1, 1, True)
            dve.wait_ge(ld_b1, 16)
            dve.wait_ge(xw_ps, 2)
            for c in range(NC):
                last = dve.tensor_tensor(x1[:, c, :], pg[:, c, :], b1_rows[:, :], ALU.add)
            last.then_inc(xd_sum, 1)
            dve.wait_ge(xw_hi, 1)
            dve.tensor_tensor(xs_lo[:, :, :], pa[:, :, :], xs_hi[:, :, :].bitcast(F32), ALU.subtract).then_inc(xw_lo, 1)
            dve.wait_ge(xw_hi, 2)
            dve.tensor_tensor(xd_lo[:, :, :], x1[:, :, :], xd_hi[:, :, :].bitcast(F32), ALU.subtract).then_inc(xw_lo, 1)

            def n_of(layer, t, u, half):
                dve.wait_ge(layer["exp"], u + 1)
                dve.tensor_scalar(t[:, half], t[:, half], EXP_CAP, None, ALU.min).then_inc(layer["cap"], 1)
                dve.wait_ge(layer["cap"], u + 1)
                dve.scalar_tensor_tensor(out=t[:, half], in0=t[:, half], scalar=2.0, in1=t[:, half],
                                         op0=ALU.add, op1=ALU.mult).then_inc(layer["n"], 1)

            def finish(layer, t, pre, u, half):
                dve.wait_ge(layer["r"], u + 1)
                dve.scalar_tensor_tensor(out=t[:, half], in0=t[:, half], scalar=-2.0, in1=pre,
                                         op0=ALU.mult, op1=ALU.mult).then_inc(layer["w"], 1)
                if layer is l1:
                    dve.wait_ge(layer["w"], u + 1)
                    dve.tensor_tensor(t[:, half], t[:, half], pre, ALU.add).then_inc(layer["y"], 1)

            def n1(s, half):
                n_of(l1, t1, 2 * s + half, half)

            def n2(s, half):
                n_of(l2, t2, 2 * s + half, half)

            def finish1(s, half):
                finish(l1, t1, l1_ps[half][:, :, :], 2 * s + half, half)

            def finish2(s, half):
                finish(l2, t2, pre2[:, half], 2 * s + half, half)

            def with_bias(s, half, first=False):
                dve.wait_ge(l2["psum"], 2 * s + half + 1)
                if not first:
                    dve.wait_ge(l2["y"], 2 * s + half - 1)
                for j in range(2):
                    last = dve.tensor_tensor(pre2[:, half, j, :], pc[:, j, :], b2_rows[:, :], ALU.add)
                last.then_inc(l2["pre"], 1)

            def step(s, parity, at=None):
                first = at == "first"
                if at != "last":
                    n1(s + 1, 1)
                    finish1(s + 1, 0)
                with_bias(s, 0, first)
                if at != "last":
                    finish1(s + 1, 1)
                n2(s, 0)
                if at not in ("no layer 1 after", "last"):
                    node_onehots(s + 2, parity)
                finish2(s, 0)
                with_bias(s, 1, first)
                dst_onehots(s, parity, at in ("first", "second"))
                n2(s, 1)
                if at not in ("no layer 1 after", "last"):
                    n1(s + 2, 0)
                finish2(s, 1)

            dve.wait_ge(ld_b2, 16)
            n1(0, 0)
            finish1(0, 0)
            n1(0, 1)
            finish1(0, 1)
            n1(1, 0)
            step(0, 0, "first")
            step(1, 1, "second")
            with dve.Fori(0, (NS - 6) // 2) as i:
                step(2 * i + 2, 0)
                step(2 * i + 3, 1)
            step(NS - 4, 0)
            step(NS - 3, 1)
            step(NS - 2, 0, "no layer 1 after")
            step(NS - 1, 1, "last")

            def fw1_low(f, parity):
                dve.wait_ge(fw1_hi_ready, f + 1)
                dve.tensor_tensor(fw1_lo[:, parity], fw1_raw[:, parity], fw1_hi[:, parity].bitcast(F32), ALU.subtract).then_inc(fw1_lo_ready, 1)

            def fw2_low(f, parity):
                dve.wait_ge(fw2_hi_ready, f + 1)
                dve.tensor_tensor(fw2_lo[:, parity], fw2_raw[:, parity], fw2_hi[:, parity].bitcast(F32), ALU.subtract).then_inc(fw2_lo_ready, 1)

            dve.wait_ge(agg_done, NS)
            dve.wait_ge(b3T_ps, 1)
            dve.tensor_copy(b3_cols[:, :], pc[:, 0, 0:DC]).then_inc(b3_ready, 1)
            dve.wait_ge(b3_ready, 1)
            dve.wait_ge(u_ps, DC)
            for c in range(DC):
                last = dve.tensor_scalar(pre_u[:, c, :], l1_ps[c // 2][:, c % 2, 0:N], b3_cols[:, c:c + 1], None, ALU.add)
            last.then_inc(u_pre, 1)
            dve.wait_ge(u_exp, 1)
            link(dve.tensor_scalar(uT[:, :, :], uT[:, :, :], EXP_CAP, None, ALU.min))
            dve.scalar_tensor_tensor(out=uT[:, :, :], in0=uT[:, :, :], scalar=2.0, in1=uT[:, :, :],
                                     op0=ALU.add, op1=ALU.mult).then_inc(u_n, 1)
            fw1_low(0, 0)
            dve.wait_ge(ld_b4, 16)
            for c in range(NC):
                last = dve.tensor_tensor(y4[:, c, :], z[:, c, :], b4_rows[:, :], ALU.add)
            link(last)
            dve.wait_ge(u_r, 1)
            link(dve.scalar_tensor_tensor(out=uT[:, :, :], in0=uT[:, :, :], scalar=-2.0, in1=pre_u[:, :, :],
                                          op0=ALU.mult, op1=ALU.mult))
            dve.tensor_tensor(uT[:, :, :], uT[:, :, :], pre_u[:, :, :], ALU.add).then_inc(u_ready, 1)

            def affine(t, gain, shift, base, dest):
                for op, other in ((ALU.mult, gain), (ALU.add, shift)):
                    for c in range(NC):
                        last = dve.tensor_tensor(t[:, c, :], t[:, c, :], other[:, :], op)
                    link(last)
                return [dve.tensor_tensor(dest[:, c, :], t[:, c, :], base[:, c, :], ALU.add) for c in range(NC)]

            dve.memset(ones_2[:, :].bitcast(F32), 1.0)
            dve.tensor_copy(signs[:, 1:2], node_id[0:2, 0:1])
            link(dve.tensor_scalar(signs[:, 0:1], node_id[0:2, 0:1], -2.0, 1.0, ALU.mult, ALU.add))
            dve.wait_ge(ld_bias_ffn, 32)
            link(dve.tensor_copy(fb1_hl[:, :], fb1_raw[:, :]))
            link(dve.tensor_scalar(fb1_raw[:, :], fb1_raw[:, :], signs[:, 1:2], None, ALU.mult))
            dve.scalar_tensor_tensor(out=fb1_hl[:, :], in0=fb1_hl[:, :].bitcast(F32), scalar=signs[:, 0:1], in1=fb1_raw[:, :],
                                     op0=ALU.mult, op1=ALU.add).then_inc(fb1_ready, 1)
            dve.wait_ge(out4_ps, NC)
            link(dve.tensor_tensor(y4[:, :, :], pg[:, :, :], y4[:, :, :], ALU.add))
            layer_norm_moments(y4, 3)
            link(normalise(y4, y4, 3, 4))
            dve.wait_ge(ld_affine, 64)
            link(affine(y4, gamma1_rows, beta1_rows, x2, x3)[-1])
            layer_norm_moments(x3, 4)
            normalise(tok, x3, 4, 5).then_inc(tok_ready, 1)

            dve.wait_ge(tokT_ready, 2)
            dve.tensor_tensor(tokT_lo[:, :, :], tokT[:, :, :], tokT_hi[:, :, :].bitcast(F32),
                              ALU.subtract).then_inc(tokT_ready, 1)
            fw1_low(1, 1)
            fw2_low(0, 0)

            dve.wait_ge(logits_ps, 1)
            for c in range(NC):
                last = dve.tensor_tensor(logits[:, c, :], pa[:, c, 0:EX], bg_rows[:, :], ALU.add)
            link(last)
            link(dve.tensor_reduce(small[:, 2, :], logits[:, :, :], AX.X, ALU.max))
            dve.tensor_scalar(small[:, 0, :], small[:, 2, :], -1.0, None, ALU.mult).then_inc(neg_max, 1)
            dve.wait_ge(exp_sum, 2)
            link(dve.reciprocal(small[:, 3, :], small[:, 1, :]))
            for c in range(NC):
                last = dve.tensor_scalar(probs[:, c, :], probs[:, c, :], small[:, 3, c:c + 1], None, ALU.mult)
            link(last)
            for c in range(NC):
                last = dve.max(top[:, c, :], probs[:, c, :])
            link(last)
            for c in range(NC):
                last = dve.max_index(top_at[:, c, :], top[:, c, :], probs[:, c, :])
            link(last)
            link(dve.tensor_copy(top_atf[:, :, :], top_at[:, :, :]))
            for c in range(NC):
                last = dve.tensor_scalar(chosen[:, c, :], iota_row[:, 0:EX], top_atf[:, c, 0:1], None, ALU.is_equal)
            link(last)
            for c in range(NC):
                last = dve.scalar_tensor_tensor(out=chosen[:, c, :], in0=iota_row[:, 0:EX], scalar=top_atf[:, c, 1:2],
                                                in1=chosen[:, c, :], op0=ALU.is_equal, op1=ALU.add)
            link(last)
            dve.tensor_tensor(gates[:, :, :], probs[:, :, :], chosen[:, :, :], ALU.mult).then_inc(gates_ready, 1)
            dve.wait_ge(gates_ready, 1)

            def gated(f, parity, first=False):
                dve.wait_ge(f1_ps, f + 1)
                if not first:
                    dve.wait_ge(gT_ps, f)
                for c in range(NC):
                    gate = gates[:, c, bass.ts(f, XS)].unsqueeze(2).broadcast_to((P, XS, EH))
                    dve.scalar_tensor_tensor(out=g_sb[:, c, :].rearrange("p (e h) -> p e h", h=EH),
                                             in0=(pb, pa)[parity][:, c, :].rearrange("p (e h) -> p e h", h=EH), scalar=0.0,
                                             in1=gate, op0=ALU.max, op1=ALU.mult).then_inc(f1_g, 1)

            def gated_low(f):
                dve.wait_ge(gT_hi_ready, f + 1)
                dve.tensor_tensor(gT_lo[:, :, :], pc.rearrange("p b (k n) -> p (b k) n", n=N), gT_hi[:, :, :].bitcast(F32),
                                  ALU.subtract).then_inc(gT_ready, 1)

            def step(f, parity, fw1_more=True, fw2_more=True, last=False):
                gated_low(f)
                if not last:
                    gated(f + 1, 1 - parity)
                if fw1_more:
                    fw1_low(f + 3, 1 - parity)
                if fw2_more:
                    fw2_low(f + 1, 1 - parity)

            gated(0, 0, True)
            fw1_low(2, 0)
            step(0, 0)
            with dve.Fori(0, (FS - 4) // 2) as i:
                step(2 * i + 1, 1)
                step(2 * i + 2, 0)
            step(FS - 3, 1, fw1_more=False)
            step(FS - 2, 0, fw1_more=False)
            step(FS - 1, 1, fw1_more=False, fw2_more=False, last=True)

            dve.wait_ge(f2_ps, FS)
            link(dve.tensor_tensor(y5[:, :, :], pg[:, :, :], tok[:, :, :], ALU.add))
            layer_norm_moments(y5, 0)
            link(normalise(y5, y5, 0, 6))
            for ins in affine(y5, gamma2_rows, beta2_rows, x3, fin):
                ins.then_inc(fin_ready, 1)


_INS = ["x", "src", "dst", "edge_attr_64", "L0_gnn_weight", "L0_gnn_bias", "L1_gnn_W1", "L1_gnn_b1", "L1_gnn_W2",
        "L1_gnn_b2", "L1_gnn_W3", "L1_gnn_b3", "L1_gnn_W4", "L1_gnn_b4", "L1_gnn_gamma", "L1_gnn_beta", "L1_ffn_Wg",
        "L1_ffn_bg", "L1_ffn_W1", "L1_ffn_b1", "L1_ffn_W2", "L1_ffn_b2", "L1_ffn_gamma", "L1_ffn_beta"]


def kernel(**inputs):
    import numpy as _np
    import concourse.bacc as _bacc
    from concourse import mybir as _mybir
    from concourse.bass_utils import run_bass_kernel_spmd as _run

    nc = _bacc.Bacc("TRN2", target_bir_lowering=False, num_devices=1)
    arrays, args = {}, []
    for name in _INS:
        a = _np.ascontiguousarray(inputs[name])
        arrays[f"in_{name}_dram"] = a
        args.append(nc.dram_tensor(f"in_{name}_dram", a.shape, _mybir.dt.from_np(a.dtype), kind="ExternalInput").ap())
    out = nc.dram_tensor("out_0_dram", inputs["x"].shape, _mybir.dt.float32, kind="ExternalOutput").ap()
    gnn_ffn_stack(nc, *args, out)
    r = _run(nc, [arrays], core_ids=[0])
    return r.results[0]["out_0_dram"]
```

```python
from contextlib import ExitStack

import concourse.bass as bass
from concourse import mybir

F32 = mybir.dt.float32
F32R = mybir.dt.float32r
BF16 = mybir.dt.bfloat16
I32 = mybir.dt.int32
U32 = mybir.dt.uint32
ALU = mybir.AluOpType
ACT = mybir.ActivationFunctionType
AX = mybir.AxisListType

P = 128
EPS = 1e-5
EXP_CAP = float(2 ** 30)
HOT = 0.5


def gnn_ffn_stack(nc, x, src, dst, edge_attr, w0, b0, w1, b1, w2, b2, w3, b3, w4, b4, gamma1, beta1,
                  wg, bg, fw1, fb1, fw2, fb2, gamma2, beta2, out):
    N, D = x.shape
    E, EA = edge_attr.shape
    NC, DC = N // P, D // P
    NT = E // P
    SE = 512
    TPS = SE // P
    NS = E // SE
    CT = 8
    AT = 8
    EX = wg.shape[1]
    EH = fw1.shape[2]
    HC = 512
    XS = HC // EH
    FS = EX * EH // HC
    assert (NC, DC, P % EA, NS % 2) == (2, 4, 0, 0)

    with ExitStack() as ctx:
        def sem(name):
            return ctx.enter_context(nc.semaphore(name))

        cursor = [(nc.sbuf_base + 31) // 32 * 32]

        def sb(name, shape, dt):
            size = 4 if dt in (F32, F32R, I32, U32) else 2
            for n in shape[1:]:
                size *= n
            t = nc.alloc_sbuf_tensor_at(name, shape, dt, offset=cursor[0])
            cursor[0] += (size + 31) // 32 * 32
            return t

        ident = sb("ident", [P, P], F32)
        zeros_pp = sb("zeros_pp", [P, P], F32)
        iota_i = sb("iota_i", [P, N], I32)
        iota_row = sb("iota_row", [P, N], F32)
        iota_bf = sb("iota_bf", [P, N], BF16)
        node_i = sb("node_i", [P, NC], I32)
        node_id = sb("node_id", [P, NC], F32)
        minus_half = sb("minus_half", [P, NC], F32)
        idx_cols = sb("idx_cols", [P, 2, NT], F32)
        x2 = sb("x2", [P, NC, D], F32)
        z = sb("z", [P, NC, D], F32)
        zT = sb("zT", [P, DC, N], F32)
        stats = sb("stats", [P, 5, NC, 6], F32)
        moments = sb("moments", [P, 5, NC, 2], F32)
        var_eps = sb("var_eps", [P, 5, NC], F32)
        rstd = sb("rstd", [P, 5, NC], F32)
        shared = cursor[0]

        eaT = sb("eaT", [P, E], F32R)
        eaT_end = cursor[0]
        w2_hi = sb("w2_hi", [P, DC, D], F32R)
        w2_lo = sb("w2_lo", [P, DC, D], F32R)
        w1c_hi = sb("w1c_hi", [P, D], F32R)
        w1c_lo = sb("w1c_lo", [EA, D], F32R)
        xs_at = cursor[0]
        xs_hi = sb("xs_hi", [P, NC, D], F32R)
        xs_lo = sb("xs_lo", [P, NC, D], F32R)
        xd_at = cursor[0]
        xd_hi = sb("xd_hi", [P, NC, D], F32R)
        xd_lo = sb("xd_lo", [P, NC, D], F32R)
        ohT_at = cursor[0]
        ohT = sb("ohT", [P, 2, 2, NC, SE], F32R)
        idx_rows = sb("idx_rows", [P, 2, 2, SE], I32)
        ohd_at = cursor[0]
        ohd = sb("ohd", [P, 2, TPS, N], F32R)
        b2_rows = sb("b2_rows", [P, D], F32)
        over = cursor[0]
        h_hi = sb("h_hi", [P, 2, DC, SE], F32R)
        h_lo = sb("h_lo", [P, 2, DC, SE], F32R)
        m_hi = sb("m_hi", [P, 2, 2, D], F32R)
        m_lo = sb("m_lo", [P, 2, 2, D], F32R)
        t1 = sb("t1", [P, 2, 2, SE], F32)
        t2 = sb("t2", [P, 2, 2, D], F32)
        pre2 = sb("pre2", [P, 2, 2, D], F32)
        edge_end = cursor[0]

        cursor[0] = over
        xin_at = cursor[0]
        xin = sb("xin", [P, NC, D], F32)
        xn = sb("xn", [P, NC, D], F32)
        xnT = sb("xnT", [P, DC, N], F32)
        y0_hi = sb("y0_hi", [P, NC, D], F32R)
        y0_lo = sb("y0_lo", [P, NC, D], F32R)
        w1_hi = sb("w1_hi", [P, 2, DC, D], F32R)
        zT_lo = sb("zT_lo", [P, DC, N], F32R)
        w0_sb = sb("w0_sb", [P, DC, D], F32)
        w1_sb_at = cursor[0]
        w1_sb = sb("w1_sb", [P, 2, DC, D], F32)
        b0_rows = sb("b0_rows", [P, D], F32)
        b1_rows = sb("b1_rows", [P, D], F32)
        idx_i = sb("idx_i", [NT, 2, P], I32)
        idx_f = sb("idx_f", [NT, 2, P], F32)
        adj = sb("adj", [P, NC, N], F32R)
        counts = sb("counts", [P, NC, N], F32)
        eye = sb("eye", [P, NC, N], F32)
        deg = sb("deg", [P, NC], F32)
        dinv = sb("dinv", [P, NC], F32)
        x1 = sb("x1", [P, NC, D], F32)
        y1 = sb("y1", [P, NC, D], F32)
        flags = sb("flags", [P, 5, NC], F32)
        masks = sb("masks", [P, 3, NC], I32)
        ranked = sb("ranked", [P, NC, 3, 16], F32)
        rank = sb("rank", [P, NC, 3], F32)
        code = sb("code", [P, NC, 3], I32)
        words = sb("words", [P, 3, NC], I32)
        digits = sb("digits", [P, NC, 2], I32)
        hit = sb("hit", [P, NC, 2, 16], F32)
        ramp_i = sb("ramp_i", [P, NC, 3, 16], I32)
        ramp = sb("ramp", [P, NC, 3, 16], F32)
        xn_shift = sb("xn_shift", [P, NC], F32)
        x2_scale = sb("x2_scale", [P, NC], F32)
        x2_shift = sb("x2_shift", [P, NC], F32)
        w1c_raw = sb("w1c_raw", [P, D], F32)
        assert max(cursor[0], edge_end) <= nc.sbuf_usable_end, (cursor[0], edge_end)
        w1_lo = nc.alloc_sbuf_tensor_at("w1_lo", [P, 2, DC, D], F32R, offset=w1_sb_at)
        zT_hi = nc.alloc_sbuf_tensor_at("zT_hi", [P, DC, N], F32R, offset=xin_at)
        oh_s = nc.alloc_sbuf_tensor_at("oh_s", [P, 2, CT, N], BF16, offset=ohT_at)
        oh_d = nc.alloc_sbuf_tensor_at("oh_d", [P, 2, CT, N], BF16, offset=ohT_at + 2 * CT * N * 2)
        ea_hl = nc.alloc_sbuf_tensor_at("ea_hl", [P, 2, AT, 2, EA], F32R, offset=ohd_at)
        ea_raw = nc.alloc_sbuf_tensor_at("ea_raw", [P, 2, 2 * AT, EA], F32, offset=xs_at)
        w2_raw = nc.alloc_sbuf_tensor_at("w2_raw", [P, DC, D], F32, offset=xd_at)

        cursor[0] = shared
        w3_sb = sb("w3_sb", [P, 2 * DC, D], F32)
        w4_sb = sb("w4_sb", [P, DC, D], F32)
        b4_rows = sb("b4_rows", [P, D], F32)
        b3_nat = sb("b3_nat", [DC, P], F32)
        assert cursor[0] <= eaT_end
        cursor[0] = eaT_end
        gamma1_rows = sb("gamma1_rows", [P, D], F32)
        beta1_rows = sb("beta1_rows", [P, D], F32)
        gamma2_rows = sb("gamma2_rows", [P, D], F32)
        beta2_rows = sb("beta2_rows", [P, D], F32)
        aggT_at = cursor[0]
        aggT_hi = sb("aggT_hi", [P, DC, N], F32R)
        aggT_lo = sb("aggT_lo", [P, DC, N], F32R)
        tokT_at = cursor[0]
        pre_u = sb("pre_u", [P, DC, N], F32)
        assert cursor[0] <= xs_at
        cursor[0] = xs_at
        w3b_hi = sb("w3b_hi", [P, DC, D], F32R)
        w4_hi = sb("w4_hi", [P, DC, D], F32R)
        assert cursor[0] <= ohT_at
        fin_at = cursor[0]
        y4 = sb("y4", [P, NC, D], F32)
        x3 = sb("x3", [P, NC, D], F32)
        tok = sb("tok", [P, NC, D], F32)
        uT = sb("uT", [P, DC, N], F32)
        agg = nc.alloc_sbuf_tensor_at("agg", [P, NC, D], F32, offset=cursor[0] - DC * N * 4)
        b3_cols = sb("b3_cols", [P, DC], F32)
        wg_sb = sb("wg_sb", [P, DC, EX], F32)
        bg_rows = sb("bg_rows", [P, EX], F32)
        logits = sb("logits", [P, NC, EX], F32)
        probs = sb("probs", [P, NC, EX], F32)
        top = sb("top", [P, NC, 8], F32)
        top_at = sb("top_at", [P, NC, 8], U32)
        top_atf = sb("top_atf", [P, NC, 8], F32)
        chosen = sb("chosen", [P, NC, EX], F32)
        gates = sb("gates", [P, NC, EX], F32)
        gatesT = sb("gatesT", [EX, N], F32)
        small = sb("small", [P, 4, NC], F32)
        fb1_rows = sb("fb1_rows", [P, EX * EH], F32)
        fb2_sb = sb("fb2_sb", [EX, D], F32)
        g_sb = sb("g_sb", [P, NC, HC], F32)
        gT_hi = sb("gT_hi", [P, HC // P, N], F32R)
        gT_lo = sb("gT_lo", [P, HC // P, N], F32R)
        y5 = sb("y5", [P, NC, D], F32)
        fw1_hi = sb("fw1_hi", [P, 2, XS, DC, EH], F32R)
        fw1_lo = sb("fw1_lo", [P, 2, XS, DC, EH], F32R)
        fw1_raw = sb("fw1_raw", [P, 2, XS, DC, EH], F32)
        fw2_raw = sb("fw2_raw", [P, 2, HC // P, D], F32)
        assert cursor[0] <= nc.sbuf_usable_end, cursor[0]
        cursor[0] = shared
        fw2_hi = sb("fw2_hi", [P, 2, HC // P, D], F32R)
        fw2_lo = sb("fw2_lo", [P, 2, HC // P, D], F32R)
        assert cursor[0] <= eaT_end
        w3b_lo = nc.alloc_sbuf_tensor_at("w3b_lo", [P, DC, D], F32R, offset=shared + DC * D * 4)
        w4_lo = nc.alloc_sbuf_tensor_at("w4_lo", [P, DC, D], F32R, offset=shared + 2 * DC * D * 4)
        uT_hi = nc.alloc_sbuf_tensor_at("uT_hi", [P, DC, N], F32R, offset=aggT_at)
        uT_lo = nc.alloc_sbuf_tensor_at("uT_lo", [P, DC, N], F32R, offset=aggT_at + DC * N * 4)
        gT2_hi = nc.alloc_sbuf_tensor_at("gT2_hi", [P, HC // P, N], F32R, offset=aggT_at)
        gT2_lo = nc.alloc_sbuf_tensor_at("gT2_lo", [P, HC // P, N], F32R, offset=aggT_at + DC * N * 4)
        tokT_hi = nc.alloc_sbuf_tensor_at("tokT_hi", [P, DC, N], F32R, offset=xs_at)
        tokT_lo = nc.alloc_sbuf_tensor_at("tokT_lo", [P, DC, N], F32R, offset=xs_at + DC * N * 4)
        tokT = nc.alloc_sbuf_tensor_at("tokT", [P, DC, N], F32, offset=tokT_at)
        fin = nc.alloc_sbuf_tensor_at("fin", [P, NC, D], F32, offset=fin_at)

        pa, pb, pc, pg = (ctx.enter_context(nc.psum_tensor(n, [P, 2, 512], F32)) for n in ("pa", "pb", "pc", "pg"))
        l1_ps = (pb, pa)

        def l1_banks(s, half):
            return ((pa, pb), (pg, pa))[s][half] if isinstance(s, int) and s < 2 else l1_ps[half]

        def l2_banks(s, half, final):
            if final:
                return l1_ps[half]
            return pg if isinstance(s, int) and (s, half) == (0, 1) else pc

        ld_idx, ld_x, ld_ea, ld_w0, ld_b0, ld_w1, ld_b1, ld_rows, ld_w2, ld_w1c, ld_b2 = map(sem, (
            "ld_idx", "ld_x", "ld_ea", "ld_w0", "ld_b0", "ld_w1", "ld_b1", "ld_rows0", "ld_w2", "ld_w1c", "ld_b2"))
        ld_rows = (ld_rows, sem("ld_rows1"))
        ld_ea = (ld_ea, sem("ld_ea_odd"))
        ld_w3, ld_w4, ld_b3, ld_b4, ld_affine, ld_wg, ld_fb2, ld_fw1, ld_fw2 = map(sem, (
            "ld_w3", "ld_w4", "ld_b3", "ld_b4", "ld_affine", "ld_wg", "ld_fb2", "ld_fw1", "ld_fw2"))
        ld_fb1 = (sem("ld_fb1_even"), sem("ld_fb1_odd"))
        ld_fw1, ld_fw2 = (ld_fw1, sem("ld_fw1_odd")), (ld_fw2, sem("ld_fw2_odd"))
        fw1_hi_ready, fw1_lo_ready, fw2_hi_ready, fw2_lo_ready, gT_hi_ready = map(sem, (
            "fw1_hi_ready", "fw1_lo_ready", "fw2_hi_ready", "fw2_lo_ready", "gT_hi_ready"))
        consts, idx_f_ready, idxT_ps, dve_link, onehots, counted = map(sem, (
            "consts", "idx_f_ready", "idxT_ps", "dve_link", "onehots", "counted"))
        pool_link, act_link = map(sem, ("pool_link", "act_link"))
        counts_ready, countsT_ps, adj_ready, deg_ready, dinv_ready, var_ready, rstd_ready = map(sem, (
            "counts_ready", "countsT_ps", "adj_ready", "deg_ready", "dinv_ready", "var_ready", "rstd_ready"))
        xn_coefs = sem("xn_coefs")
        x2_coefs, x2_rest, w1_hi_ready, w1_lo_ready, xs_sum = map(sem, (
            "x2_coefs", "x2_rest", "w1_hi_ready", "w1_lo_ready", "xs_sum"))
        xn_ready, xnT_ps, xnT_ready, y0_ps, y0_hi_ready, y0_lo_ready, zT_hi_ready, zT_lo_ready = map(sem, (
            "xn_ready", "xnT_ps", "xnT_ready", "y0_ps", "y0_hi_ready", "y0_lo_ready", "zT_hi_ready", "zT_lo_ready"))
        conv_ps, z_ready, zT_ps, zT_ready, xw_ps = map(sem, (
            "conv_ps", "z_ready", "zT_ps", "zT_ready", "xw_ps"))
        ea_hi_ready, ea_lo_ready, eaT_ps, eaT_ready, w_hi_ready, w_lo_ready, xw_hi, xw_lo = map(sem, (
            "ea_hi_ready", "ea_lo_ready", "eaT_ps", "eaT_ready", "w_hi_ready", "w_lo_ready", "xw_hi", "xw_lo"))
        ohT_ready, ohd_ready, agg_done = map(sem, ("ohT_ready", "ohd_ready", "agg_done"))
        l1 = {k: sem("l1_" + k) for k in ("psum", "exp", "cap", "square", "ln", "r", "y", "hi", "lo")}
        l2 = {k: sem("l2_" + k) for k in ("psum", "pre", "exp", "cap", "square", "ln", "r", "y", "hi", "lo")}
        agg_ready, aggT_ps = sem("agg_ready"), sem("aggT_ps")
        wu_hi_ready, wu_lo_ready, aggT_hi_ready, aggT_lo_ready, b3T_ps, b3_ready = map(sem, (
            "wu_hi_ready", "wu_lo_ready", "aggT_hi_ready", "aggT_lo_ready", "b3T_ps", "b3_ready"))
        u_square, residual = sem("u_square"), sem("residual")
        u_ps, u_pre, u_exp, u_cap, u_ln, u_r, u_ready, u_hi, u_lo, out4_ps = map(sem, (
            "u_ps", "u_pre", "u_exp", "u_cap", "u_ln", "u_r", "u_ready", "u_hi", "u_lo", "out4_ps"))
        chunk_var, chunk_rstd, tok_ready, tokT_ps, tokT_hi_ready, tokT_ready, tokT_lo_ready = map(sem, (
            "chunk_var", "chunk_rstd", "tok_ready", "tokT_ps", "tokT_hi_ready", "tokT_ready", "tokT_lo_ready"))
        logits_ps, neg_max, exp_sum, gates_ready, gatesT_ps, gatesT_ready, f1_sum = map(sem, (
            "logits_ps", "neg_max", "exp_sum", "gates_ready", "gatesT_ps", "gatesT_ready", "f1_sum"))
        f1_ps, f1_g, gT_ps, gT_ready, f2_ps, f2_chunk, fin_ready, stored = map(sem, (
            "f1_ps", "f1_g", "gT_ps", "gT_ready", "f2_ps", "f2_chunk", "fin_ready", "stored"))

        by_node = lambda a: a.rearrange("(c p) d -> p c d", p=P)
        rows = lambda a, n: a.unsqueeze(0).broadcast_to((P, n))

        block = ctx.enter_context(nc.Block())

        @block.sync
        def _(sp):
            for k, idx in enumerate((src, dst)):
                sp.dma_start(idx_i[:, k, :], idx.rearrange("(t p) -> t p", p=P)).then_inc(ld_idx, 16)
            sp.dma_start(xin[:, :, :], by_node(x)).then_inc(ld_x, 16)
            ea_tiles = edge_attr.rearrange("(t p) a -> p t a", p=P)

            def load_ea(c):
                if c >= 2:
                    sp.wait_ge(ea_lo_ready, 2 * c - 2)
                sp.dma_start(ea_raw[:, c % 2], ea_tiles[:, 2 * AT * c:2 * AT * (c + 1), :]).then_inc(ld_ea[c % 2], 16)

            load_ea(0)
            sp.dma_start(w0_sb[:, :, :], w0.rearrange("(k p) n -> p k n", p=P)).then_inc(ld_w0, 16)
            for half in range(2):
                sp.dma_start(w1c_raw[half * EA:half * EA + EA, :], w1[2 * D:2 * D + EA, :]).then_inc(ld_w1c, 16)
            sp.dma_start(w1_sb[:, :, :, :], w1[0:2 * D, :].rearrange("(g k p) n -> p g k n", g=2, p=P)).then_inc(ld_w1, 16)
            load_ea(1)
            sp.dma_start(b0_rows[:, :], rows(b0, D)).then_inc(ld_b0, 16)
            sp.dma_start(w2_raw[:, :, :], w2.rearrange("(k p) n -> p k n", p=P)).then_inc(ld_w2, 16)
            sp.dma_start(b1_rows[:, :], rows(b1, D)).then_inc(ld_b1, 16)
            sp.dma_start(b2_rows[:, :], rows(b2, D)).then_inc(ld_b2, 16)

            def load_idx_rows(s, parity):
                for k, idx in enumerate((src, dst)):
                    sp.dma_start(idx_rows[:, parity, k, :], rows(idx[bass.ts(s, SE)], SE)).then_inc(ld_rows[parity], 16)

            load_idx_rows(0, 0)
            load_idx_rows(1, 1)
            load_ea(2)
            load_ea(3)
            with sp.Fori(1, NS // 2) as i:
                for parity in range(2):
                    sp.wait_ge(ohT_ready, 2 * i + parity - 1)
                    load_idx_rows(2 * i + parity, parity)

            sp.wait_ge(l1["psum"], 2 * NS)
            sp.dma_start(b3_nat[:, :], b3.rearrange("(c p) -> c p", p=P)).then_inc(ld_b3, 16)
            sp.dma_start(w3_sb[:, :, :], w3.rearrange("(k p) n -> p k n", p=P)).then_inc(ld_w3, 16)
            sp.dma_start(w4_sb[:, :, :], w4.rearrange("(k p) n -> p k n", p=P)).then_inc(ld_w4, 16)
            sp.dma_start(b4_rows[:, :], rows(b4, D)).then_inc(ld_b4, 16)
            sp.wait_ge(agg_done, NS)
            sp.dma_start(fb2_sb[:, :], fb2).then_inc(ld_fb2, 16)
            for t, a in ((gamma1_rows, gamma1), (beta1_rows, beta1), (gamma2_rows, gamma2), (beta2_rows, beta2)):
                sp.dma_start(t[:, :], rows(a, D)).then_inc(ld_affine, 16)
            sp.dma_start(wg_sb[:, :, :], wg.rearrange("(p k) e -> p k e", k=DC)).then_inc(ld_wg, 16)
            sp.dma_start(bg_rows[:, :], rows(bg, EX)).then_inc(ld_wg, 16)
            fw1_steps = fw1.rearrange("e (p k) h -> p e k h", k=DC)
            fw2_steps = fw2.rearrange("e h d -> (e h) d").rearrange("(f j p) d -> p f j d", j=HC // P, p=P)

            fb1_row = fb1.rearrange("e h -> (e h)")

            def load_fw(f, parity):
                sp.dma_start(fb1_rows[:, bass.ts(f, HC)], rows(fb1_row[bass.ts(f, HC)], HC)).then_inc(ld_fb1[parity], 16)
                sp.dma_start(fw1_raw[:, parity], fw1_steps[:, bass.ts(f, XS)]).then_inc(ld_fw1[parity], 16)

            def load_fw2(f, parity):
                sp.dma_start(fw2_raw[:, parity], fw2_steps[:, bass.ds(f, 1)].rearrange("p f j d -> p (f j) d")).then_inc(ld_fw2[parity], 16)

            for f in range(2):
                load_fw(f, f)
            for f in range(2):
                load_fw2(f, f)
            for f in range(2, 4):
                sp.wait_ge(fw1_lo_ready, f - 1)
                load_fw(f, f % 2)
            with sp.Fori(1, FS // 2 - 1) as i:
                for parity in range(2):
                    sp.wait_ge(fw2_lo_ready, 2 * i + parity - 1)
                    load_fw2(2 * i + parity, parity)
                    sp.wait_ge(fw1_lo_ready, 2 * i + parity + 1)
                    load_fw(2 * i + parity + 2, parity)
            for f in range(FS - 2, FS):
                sp.wait_ge(fw2_lo_ready, f - 1)
                load_fw2(f, f % 2)
            for c in range(NC):
                sp.wait_ge(fin_ready, c + 1)
                sp.dma_start(by_node(out)[:, c, :], fin[:, c, :]).then_inc(stored, 16)
            sp.wait_ge(stored, 16 * NC)

        @block.gpsimd
        def _(pool):
            linked = [0]

            def link(ins):
                linked[0] += 1
                ins.then_inc(pool_link, 1)
                pool.wait_ge(pool_link, linked[0])

            link(pool.memset(zeros_pp[:, :], 0.0))
            pool.affine_select(out=ident[:, :], in_=zeros_pp[:, :], compare_op=ALU.not_equal, fill=1.0,
                               base=0, pattern=[[-1, P]], channel_multiplier=1).then_inc(consts, 1)
            pool.iota(iota_i[:, :], pattern=[[1, N]], base=0, channel_multiplier=0).then_inc(consts, 1)
            pool.iota(node_i[:, :], pattern=[[P, NC]], base=0, channel_multiplier=1).then_inc(consts, 1)
            pool.iota(ramp_i[:, :, :, :].rearrange("p c f w -> p (c f) w"), pattern=[[0, 3 * NC], [-1, 16]], base=16, channel_multiplier=0).then_inc(consts, 1)
            pool.memset(minus_half[:, :], -0.5).then_inc(consts, 1)
            link(pool.memset(eye[:, :, :], 0.0))
            for c in range(NC):
                pool.affine_select(out=eye[:, c, :], in_=eye[:, c, :], compare_op=ALU.not_equal, fill=1.0,
                                   base=c * P, pattern=[[-1, N]], channel_multiplier=1).then_inc(consts, 1)

            def inverse_root(which, ready, ready_at, result, done):
                pool.wait_ge(ready, ready_at)
                pool.tensor_tensor(result, which, minus_half[:, :], ALU.pow).then_inc(done, 1)

            inverse_root(var_eps[:, 0, :], var_ready, 1, rstd[:, 0, :], rstd_ready)

            def ea_low(e):
                pool.wait_ge(ea_hi_ready, e + 1)
                pool.tensor_tensor(ea_hl[:, e % 2, :, 1, :], ea_raw[:, e // 2 % 2, e % 2 * AT:(e % 2 + 1) * AT, :],
                                   ea_hl[:, e % 2, :, 0, :].bitcast(F32), ALU.subtract).then_inc(ea_lo_ready, 1)

            def w1_low(g):
                pool.wait_ge(w1_hi_ready, g + 1)
                pool.tensor_tensor(w1_lo[:, g], w1_sb[:, g], w1_hi[:, g].bitcast(F32), ALU.subtract).then_inc(w1_lo_ready, 1)

            ea_low(0)
            ea_low(1)
            pool.wait_ge(w_hi_ready, 1)
            pool.tensor_tensor(w1c_lo[:, :], w1c_raw[0:EA, :], w1c_hi[0:EA, :].bitcast(F32), ALU.subtract).then_inc(w_lo_ready, 1)
            w1_low(0)
            inverse_root(deg[:, :], deg_ready, 1, dinv[:, :], dinv_ready)
            ea_low(2)
            ea_low(3)
            w1_low(1)
            inverse_root(var_eps[:, 1, :], var_ready, 2, rstd[:, 1, :], rstd_ready)
            for e in range(4, NT // AT - 1):
                ea_low(e)
            inverse_root(var_eps[:, 2, :], var_ready, 3, rstd[:, 2, :], rstd_ready)
            ea_low(NT // AT - 1)
            pool.wait_ge(w_hi_ready, 2)
            pool.tensor_tensor(w2_lo[:, :, :], w2_raw[:, :, :], w2_hi[:, :, :].bitcast(F32), ALU.subtract).then_inc(w_lo_ready, 1)

            def low1(s, parity):
                for half in range(2):
                    pool.wait_ge(l1["hi"], 2 * s + half + 1)
                    pool.tensor_tensor(h_lo[:, parity, 2 * half:2 * half + 2, :], t1[:, half],
                                       h_hi[:, parity, 2 * half:2 * half + 2, :].bitcast(F32), ALU.subtract).then_inc(l1["lo"], 1)

            with pool.Fori(0, NS // 2) as i:
                for parity in range(2):
                    low1(2 * i + parity, parity)

            pool.wait_ge(wu_hi_ready, 1)
            pool.tensor_tensor(w3b_lo[:, :, :], w3_sb[:, DC:2 * DC, :], w3b_hi[:, :, :].bitcast(F32), ALU.subtract).then_inc(wu_lo_ready, 1)
            pool.wait_ge(wu_hi_ready, 2)
            pool.tensor_tensor(w4_lo[:, :, :], w4_sb[:, :, :], w4_hi[:, :, :].bitcast(F32), ALU.subtract).then_inc(wu_lo_ready, 1)
            for n, (which, c) in enumerate((which, c) for which in (3, 4, 0) for c in range(NC)):
                pool.wait_ge(chunk_var, n + 1)
                pool.tensor_tensor(rstd[:, which, c:c + 1], var_eps[:, which, c:c + 1], minus_half[:, 0:1], ALU.pow).then_inc(chunk_rstd, 1)

        @block.scalar
        def _(act):
            act.preload_act_table_set("natural_log_exp_and_others")

            def ea_high(e):
                c = e // 2
                act.wait_ge(ld_ea[c % 2], 16 * (c // 2 + 1))
                if e >= 2:
                    act.wait_ge(eaT_ps, 2 * e - 2)
                act.activation(ea_hl[:, e % 2, :, 0, :], ea_raw[:, c % 2, e % 2 * AT:(e % 2 + 1) * AT, :], ACT.Copy).then_inc(ea_hi_ready, 1)

            def ea_out(e):
                for n in range(2 * e, 2 * e + 2):
                    act.wait_ge(eaT_ps, n + 1)
                    act.activation(eaT[:, bass.ts(n, 4 * P)], pb[:, n % 2, :], ACT.Copy).then_inc(eaT_ready, 1)

            ea_high(0)
            ea_high(1)
            ea_out(0)
            ea_out(1)
            act.wait_ge(ld_w1c, 32)
            act.activation(w1c_hi[:, :], w1c_raw[:, :], ACT.Copy).then_inc(w_hi_ready, 1)
            act.wait_ge(xn_coefs, 1)
            for c in range(NC):
                act.activation(xn[:, c, :], xin[:, c, :], ACT.Identity, bias=xn_shift[:, c:c + 1],
                               scale=rstd[:, 0, c:c + 1]).then_inc(xn_ready, 1)
            act.wait_ge(xnT_ps, 1)
            act.activation(xnT[:, :, :], pg.rearrange("p b (k n) -> p (b k) n", n=N), ACT.Copy).then_inc(xnT_ready, 1)
            act.wait_ge(ld_w1, 16)
            for g in range(2):
                act.activation(w1_hi[:, g], w1_sb[:, g], ACT.Copy).then_inc(w1_hi_ready, 1)
            ea_high(2)
            ea_high(3)
            act.wait_ge(ld_w2, 16)
            act.activation(w2_raw[:, :, :], w2_raw[:, :, :], ACT.Copy, scale=-2.0).then_inc(act_link, 1)
            act.wait_ge(act_link, 1)
            act.activation(w2_hi[:, :, :], w2_raw[:, :, :], ACT.Copy).then_inc(w_hi_ready, 1)
            act.wait_ge(dinv_ready, 1)
            for c in range(NC):
                act.wait_ge(y0_ps, c + 1)
                act.activation(y0_hi[:, c, :], pc[:, c, :], ACT.Copy, scale=dinv[:, c:c + 1]).then_inc(y0_hi_ready, 1)
            ea_out(2)
            ea_high(4)
            ea_out(3)
            ea_high(5)
            act.wait_ge(x2_coefs, 1)
            for c in range(NC):
                for cols in (slice(0, 128), slice(160, D)):
                    act.activation(x2[:, c, cols], x1[:, c, cols], ACT.Identity, bias=x2_shift[:, c:c + 1],
                                   scale=x2_scale[:, c:c + 1]).then_inc(x2_rest, 1)
            ea_out(4)
            ea_high(6)
            ea_out(5)
            ea_high(7)
            ea_out(6)
            for c in range(NC):
                act.wait_ge(zT_ps, c + 1)
                act.activation(zT_hi[:, :, c * P:(c + 1) * P], pc[:, c, :].rearrange("p (k n) -> p k n", n=P), ACT.Copy).then_inc(zT_hi_ready, 1)
            act.wait_ge(zT_lo_ready, NC)
            for c in range(NC):
                act.activation(zT[:, :, c * P:(c + 1) * P], pc[:, c, :].rearrange("p (k n) -> p k n", n=P), ACT.Copy).then_inc(zT_ready, 1)
            ea_out(7)
            act.wait_ge(ea_lo_ready, NT // AT)
            for c in range(NC):
                act.wait_ge(xs_sum, c + 1)
                act.activation(xs_hi[:, c, :], x1[:, c, :], ACT.Copy).then_inc(xw_hi, 1)
            for c in range(NC):
                act.wait_ge(xw_ps, NC + c + 1)
                if c == 0:
                    act.wait_ge(w_lo_ready, 2)
                act.activation(xd_hi[:, c, :], pg[:, c, :], ACT.Copy).then_inc(xw_hi, 1)

            def exp(layer, t, source, u, half, ready):
                act.wait_ge(ready, u + 1)
                act.activation(t[:, half], source, ACT.Exp).then_inc(layer["exp"], 1)

            def exp1(s, half, first=False):
                if not first:
                    act.wait_ge(l1["lo"], 2 * s + half - 1)
                exp(l1, t1, l1_banks(s, half)[:, :, :], 2 * s + half, half, l1["psum"])

            def exp2(s, half, first=False):
                if not first:
                    act.wait_ge(l2["lo"], 2 * s + half - 1)
                exp(l2, t2, pre2[:, half], 2 * s + half, half, l2["pre"])

            def quotient(layer, t, u, half, final=False):
                square_here = layer is l2 and not final
                if square_here:
                    act.wait_ge(layer["cap"], u + 1)
                    act.activation(t[:, half], t[:, half], ACT.Square, bias=1.0).then_inc(layer["square"], 1)
                act.wait_ge(layer["square"], u + 1)
                act.activation(t[:, half], t[:, half], ACT.Ln, bias=1.0 if square_here else 2.0).then_inc(layer["ln"], 1)
                act.wait_ge(layer["ln"], u + 1)
                act.activation(t[:, half], t[:, half], ACT.Exp, scale=-1.0).then_inc(layer["r"], 1)

            def high1(s, parity, half, first=False):
                act.wait_ge(l1["y"], 2 * s + half + 1)
                if not first:
                    act.wait_ge(l2["psum"], 2 * s - 2)
                act.activation(h_hi[:, parity, 2 * half:2 * half + 2, :], t1[:, half], ACT.Copy).then_inc(l1["hi"], 1)

            def high2(s, half, first=False):
                act.wait_ge(l2["y"], 2 * s + half + 1)
                if not first:
                    act.wait_ge(agg_done, s)
                act.activation(m_hi[:, half], t2[:, half], ACT.Copy).then_inc(l2["hi"], 1)

            def step(s, parity, at=None):
                first = at == "first"
                exp1(s + 1, 1)
                quotient(l1, t1, 2 * s + 2, 0)
                if not first:
                    high2(s - 1, 1, at == "second")
                quotient(l1, t1, 2 * s + 3, 1)
                exp2(s, 0, first)
                high1(s + 1, 1 - parity, 0, first)
                high1(s + 1, 1 - parity, 1, first)
                quotient(l2, t2, 2 * s, 0)
                exp2(s, 1, first)
                high2(s, 0, first)
                if at != "no layer 1 after":
                    exp1(s + 2, 0)
                quotient(l2, t2, 2 * s + 1, 1)

            exp1(0, 0, True)
            quotient(l1, t1, 0, 0)
            exp1(0, 1, True)
            high1(0, 0, 0, True)
            quotient(l1, t1, 1, 1)
            high1(0, 0, 1, True)
            exp1(1, 0)
            step(0, 0, "first")
            step(1, 1, "second")
            with act.Fori(0, (NS - 6) // 2) as i:
                step(2 * i + 2, 0)
                step(2 * i + 3, 1)
            step(NS - 4, 0)
            step(NS - 3, 1)
            step(NS - 2, 0, "no layer 1 after")
            act.wait_ge(l1["psum"], 2 * NS)
            act.wait_ge(ld_w3, 16)
            act.activation(w3b_hi[:, :, :], w3_sb[:, DC:2 * DC, :], ACT.Copy).then_inc(wu_hi_ready, 1)
            high2(NS - 2, 1)
            for half in range(2):
                exp2(NS - 1, half)
            for half in range(2):
                quotient(l2, t2, 2 * NS - 2 + half, half, final=True)
            for half in range(2):
                high2(NS - 1, half)
            act.wait_ge(ld_w4, 16)
            act.activation(w4_hi[:, :, :], w4_sb[:, :, :], ACT.Copy).then_inc(wu_hi_ready, 1)

            act.wait_ge(agg_done, NS)
            for c in range(NC):
                act.activation(agg[:, c, :], pg[:, c, :], ACT.Copy, scale=-2.0).then_inc(agg_ready, 1)
            for c in range(NC):
                act.wait_ge(aggT_ps, c + 1)
                act.activation(aggT_hi[:, :, c * P:(c + 1) * P], pb[:, c, :].rearrange("p (k n) -> p k n", n=P), ACT.Copy).then_inc(aggT_hi_ready, 1)
            def fw1_high(f, parity, first=False):
                act.wait_ge(ld_fw1[parity], 8 * (f - parity) + 16)
                if not first:
                    act.wait_ge(f1_ps, f - 1)
                act.activation(fw1_hi[:, parity], fw1_raw[:, parity], ACT.Copy).then_inc(fw1_hi_ready, 1)

            def fw2_high(f, parity, first=False):
                act.wait_ge(ld_fw2[parity], 8 * (f - parity) + 16)
                if first:
                    act.wait_ge(out4_ps, NC)
                else:
                    act.wait_ge(f2_ps, f - 1)
                act.activation(fw2_hi[:, parity], fw2_raw[:, parity], ACT.Copy).then_inc(fw2_hi_ready, 1)

            for h in range(2):
                act.wait_ge(u_pre, h + 1)
                act.activation(uT[:, 2 * h:2 * h + 2, :], pre_u[:, 2 * h:2 * h + 2, :], ACT.Exp).then_inc(u_exp, 1)
                act.wait_ge(u_cap, h + 1)
                act.activation(uT[:, 2 * h:2 * h + 2, :], uT[:, 2 * h:2 * h + 2, :], ACT.Square, bias=1.0).then_inc(u_square, 1)
                act.wait_ge(u_square, h + 1)
                act.activation(uT[:, 2 * h:2 * h + 2, :], uT[:, 2 * h:2 * h + 2, :], ACT.Ln, bias=1.0).then_inc(u_ln, 1)
                act.wait_ge(u_ln, h + 1)
                act.activation(uT[:, 2 * h:2 * h + 2, :], uT[:, 2 * h:2 * h + 2, :], ACT.Exp, scale=-1.0).then_inc(u_r, 1)
            for h in range(2):
                act.wait_ge(u_ready, h + 1)
                act.activation(uT_hi[:, 2 * h:2 * h + 2, :], uT[:, 2 * h:2 * h + 2, :], ACT.Copy, scale=-2.0).then_inc(u_hi, 1)
            fw1_high(0, 0, True)
            fw1_high(1, 1, True)
            fw2_high(0, 0, True)
            for c in range(NC):
                act.wait_ge(tokT_ps, c + 1)
                act.activation(tokT_hi[:, :, c * P:(c + 1) * P], pc[:, c, :].rearrange("p (k n) -> p k n", n=P), ACT.Copy).then_inc(tokT_hi_ready, 1)
            for c in range(NC):
                act.wait_ge(neg_max, 1)
                act.activation(probs[:, c, :], logits[:, c, :], ACT.Exp, bias=small[:, 0, c:c + 1],
                               accum_out=small[:, 1, c:c + 1]).then_inc(exp_sum, 1)
            fw1_high(2, 0)
            act.wait_ge(gatesT_ps, 1)
            act.activation(gatesT[:, :], pc[0:EX, 0, 0:N], ACT.Copy).then_inc(gatesT_ready, 1)
            def gated_high(f, first=False, used=None, dest=gT_hi, source=pc):
                act.wait_ge(gT_ps, f + 1)
                if not first:
                    act.wait_ge(f2_ps, used or f)
                act.activation(dest[:, :, :], source.rearrange("p b (k n) -> p (b k) n", n=N), ACT.Copy).then_inc(gT_hi_ready, 1)

            def step(f, parity, fw1_more=True, fw2_more=True, first=False):
                gated_high(f, first)
                if fw1_more:
                    fw1_high(f + 3, 1 - parity)
                if fw2_more:
                    fw2_high(f + 1, 1 - parity, first)

            step(0, 0, first=True)
            with act.Fori(0, (FS - 4) // 2) as i:
                step(2 * i + 1, 1)
                step(2 * i + 2, 0)
            step(FS - 3, 1, fw1_more=False)
            gated_high(FS - 2, first=True, dest=gT2_hi, source=pb)
            fw2_high(FS - 1, 1)
            gated_high(FS - 1, used=FS - 2)

        @block.tensor
        def _(pe):
            def transposed(dest, source, rows_in):
                return pe.transpose(dest, source, ident[0:rows_in, 0:rows_in])

            pe.wait_ge(consts, 1)
            pe.wait_ge(idx_f_ready, 1)
            for k in range(2):
                last = transposed(pc[:, 0, k * NT:(k + 1) * NT], idx_f[:, k, :], NT)
            last.then_inc(idxT_ps, 1)

            def ea_transposes(e):
                pe.wait_ge(ea_lo_ready, e + 1)
                for g in range(2):
                    n = 2 * e + g
                    if n >= 2:
                        pe.wait_ge(eaT_ready, n - 1)
                    for j in range(4):
                        last = transposed(pb[:, n % 2, j * P:(j + 1) * P],
                                          ea_hl[:, e % 2, 4 * g + j, :, :].rearrange("p h a -> p (h a)").bitcast(F32), P)
                    last.then_inc(eaT_ps, 1)

            def count(c, parity, start, stop):
                for t in range(CT):
                    if t % (CT // 2) == 0:
                        pe.wait_ge(onehots, 2 * c + t // (CT // 2) + 1)
                    for k in range(NC):
                        last = pe.matmul(pa[:, k, 0:N], oh_s[:, parity, t, k * P:(k + 1) * P], oh_d[:, parity, t, :],
                                         start=start and t == 0, stop=stop and t == CT - 1)
                last.then_inc(counted, 1)

            def x_times_w0(n, ks):
                for k in ks:
                    last = pe.matmul(pc[:, n, :], xnT[:, k, n * P:(n + 1) * P], w0_sb[:, k, :],
                                     start=k == 0, stop=k == DC - 1)
                if k == DC - 1:
                    last.then_inc(y0_ps, 1)

            NCH = NT // CT
            for c in range(NCH):
                count(c, c % 2, c == 0, c == NCH - 1)
                if c in (1, 2):
                    ea_transposes(c - 1)
                elif c == 3:
                    pe.wait_ge(xn_ready, NC)
                    for n in range(NC):
                        for k in range(DC):
                            last = transposed(pg.rearrange("p b (k n) -> p (b k) n", n=N)[:, k, n * P:(n + 1) * P],
                                              xn[:, n, k * P:(k + 1) * P], P)
                    last.then_inc(xnT_ps, 1)
                elif c == 4:
                    pe.wait_ge(xnT_ready, 1)
                    pe.wait_ge(ld_w0, 16)
                    x_times_w0(0, range(2))
                elif c == 5:
                    x_times_w0(0, range(2, DC))

            pe.wait_ge(counts_ready, 1)
            for k in range(NC):
                for j in range(NC):
                    last = transposed(pg[:, 0, k * N + j * P:k * N + (j + 1) * P], counts[:, j, k * P:(k + 1) * P], P)
            last.then_inc(countsT_ps, 1)
            x_times_w0(1, range(DC))

            pe.wait_ge(adj_ready, 1)
            for k in range(NC):
                pe.wait_ge(y0_lo_ready, k + 1)
                for n in range(NC):
                    for part in (y0_hi, y0_lo):
                        last = pe.matmul(pa[:, n, :], adj[:, k, n * P:(n + 1) * P], part[:, k, :],
                                         start=k == 0 and part is y0_hi, stop=k == NC - 1 and part is y0_lo)
            last.then_inc(conv_ps, 1)
            for e in range(2, NT // AT - 1):
                ea_transposes(e)

            for n in range(NC):
                pe.wait_ge(z_ready, n + 1)
                for k in range(DC):
                    last = transposed(pc[:, n, k * P:(k + 1) * P], z[:, n, k * P:(k + 1) * P], P)
                last.then_inc(zT_ps, 1)
            ea_transposes(NT // AT - 1)
            for g, dest in enumerate((pa, pg)):
                pe.wait_ge(w1_lo_ready, g + 1)
                for n in range(NC):
                    if g == 0:
                        pe.wait_ge(zT_lo_ready, n + 1)
                    at = slice(n * P, (n + 1) * P)
                    for k in range(DC):
                        for a, b in ((zT_hi, w1_hi), (zT_hi, w1_lo), (zT_lo, w1_hi)):
                            last = pe.matmul(dest[:, n, :], a[:, k, at], b[:, g, k, :],
                                             start=k == 0 and a is zT_hi and b is w1_hi, stop=k == DC - 1 and a is zT_lo)
                    last.then_inc(xw_ps, 1)

            def layer1(s, parity, half, first=False, at_once=False):
                if half == 0:
                    pe.wait_ge(ohT_ready, s + 1)
                if isinstance(s, int) and s == 1:
                    pe.wait_ge(*((xw_lo, 2 * NC), (l1["y"], 1))[half])
                elif isinstance(s, int) and s == 2:
                    pe.wait_ge(l1["y"], (2, 4)[half])
                elif not first:
                    pe.wait_ge(l1["y"], 2 * s + half - 1)
                both_parts = eaT[:, bass.ts(s, SE)]
                high_part = eaT[0:EA, bass.ts(s, SE)]
                for j in range(2):
                    c = 2 * half + j
                    cols = slice(c * P, (c + 1) * P)
                    dest = l1_banks(s, half)[:, j, :]
                    for n, (part, which, k) in enumerate((part, which, k) for which, parts in enumerate(((xs_hi, xs_lo), (xd_hi, xd_lo)))
                                                         for k in range(NC) for part in parts):
                        if at_once and j == 0 and part in (xs_hi, xd_hi):
                            pe.wait_ge(xw_lo, NC * which + k + 1)
                        pe.matmul(dest, part[:, k, cols], ohT[:, parity, which, k, :], start=n == 0, stop=False)
                    pe.matmul(dest, w1c_hi[:, cols], both_parts, start=False, stop=False)
                    last = pe.matmul(dest, w1c_lo[:, cols], high_part, start=False, stop=True)
                last.then_inc(l1["psum"], 1)

            def layer2(s, parity, half, first=False, final=False):
                pe.wait_ge(l1["lo"], 2 * s + 2)
                if final:
                    pe.wait_ge(l1["y"], 2 * NS)
                elif first and half == 1:
                    pe.wait_ge(l1["y"], 3)
                elif not first:
                    pe.wait_ge(l2["pre"], 2 * s + half)
                dest = l2_banks(s, half, final)
                for j in range(2):
                    at = slice((2 * half + j) * P, (2 * half + j + 1) * P)
                    n = 0
                    for k in range(DC):
                        for a, b in ((h_hi, w2_hi), (h_hi, w2_lo), (h_lo, w2_hi)):
                            last = pe.matmul(dest[:, j, :], a[:, parity, k, at], b[:, k, :], start=n == 0, stop=n == 3 * DC - 1)
                            n += 1
                last.then_inc(l2["psum"], 1)

            def sum_messages(s, parity, first=False, final=False):
                pe.wait_ge(ohd_ready, s + 1)
                for half in range(2):
                    pe.wait_ge(l2["lo"], 2 * s + half + 1)
                    for j in range(2):
                        for n in range(NC):
                            for part in (m_hi, m_lo):
                                last = pe.matmul(pg[:, n, :], ohd[:, parity, 2 * half + j, n * P:(n + 1) * P], part[:, half, j, :],
                                                 start=first and half == 0 and j == 0 and part is m_hi,
                                                 stop=final and half == 1 and j == 1 and part is m_lo)
                last.then_inc(agg_done, 1)

            def step(s, parity, more=True, first=False, second=False):
                layer2(s, parity, 0, first)
                if not first and not second:
                    sum_messages(s - 1, 1 - parity)
                layer2(s, parity, 1, first)
                if second:
                    sum_messages(s - 1, 1 - parity, first=True)
                if more:
                    if not first:
                        layer1(s + 2, parity, 0)
                    layer1(s + 2, parity, 1)

            pe.wait_ge(w_lo_ready, 1)
            pe.wait_ge(eaT_ready, NT // 4)
            layer1(0, 0, 0, True, at_once=True)
            layer1(0, 0, 1, True)
            layer1(1, 1, 0)
            layer1(1, 1, 1)
            layer1(2, 0, 0)
            pe.wait_ge(w_lo_ready, 2)
            step(0, 0, first=True)
            step(1, 1, second=True)
            with pe.Fori(0, (NS - 6) // 2) as i:
                step(2 * i + 2, 0)
                step(2 * i + 3, 1)
            step(NS - 4, 0)
            step(NS - 3, 1)
            step(NS - 2, 0, more=False)
            layer2(NS - 1, 1, 0, final=True)
            layer2(NS - 1, 1, 1, final=True)

            uT_ps = pc.rearrange("p b (k n) -> p (b k) n", n=N)

            def update_of_z(c):
                for k in range(DC):
                    pe.matmul(uT_ps[:, c, :], w3_sb[:, k, c * P:(c + 1) * P], zT[:, k, :],
                              start=k == 0 and c % 2 == 0, stop=False)

            pe.wait_ge(ld_w3, 16)
            pe.wait_ge(zT_ready, NC)
            pe.wait_ge(l2["pre"], 2 * NS - 2)
            update_of_z(0)
            update_of_z(1)
            sum_messages(NS - 2, 0)
            update_of_z(2)
            update_of_z(3)

            pe.wait_ge(ld_b3, 16)
            pe.wait_ge(l2["pre"], 2 * NS)
            transposed(pa[:, 0, 0:DC], b3_nat[:, :], DC).then_inc(b3T_ps, 1)
            sum_messages(NS - 1, 1, final=True)
            for n in range(NC):
                pe.wait_ge(agg_ready, n + 1)
                for k in range(DC):
                    last = transposed(pb[:, n, k * P:(k + 1) * P], agg[:, n, k * P:(k + 1) * P], P)
                last.then_inc(aggT_ps, 1)
            pe.wait_ge(wu_lo_ready, 1)
            pe.wait_ge(aggT_lo_ready, NC)
            for c in range(DC):
                for k in range(DC):
                    for a, b in ((w3b_hi, aggT_hi), (w3b_lo, aggT_hi), (w3b_hi, aggT_lo)):
                        last = pe.matmul(uT_ps[:, c, :], a[:, k, c * P:(c + 1) * P], b[:, k, :], start=False,
                                         stop=k == DC - 1 and b is aggT_lo and c % 2 == 1)
                last.then_inc(u_ps, 1)
            pe.wait_ge(residual, NC)
            pe.wait_ge(agg_ready, NC)
            for n in range(NC):
                pe.matmul(pg[:, n, :], ident[:, :], y4[:, n, :], start=True, stop=False)
            pe.wait_ge(wu_lo_ready, 2)
            for n in range(NC):
                for k in range(DC):
                    if n == 0 and k % 2 == 0:
                        pe.wait_ge(u_lo, k // 2 + 1)
                    for a, b in ((uT_hi, w4_hi), (uT_hi, w4_lo), (uT_lo, w4_hi)):
                        last = pe.matmul(pg[:, n, :], a[:, k, n * P:(n + 1) * P], b[:, k, :],
                                         start=False, stop=k == DC - 1 and a is uT_lo)
                last.then_inc(out4_ps, 1)

            for n in range(NC):
                pe.wait_ge(tok_ready, n + 1)
                for k in range(DC):
                    last = transposed(pc[:, n, k * P:(k + 1) * P], tok[:, n, k::DC], P)
                last.then_inc(tokT_ps, 1)
            pe.wait_ge(ld_wg, 32)
            for n in range(NC):
                pe.wait_ge(tokT_ready, n + 1)
                for k in range(DC):
                    last = pe.matmul(pa[:, n, 0:EX], tokT[:, k, n * P:(n + 1) * P], wg_sb[:, k, :], start=k == 0, stop=k == DC - 1)
            last.then_inc(logits_ps, 1)

            def hidden(f, parity):
                pe.wait_ge(fw1_lo_ready, f + 1)
                dest = (pb, pa)[parity]
                for n in range(NC):
                    at = slice(n * P, (n + 1) * P)
                    for k in range(DC):
                        for a, b in ((tokT_hi, fw1_hi), (tokT_hi, fw1_lo), (tokT_lo, fw1_hi)):
                            last = pe.matmul(dest[:, n, :], a[:, k, at], b[:, parity, :, k, :],
                                             start=k == 0 and a is tokT_hi and b is fw1_hi, stop=k == DC - 1 and a is tokT_lo)
                last.then_inc(f1_ps, 1)

            def gated_transposes(f, first=False, dest=pc, left=None):
                pe.wait_ge(f1_g, 2 * f + 2)
                if not first:
                    pe.wait_ge(gT_ready, left or f)
                view = dest.rearrange("p b (k n) -> p (b k) n", n=N)
                for n in range(NC):
                    for k in range(HC // P):
                        last = transposed(view[:, k, n * P:(n + 1) * P], g_sb[:, n, k * P:(k + 1) * P], P)
                last.then_inc(gT_ps, 1)

            def expert_out(f, parity, final=False, parts=(gT_hi, gT_lo)):
                pe.wait_ge(gT_ready, f + 1)
                pe.wait_ge(fw2_lo_ready, f + 1)
                for n in range(NC):
                    at = slice(n * P, (n + 1) * P)
                    hi, lo = parts
                    for k in range(HC // P):
                        for a, b in ((hi, fw2_hi), (hi, fw2_lo), (lo, fw2_hi)):
                            last = pe.matmul(pg[:, n, :], a[:, k, at], b[:, parity, k, :],
                                             start=False, stop=final and k == HC // P - 1 and a is lo)
                    if final:
                        last.then_inc(f2_chunk, 1)
                if not final:
                    last.then_inc(f2_ps, 1)

            pe.wait_ge(tokT_lo_ready, NC)
            hidden(0, 0)
            pe.wait_ge(gates_ready, 1)
            for n in range(NC):
                last = transposed(pc[0:EX, 0, n * P:(n + 1) * P], gates[:, n, :], P)
            last.then_inc(gatesT_ps, 1)
            pe.wait_ge(neg_max, 1)
            hidden(1, 1)
            pe.wait_ge(gatesT_ready, 1)
            pe.wait_ge(ld_fb2, 16)
            for n in range(NC):
                pe.matmul(pg[:, n, :], gatesT[:, n * P:(n + 1) * P], fb2_sb[:, :], start=True, stop=False)

            def step(f, parity, more=True, first=False, final=False):
                gated_transposes(f, first)
                if more:
                    hidden(f + 2, parity)
                expert_out(f, parity, final)

            step(0, 0, first=True)
            with pe.Fori(0, (FS - 4) // 2) as i:
                step(2 * i + 1, 1)
                step(2 * i + 2, 0)
            gated_transposes(FS - 3)
            hidden(FS - 1, 1)
            gated_transposes(FS - 2, first=True, dest=pb)
            expert_out(FS - 3, 1)
            gated_transposes(FS - 1, left=FS - 2)
            expert_out(FS - 2, 0, parts=(gT2_hi, gT2_lo))
            expert_out(FS - 1, 1, final=True)

        @block.vector
        def _(dve):
            linked = [0]

            def link(ins):
                linked[0] += 1
                ins.then_inc(dve_link, 1)
                dve.wait_ge(dve_link, linked[0])

            def layer_norm_moments(t, which):
                for c in range(NC):
                    last = dve.bn_stats(stats[:, which, c, :], t[:, c, :])
                link(last)
                for c in range(NC):
                    last = dve.bn_aggr(moments[:, which, c, :], stats[:, which, c, :])
                link(last)
                dve.tensor_scalar(var_eps[:, which % 5, :], moments[:, which, :, 1], EPS, None, ALU.add).then_inc(var_ready, 1)

            dve.wait_ge(ld_idx, 32)
            dve.tensor_copy(idx_f[:, :, :], idx_i[:, :, :]).then_inc(idx_f_ready, 1)
            dve.wait_ge(consts, 5)
            dve.tensor_copy(iota_row[:, :], iota_i[:, :])
            dve.tensor_copy(iota_bf[:, :], iota_i[:, :])
            dve.tensor_copy(node_id[:, :], node_i[:, :])
            link(dve.tensor_copy(ramp[:, :, :, :], ramp_i[:, :, :, :]))
            dve.wait_ge(idxT_ps, 1)
            link(dve.tensor_copy(idx_cols[:, :, :], pc[:, 0, 0:2 * NT].rearrange("p (k t) -> p k t", k=2)))

            def onehots_of(c, parity, first=False):
                if not first:
                    dve.wait_ge(counted, c - 1)
                for t in range(CT):
                    for dest, k in ((oh_s, 0), (oh_d, 1)):
                        at = c * CT + t
                        last = dve.tensor_scalar(dest[:, parity, t, :], iota_bf[:, :], idx_cols[:, k, bass.ds(at, 1)], None, ALU.is_equal)
                    if t % (CT // 2) == CT // 2 - 1:
                        last.then_inc(onehots, 1)

            def onehot_pair(i):
                onehots_of(2 * i, 0)
                onehots_of(2 * i + 1, 1)

            onehots_of(0, 0, True)
            onehots_of(1, 1, True)
            dve.wait_ge(ld_x, 16)
            layer_norm_moments(xin, 0)
            onehot_pair(1)
            dve.wait_ge(rstd_ready, 1)
            dve.scalar_tensor_tensor(out=xn_shift[:, :], in0=moments[:, 0, :, 0], scalar=-1.0, in1=rstd[:, 0, :],
                                     op0=ALU.mult, op1=ALU.mult).then_inc(xn_coefs, 1)
            with dve.Fori(2, NT // CT // 2) as i:
                onehot_pair(i)

            dve.wait_ge(counted, NT // CT)
            dve.tensor_copy(counts[:, :, :], pa[:, :, 0:N]).then_inc(counts_ready, 1)
            dve.wait_ge(counts_ready, 1)
            dve.wait_ge(countsT_ps, 1)
            link(dve.tensor_tensor(counts[:, :, :], pg[:, 0, :].rearrange("p (k n) -> p k n", n=N), counts[:, :, :], ALU.add))
            dve.wait_ge(consts, 7)
            dve.scalar_tensor_tensor(out=adj[:, :, :], in0=counts[:, :, :], scalar=1.0, in1=eye[:, :, :],
                                     op0=ALU.min, op1=ALU.add).then_inc(adj_ready, 1)
            dve.wait_ge(adj_ready, 1)
            dve.tensor_reduce(deg[:, :], adj[:, :, :].bitcast(F32), AX.X, ALU.add).then_inc(deg_ready, 1)
            dve.wait_ge(ld_b0, 16)
            for c in range(NC):
                last = dve.tensor_tensor(x1[:, c, :], xin[:, c, :], b0_rows[:, :], ALU.add)
            for c in range(NC):
                dve.wait_ge(y0_hi_ready, c + 1)
                dve.scalar_tensor_tensor(out=y0_lo[:, c, :], in0=pc[:, c, :], scalar=dinv[:, c:c + 1],
                                         in1=y0_hi[:, c, :].bitcast(F32), op0=ALU.mult, op1=ALU.subtract).then_inc(y0_lo_ready, 1)

            def node_onehots(s, parity, first=False):
                dve.wait_ge(ld_rows[parity], 16 * (s - parity) + 32)
                if not first:
                    dve.wait_ge(l1["psum"], 2 * s - 2)
                for which in range(2):
                    for k in range(NC):
                        last = dve.tensor_scalar(ohT[:, parity, which, k, :], idx_rows[:, parity, which, :], node_id[:, k:k + 1], None, ALU.is_equal)
                last.then_inc(ohT_ready, 1)

            def dst_onehots(s, parity, first=False):
                if not first:
                    dve.wait_ge(agg_done, s - 1)
                for t in range(TPS):
                    last = dve.tensor_scalar(ohd[:, parity, t, :], iota_row[:, :], idx_cols[:, 1, bass.ds(s * TPS + t, 1)], None, ALU.is_equal)
                last.then_inc(ohd_ready, 1)

            node_onehots(0, 0, True)
            dve.wait_ge(conv_ps, 1)
            for c in range(NC):
                last = dve.scalar_tensor_tensor(out=x1[:, c, :], in0=pa[:, c, :], scalar=dinv[:, c:c + 1], in1=x1[:, c, :],
                                                op0=ALU.mult, op1=ALU.add)
            link(last)

            layer_norm_moments(x1, 1)
            dve.wait_ge(rstd_ready, 2)
            for c in range(NC):
                last = dve.tensor_scalar(y1[:, c, 0:160], x1[:, c, 0:160], moments[:, 1, c, 0:1], rstd[:, 1, c:c + 1],
                                         ALU.subtract, ALU.mult)
            dve.tensor_scalar(x2_scale[:, :], rstd[:, 1, :], 1.0, None, ALU.add)
            dve.scalar_tensor_tensor(out=x2_shift[:, :], in0=moments[:, 1, :, 0], scalar=-1.0, in1=rstd[:, 1, :],
                                     op0=ALU.mult, op1=ALU.mult).then_inc(x2_coefs, 1)
            dve.wait_ge(x2_coefs, 1)
            is_shl, do_shl, do_shr, marked_shr, active = (flags[:, f, :] for f in range(5))
            keep_shl, keep_shr, inactive = (masks[:, f, :] for f in range(3))
            value, left, right = (words[:, f, :] for f in range(3))
            dve.scalar_tensor_tensor(out=ranked[:, :, :, :], in0=y1[:, :, 64:112].rearrange("p c (f w) -> p c f w", f=3), scalar=HOT,
                                     in1=ramp[:, :, :, :], op0=ALU.is_gt, op1=ALU.mult)
            dve.tensor_scalar(is_shl, y1[:, :, 39], HOT, None, ALU.is_gt)
            dve.tensor_scalar(marked_shr, y1[:, :, 40], HOT, None, ALU.is_gt)
            link(dve.tensor_scalar(active, y1[:, :, 0], HOT, None, ALU.is_gt))
            dve.tensor_reduce(rank[:, :, :], ranked[:, :, :, :], AX.X, ALU.max)
            dve.tensor_tensor(do_shl, is_shl, active, ALU.mult)
            link(dve.tensor_tensor(marked_shr, marked_shr, active, ALU.mult))
            dve.tensor_scalar(code[:, :, :], rank[:, :, :], -1.0, 16.0, ALU.mult, ALU.add)
            link(dve.tensor_tensor(do_shr, marked_shr, is_shl, ALU.is_gt))
            dve.tensor_scalar(code[:, :, :], code[:, :, :], 15, None, ALU.bitwise_and)
            dve.tensor_scalar(keep_shl, do_shl, 255.0, None, ALU.mult)
            dve.tensor_scalar(keep_shr, do_shr, 255.0, None, ALU.mult)
            link(dve.tensor_tensor(active, do_shl, do_shr, ALU.add))
            dve.scalar_tensor_tensor(out=value, in0=code[:, :, 1], scalar=16.0, in1=code[:, :, 0], op0=ALU.mult, op1=ALU.add)
            link(dve.tensor_scalar(inactive, active, -4096.0, 4096.0, ALU.mult, ALU.add))
            dve.tensor_tensor(left, value, code[:, :, 2], ALU.logical_shift_left)
            link(dve.tensor_tensor(right, value, code[:, :, 2], ALU.logical_shift_right))
            dve.tensor_tensor(left, left, keep_shl, ALU.bitwise_and)
            dve.tensor_tensor(right, right, keep_shr, ALU.bitwise_and)
            link(dve.tensor_tensor(x2[:, :, 128:160], x1[:, :, 128:160], y1[:, :, 128:160], ALU.add))
            link(dve.tensor_tensor(left, left, right, ALU.bitwise_or))
            link(dve.tensor_tensor(left, left, inactive, ALU.bitwise_or))
            dve.tensor_scalar(digits[:, :, 0], left, 15 + 4096, None, ALU.bitwise_and)
            link(dve.tensor_scalar(digits[:, :, 1], left, 4, None, ALU.logical_shift_right))
            link(dve.tensor_tensor(hit[:, :, :, :], digits[:, :, :].unsqueeze(3).broadcast_to((P, NC, 2, 16)),
                                   iota_i[:, 0:16].unsqueeze(1).unsqueeze(1).broadcast_to((P, NC, 2, 16)), ALU.is_equal))
            dve.wait_ge(x2_rest, 2 * NC)
            link(dve.scalar_tensor_tensor(out=x2[:, :, 128:160], in0=hit[:, :, :, :].rearrange("p c f w -> p c (f w)"), scalar=2.0,
                                          in1=x2[:, :, 128:160], op0=ALU.mult, op1=ALU.add))

            layer_norm_moments(x2, 2)
            dve.wait_ge(rstd_ready, 3)
            for c in range(NC):
                dve.tensor_scalar(z[:, c, :], x2[:, c, :], moments[:, 2, c, 0:1], rstd[:, 2, c:c + 1],
                                  ALU.subtract, ALU.mult).then_inc(z_ready, 1)
            for c in range(NC):
                dve.wait_ge(zT_hi_ready, c + 1)
                dve.tensor_tensor(zT_lo[:, :, c * P:(c + 1) * P], pc[:, c, :].rearrange("p (k n) -> p k n", n=P),
                                  zT_hi[:, :, c * P:(c + 1) * P].bitcast(F32), ALU.subtract).then_inc(zT_lo_ready, 1)
            node_onehots(1, 1, True)
            dve.wait_ge(ld_b1, 16)
            for c in range(NC):
                dve.wait_ge(xw_ps, c + 1)
                dve.tensor_tensor(x1[:, c, :], pa[:, c, :], b1_rows[:, :], ALU.add).then_inc(xs_sum, 1)
            for c in range(NC):
                dve.wait_ge(xw_hi, c + 1)
                dve.tensor_tensor(xs_lo[:, c, :], x1[:, c, :], xs_hi[:, c, :].bitcast(F32), ALU.subtract).then_inc(xw_lo, 1)
            for c in range(NC):
                dve.wait_ge(xw_hi, NC + c + 1)
                dve.tensor_tensor(xd_lo[:, c, :], pg[:, c, :], xd_hi[:, c, :].bitcast(F32), ALU.subtract).then_inc(xw_lo, 1)

            def cap(layer, t, u, half, final=False):
                dve.wait_ge(layer["exp"], u + 1)
                dve.tensor_scalar(t[:, half], t[:, half], EXP_CAP, None, ALU.min).then_inc(layer["cap"], 1)
                if layer is l1 or final:
                    dve.wait_ge(layer["cap"], u + 1)
                    dve.scalar_tensor_tensor(out=t[:, half], in0=t[:, half], scalar=2.0, in1=t[:, half],
                                             op0=ALU.add, op1=ALU.mult).then_inc(layer["square"], 1)

            def finish(layer, t, pre, u, half):
                dve.wait_ge(layer["r"], u + 1)
                dve.scalar_tensor_tensor(out=t[:, half], in0=t[:, half], scalar=0.5, in1=pre,
                                         op0=ALU.subtract, op1=ALU.mult).then_inc(layer["y"], 1)

            def cap1(s, half):
                cap(l1, t1, 2 * s + half, half)

            def cap2(s, half, final=False):
                cap(l2, t2, 2 * s + half, half, final)

            def finish1(s, half):
                finish(l1, t1, l1_banks(s, half)[:, :, :], 2 * s + half, half)

            def finish2(s, half):
                finish(l2, t2, pre2[:, half], 2 * s + half, half)

            def low2(s, half):
                dve.wait_ge(l2["hi"], 2 * s + half + 1)
                dve.tensor_tensor(m_lo[:, half], t2[:, half], m_hi[:, half].bitcast(F32), ALU.subtract).then_inc(l2["lo"], 1)

            def with_bias(s, half, first=False, final=False):
                dve.wait_ge(l2["psum"], 2 * s + half + 1)
                if not first:
                    dve.wait_ge(l2["y"], 2 * s + half - 1)
                source = l2_banks(s, half, final)
                for j in range(2):
                    last = dve.tensor_tensor(pre2[:, half, j, :], source[:, j, :], b2_rows[:, :], ALU.add)
                last.then_inc(l2["pre"], 1)

            def step(s, parity, at=None):
                first = at == "first"
                if at == "second":
                    with_bias(s, 0)
                cap1(s + 1, 1)
                finish1(s + 1, 0)
                if not first:
                    low2(s - 1, 1)
                if at != "second":
                    with_bias(s, 0, first)
                finish1(s + 1, 1)
                cap2(s, 0)
                if at not in ("first", "no layer 1 after"):
                    node_onehots(s + 2, parity)
                if at in ("first", "second"):
                    with_bias(s, 1, first)
                finish2(s, 0)
                if at not in ("first", "second"):
                    with_bias(s, 1)
                dst_onehots(s, parity, at in ("first", "second"))
                cap2(s, 1)
                low2(s, 0)
                if at != "no layer 1 after":
                    cap1(s + 2, 0)
                finish2(s, 1)

            dve.wait_ge(ld_b2, 16)
            cap1(0, 0)
            finish1(0, 0)
            cap1(0, 1)
            node_onehots(2, 0)
            finish1(0, 1)
            cap1(1, 0)
            step(0, 0, "first")
            step(1, 1, "second")
            with dve.Fori(0, (NS - 6) // 2) as i:
                step(2 * i + 2, 0)
                step(2 * i + 3, 1)
            step(NS - 4, 0)
            step(NS - 3, 1)
            step(NS - 2, 0, "no layer 1 after")
            with_bias(NS - 1, 0, final=True)
            low2(NS - 2, 1)
            with_bias(NS - 1, 1, final=True)
            cap2(NS - 1, 0, final=True)
            cap2(NS - 1, 1, final=True)
            dst_onehots(NS - 1, 1)
            finish2(NS - 1, 0)
            finish2(NS - 1, 1)
            low2(NS - 1, 0)
            low2(NS - 1, 1)

            def fw1_low(f, parity):
                dve.wait_ge(fw1_hi_ready, f + 1)
                dve.tensor_tensor(fw1_lo[:, parity], fw1_raw[:, parity], fw1_hi[:, parity].bitcast(F32), ALU.subtract).then_inc(fw1_lo_ready, 1)

            def fw2_low(f, parity):
                dve.wait_ge(fw2_hi_ready, f + 1)
                dve.tensor_tensor(fw2_lo[:, parity], fw2_raw[:, parity], fw2_hi[:, parity].bitcast(F32), ALU.subtract).then_inc(fw2_lo_ready, 1)

            dve.wait_ge(b3T_ps, 1)
            dve.tensor_copy(b3_cols[:, :], pa[:, 0, 0:DC]).then_inc(b3_ready, 1)
            dve.wait_ge(ld_b4, 16)
            for c in range(NC):
                dve.tensor_tensor(y4[:, c, :], z[:, c, :], b4_rows[:, :], ALU.add).then_inc(residual, 1)
            for c in range(NC):
                dve.wait_ge(aggT_hi_ready, c + 1)
                dve.tensor_tensor(aggT_lo[:, :, c * P:(c + 1) * P], pb[:, c, :].rearrange("p (k n) -> p k n", n=P),
                                  aggT_hi[:, :, c * P:(c + 1) * P].bitcast(F32), ALU.subtract).then_inc(aggT_lo_ready, 1)
            dve.wait_ge(b3_ready, 1)
            half = lambda t, h: t[:, 2 * h:2 * h + 2, :]
            for h in range(2):
                dve.wait_ge(u_ps, 2 * h + 2)
                for c in range(2 * h, 2 * h + 2):
                    last = dve.tensor_scalar(pre_u[:, c, :], pc[:, c // 2, c % 2 * N:(c % 2 + 1) * N], b3_cols[:, c:c + 1], None, ALU.add)
                last.then_inc(u_pre, 1)
                dve.wait_ge(u_exp, h + 1)
                dve.tensor_scalar(half(uT, h), half(uT, h), EXP_CAP, None, ALU.min).then_inc(u_cap, 1)
            for h in range(2):
                dve.wait_ge(u_r, h + 1)
                dve.scalar_tensor_tensor(out=half(uT, h), in0=half(uT, h), scalar=0.5, in1=half(pre_u, h),
                                         op0=ALU.subtract, op1=ALU.mult).then_inc(u_ready, 1)
            for h in range(2):
                dve.wait_ge(u_hi, h + 1)
                dve.scalar_tensor_tensor(out=half(uT_lo, h), in0=half(uT, h), scalar=-2.0, in1=half(uT_hi, h).bitcast(F32),
                                         op0=ALU.mult, op1=ALU.subtract).then_inc(u_lo, 1)
            dve.wait_ge(ld_affine, 64)
            for c in range(NC):
                last = dve.tensor_tensor(x2[:, c, :], x2[:, c, :], beta1_rows[:, :], ALU.add)
            fw1_low(0, 0)

            def centred(t, which, c, gain, dest=None):
                link(dve.bn_stats(stats[:, which, c, :], t[:, c, :]))
                link(dve.bn_aggr(moments[:, which, c, :], stats[:, which, c, :]))
                dve.tensor_scalar(var_eps[:, which, c:c + 1], moments[:, which, c, 1:2], EPS, None, ALU.add).then_inc(chunk_var, 1)
                if gain is not None:
                    link(dve.scalar_tensor_tensor(out=(dest or t)[:, c, :], in0=t[:, c, :], scalar=moments[:, which, c, 0:1], in1=gain[:, :],
                                                  op0=ALU.subtract, op1=ALU.mult))

            def scaled(dest, t, which, c, base, count):
                dve.wait_ge(chunk_rstd, count)
                return dve.scalar_tensor_tensor(out=dest[:, c, :], in0=t[:, c, :], scalar=rstd[:, which, c:c + 1], in1=base[:, c, :],
                                                op0=ALU.mult, op1=ALU.add)

            for c in range(NC):
                dve.wait_ge(out4_ps, c + 1)
                centred(pg, 3, c, gamma1_rows, y4)
                if c == 0:
                    link(scaled(x3, y4, 3, c, x2, c + 1))
            centred(x3, 4, 0, None)
            link(scaled(x3, y4, 3, 1, x2, 2))
            centred(x3, 4, 1, None)
            for c in range(NC):
                dve.wait_ge(chunk_rstd, NC + c + 1)
                dve.tensor_scalar(tok[:, c, :], x3[:, c, :], moments[:, 4, c, 0:1], rstd[:, 4, c:c + 1],
                                  ALU.subtract, ALU.mult).then_inc(tok_ready, 1)
            for c in range(NC):
                dve.wait_ge(tokT_hi_ready, c + 1)
                chunk = pc[:, c, :].rearrange("p (k n) -> p k n", n=P)
                dve.tensor_copy(tokT[:, :, c * P:(c + 1) * P], chunk).then_inc(tokT_ready, 1)
                dve.tensor_tensor(tokT_lo[:, :, c * P:(c + 1) * P], chunk, tokT_hi[:, :, c * P:(c + 1) * P].bitcast(F32),
                                  ALU.subtract).then_inc(tokT_lo_ready, 1)

            fw1_low(1, 1)

            dve.wait_ge(logits_ps, 1)
            for c in range(NC):
                last = dve.tensor_tensor(logits[:, c, :], pa[:, c, 0:EX], bg_rows[:, :], ALU.add)
            link(last)
            link(dve.tensor_reduce(small[:, 2, :], logits[:, :, :], AX.X, ALU.max))
            dve.tensor_scalar(small[:, 0, :], small[:, 2, :], -1.0, None, ALU.mult).then_inc(neg_max, 1)
            dve.wait_ge(exp_sum, 2)
            link(dve.reciprocal(small[:, 3, :], small[:, 1, :]))
            for c in range(NC):
                last = dve.tensor_scalar(probs[:, c, :], probs[:, c, :], small[:, 3, c:c + 1], None, ALU.mult)
            link(last)
            for c in range(NC):
                last = dve.max(top[:, c, :], probs[:, c, :])
            link(last)
            for c in range(NC):
                last = dve.max_index(top_at[:, c, :], top[:, c, :], probs[:, c, :])
            link(last)
            link(dve.tensor_copy(top_atf[:, :, :], top_at[:, :, :]))
            for c in range(NC):
                last = dve.tensor_scalar(chosen[:, c, :], iota_row[:, 0:EX], top_atf[:, c, 0:1], None, ALU.is_equal)
            link(last)
            for c in range(NC):
                last = dve.scalar_tensor_tensor(out=chosen[:, c, :], in0=iota_row[:, 0:EX], scalar=top_atf[:, c, 1:2],
                                                in1=chosen[:, c, :], op0=ALU.is_equal, op1=ALU.add)
            link(last)
            dve.tensor_tensor(gates[:, :, :], probs[:, :, :], chosen[:, :, :], ALU.mult).then_inc(gates_ready, 1)
            dve.wait_ge(gates_ready, 1)

            def gated(f, parity, first=False):
                dve.wait_ge(f1_ps, f + 1)
                dve.wait_ge(ld_fb1[parity], 8 * (f - parity) + 16)
                if not first:
                    dve.wait_ge(gT_ps, f)
                for c in range(NC):
                    dve.tensor_tensor(g_sb[:, c, :], (pb, pa)[parity][:, c, :], fb1_rows[:, bass.ts(f, HC)], ALU.add).then_inc(f1_sum, 1)
                for c in range(NC):
                    dve.wait_ge(f1_sum, 2 * f + c + 1)
                    gate = gates[:, c, bass.ts(f, XS)].unsqueeze(2).broadcast_to((P, XS, EH))
                    by_expert = g_sb[:, c, :].rearrange("p (e h) -> p e h", h=EH)
                    dve.scalar_tensor_tensor(out=by_expert, in0=by_expert, scalar=0.0, in1=gate,
                                             op0=ALU.max, op1=ALU.mult).then_inc(f1_g, 1)

            def gated_low(f, parts=(gT_hi, gT_lo), source=pc):
                hi, lo = parts
                dve.wait_ge(gT_hi_ready, f + 1)
                dve.tensor_tensor(lo[:, :, :], source.rearrange("p b (k n) -> p (b k) n", n=N), hi[:, :, :].bitcast(F32),
                                  ALU.subtract).then_inc(gT_ready, 1)

            def step(f, parity, fw1_more=True, fw2_more=True, last=False):
                gated_low(f)
                if not last:
                    gated(f + 1, 1 - parity)
                if fw1_more:
                    fw1_low(f + 3, 1 - parity)
                if fw2_more:
                    fw2_low(f + 1, 1 - parity)

            gated(0, 0, True)
            fw2_low(0, 0)
            for c in range(NC):
                dve.tensor_tensor(x3[:, c, :], x3[:, c, :], beta2_rows[:, :], ALU.add)
            fw1_low(2, 0)
            step(0, 0)
            with dve.Fori(0, (FS - 4) // 2) as i:
                step(2 * i + 1, 1)
                step(2 * i + 2, 0)
            step(FS - 3, 1, fw1_more=False)
            gated(FS - 1, 1)
            gated_low(FS - 2, (gT2_hi, gT2_lo), pb)
            fw2_low(FS - 1, 1)
            gated_low(FS - 1)

            for c in range(NC):
                dve.wait_ge(f2_chunk, c + 1)
                link(dve.tensor_tensor(y5[:, c, :], pg[:, c, :], tok[:, c, :], ALU.add))
                centred(y5, 0, c, gamma2_rows)
            for c in range(NC):
                scaled(fin, y5, 0, c, x3, 2 * NC + c + 1).then_inc(fin_ready, 1)


_INS = ["x", "src", "dst", "edge_attr_64", "L0_gnn_weight", "L0_gnn_bias", "L1_gnn_W1", "L1_gnn_b1", "L1_gnn_W2",
        "L1_gnn_b2", "L1_gnn_W3", "L1_gnn_b3", "L1_gnn_W4", "L1_gnn_b4", "L1_gnn_gamma", "L1_gnn_beta", "L1_ffn_Wg",
        "L1_ffn_bg", "L1_ffn_W1", "L1_ffn_b1", "L1_ffn_W2", "L1_ffn_b2", "L1_ffn_gamma", "L1_ffn_beta"]


def kernel(**inputs):
    import numpy as _np
    import concourse.bacc as _bacc
    from concourse import mybir as _mybir
    from concourse.bass_utils import run_bass_kernel_spmd as _run

    nc = _bacc.Bacc("TRN2", target_bir_lowering=False, num_devices=1)
    arrays, args = {}, []
    for name in _INS:
        a = _np.ascontiguousarray(inputs[name])
        arrays[f"in_{name}_dram"] = a
        args.append(nc.dram_tensor(f"in_{name}_dram", a.shape, _mybir.dt.from_np(a.dtype), kind="ExternalInput").ap())
    out = nc.dram_tensor("out_0_dram", inputs["x"].shape, _mybir.dt.float32, kind="ExternalOutput").ap()
    gnn_ffn_stack(nc, *args, out)
    r = _run(nc, [arrays], core_ids=[0])
    return r.results[0]["out_0_dram"]
```
